# Optimizing a Trainium2 kernel written in Bass

```python
import numpy as np
import jax
import jax.numpy as jnp

def _softmax(x, axis=-1):
    return jax.nn.softmax(x, axis=axis)

def _gelu(x):
    return jax.nn.gelu(x, approximate=True)

def _silu(x):
    return jax.nn.silu(x)

def _sigmoid(x):
    return jax.nn.sigmoid(x)

def _layernorm(x, axis=-1, eps=1e-05):
    m = jnp.mean(x, axis=axis, keepdims=True)
    v = jnp.var(x, axis=axis, keepdims=True)
    return (x - m) / jnp.sqrt(v + eps)

def _scatter_add(tgt, idx, src, axis=0):
    return tgt.at[idx].add(src)

def _segment_sum(src, seg, n):
    return jax.ops.segment_sum(src, seg, n)
kernel_name = 'mk_early_fusion_d1_tok_img1024_r4_38bcdd'

def setup_inputs(seed: int=0):
    np.random.seed(seed)
    _w = jnp.asarray

    def _rec_inputs():
        import jax
        import jax.numpy as jnp
        _rk = jax.random.key(seed)
        x = -0.000348323 + 0.999952 * jax.random.normal(jax.random.fold_in(_rk, 1), (64, 3, 84, 84), jnp.float32)
        txt = -0.000563189 + 0.999639 * jax.random.normal(jax.random.fold_in(_rk, 2), (64, 77, 256), jnp.float32)
        return (x, txt)
    x, txt = _rec_inputs()

    def _L0_tok_setup():
        import jax, jax.numpy as jnp
        import numpy as np
        from jax import lax
        PATCH = 16
        key = jax.random.key(seed)
        k1, k2 = jax.random.split(key)
        B, C, IMG, HID = (32, 3, 96, 256)
        inputs = jax.random.normal(k1, (B, C, IMG, IMG), dtype=jnp.float32)
        flat = C * PATCH * PATCH
        W = jax.random.normal(k2, (flat, HID), dtype=jnp.float32) / np.sqrt(flat)
        return {'inputs': inputs, 'W': W}
    _L0_tok_all = _L0_tok_setup()
    _L0_tok_in = {k: v for k, v in _L0_tok_all.items() if k in ('W',)}
    del _L0_tok_all

    def _L0_attn_setup():
        import jax, jax.numpy as jnp
        import numpy as np
        DIM = 256
        HEADS = 16
        HEAD_DIM = DIM // HEADS
        THRESH = 0.29514
        SHARP = 15.0
        LN_EPS = 1e-05
        NORM_EPS = 1e-12

        def _l2norm(t):
            n = jnp.sqrt(jnp.sum(t * t, axis=-1, keepdims=True))
            return t / jnp.maximum(n, NORM_EPS)
        key = jax.random.key(seed)
        ks = jax.random.split(key, 8)
        s = 1.0 / np.sqrt(DIM)
        sg = 1.0 / np.sqrt(HEAD_DIM)
        return {'x': jax.random.normal(ks[0], (2, 512, DIM), dtype=jnp.float32), 'Wq': jax.random.uniform(ks[1], (DIM, DIM), jnp.float32, -s, s), 'Wk': jax.random.uniform(ks[2], (DIM, DIM), jnp.float32, -s, s), 'Wv': jax.random.uniform(ks[3], (DIM, DIM), jnp.float32, -s, s), 'gq': jax.random.uniform(ks[4], (HEAD_DIM,), jnp.float32, -sg, sg), 'gk': jax.random.uniform(ks[5], (HEAD_DIM,), jnp.float32, -sg, sg), 'Wo': jax.random.uniform(ks[6], (DIM, DIM), jnp.float32, -s, s), 'bo': jax.random.uniform(ks[7], (DIM,), jnp.float32, -s, s), 'ln_w': jnp.ones((DIM,), jnp.float32), 'ln_b': jnp.zeros((DIM,), jnp.float32)}
    _L0_attn_all = _L0_attn_setup()
    _L0_attn_in = {k: v for k, v in _L0_attn_all.items() if k in ('Wq', 'Wk', 'Wv', 'gq', 'gk', 'Wo', 'bo', 'ln_w', 'ln_b')}
    del _L0_attn_all

    def _L0_ffn_setup():
        import jax, jax.numpy as jnp
        import numpy as np
        B, S, D, F, E, K = (2, 512, 256, 1024, 8, 2)
        key = jax.random.key(seed)
        ks = jax.random.split(key, 5)
        x = jax.random.normal(ks[0], (B, S, D), dtype=jnp.float32)
        Wg = jax.random.normal(ks[1], (D, E), dtype=jnp.float32) * 0.02
        W1 = jax.random.normal(ks[2], (E, D, F), dtype=jnp.float32) * 0.02
        b1 = jnp.zeros((E, F), dtype=jnp.float32)
        W2 = jax.random.normal(ks[3], (E, F, D), dtype=jnp.float32) * 0.02
        b2 = jnp.zeros((E, D), dtype=jnp.float32)
        return {'x': x, 'Wg': Wg, 'W1': W1, 'b1': b1, 'W2': W2, 'b2': b2}
    _L0_ffn_all = _L0_ffn_setup()
    _L0_ffn_in = {k: v for k, v in _L0_ffn_all.items() if k in ('Wg', 'W1', 'b1', 'W2', 'b2')}
    del _L0_ffn_all
    return {'x': x, 'txt': txt, 'L0_tok_W': _L0_tok_in['W'], 'L0_attn_Wq': _L0_attn_in['Wq'], 'L0_attn_Wk': _L0_attn_in['Wk'], 'L0_attn_Wv': _L0_attn_in['Wv'], 'L0_attn_gq': _L0_attn_in['gq'], 'L0_attn_gk': _L0_attn_in['gk'], 'L0_attn_Wo': _L0_attn_in['Wo'], 'L0_attn_bo': _L0_attn_in['bo'], 'L0_attn_ln_w': _L0_attn_in['ln_w'], 'L0_attn_ln_b': _L0_attn_in['ln_b'], 'L0_ffn_Wg': _L0_ffn_in['Wg'], 'L0_ffn_W1': _L0_ffn_in['W1'], 'L0_ffn_b1': _L0_ffn_in['b1'], 'L0_ffn_W2': _L0_ffn_in['W2'], 'L0_ffn_b2': _L0_ffn_in['b2']}

def reference(x, txt, L0_tok_W, L0_attn_Wq, L0_attn_Wk, L0_attn_Wv, L0_attn_gq, L0_attn_gk, L0_attn_Wo, L0_attn_bo, L0_attn_ln_w, L0_attn_ln_b, L0_ffn_Wg, L0_ffn_W1, L0_ffn_b1, L0_ffn_W2, L0_ffn_b2):
    import jax
    import jax.numpy as jnp

    def _L0_tok_ref(inputs, W):
        import jax, jax.numpy as jnp
        import numpy as np
        from jax import lax
        PATCH = 16
        B, C, H, Wimg = inputs.shape
        patches = lax.conv_general_dilated_patches(inputs, filter_shape=[PATCH, PATCH], window_strides=[PATCH, PATCH], padding='VALID', dimension_numbers=('NCHW', 'HWIO', 'NCHW'))
        patches = patches.reshape(B, -1, C * PATCH * PATCH)
        return jnp.einsum('bnf,fh->bnh', patches, W)

    def _L0_attn_ref(x, Wq, Wk, Wv, gq, gk, Wo, bo, ln_w, ln_b):
        import jax, jax.numpy as jnp
        import numpy as np
        DIM = 256
        HEADS = 16
        HEAD_DIM = DIM // HEADS
        THRESH = 0.29514
        SHARP = 15.0
        LN_EPS = 1e-05
        NORM_EPS = 1e-12

        def _l2norm(t):
            n = jnp.sqrt(jnp.sum(t * t, axis=-1, keepdims=True))
            return t / jnp.maximum(n, NORM_EPS)
        B, T, D = x.shape
        mu = jnp.mean(x, axis=-1, keepdims=True)
        var = jnp.mean((x - mu) ** 2, axis=-1, keepdims=True)
        x_norm = (x - mu) / jnp.sqrt(var + LN_EPS) * ln_w + ln_b

        def split_heads(t):
            return t.reshape(B, T, HEADS, HEAD_DIM).transpose(0, 2, 1, 3)
        q = _l2norm(split_heads(x_norm @ Wq))
        k = _l2norm(split_heads(x_norm @ Wk))
        v = split_heads(x @ Wv)
        align = jnp.einsum('bhtd,bhsd->bhts', q, k)
        resonance = jax.nn.sigmoid((align - THRESH) * SHARP)
        gate_q = jnp.einsum('bhtd,d->bht', q, gq)
        gate_k = jnp.einsum('bhsd,d->bhs', k, gk)
        modulation = resonance * gate_q[..., :, None] * gate_k[..., None, :]
        collapse = jnp.einsum('bhts,bhsd->bhtd', modulation, v)
        collapse = collapse.transpose(0, 2, 1, 3).reshape(B, T, D)
        return collapse @ Wo + bo

    def _L0_ffn_ref(x, Wg, W1, b1, W2, b2):
        import jax, jax.numpy as jnp
        import numpy as np
        B, S, D, F, E, K = (2, 512, 256, 1024, 8, 2)
        b, s, d = x.shape
        e = Wg.shape[1]
        T = b * s
        C = 2 * K * T // e
        xt = x.reshape(T, d)
        logits = xt.astype(jnp.float32) @ Wg.astype(jnp.float32)
        gates = jax.nn.softmax(logits, axis=-1)
        idx1 = jnp.argmax(gates, axis=-1)
        mask1 = jax.nn.one_hot(idx1, e, dtype=gates.dtype)
        gate1 = jnp.sum(gates * mask1, axis=-1)
        logits2 = jnp.where(mask1 > 0, -jnp.inf, logits)
        idx2 = jnp.argmax(logits2, axis=-1)
        mask2 = jax.nn.one_hot(idx2, e, dtype=gates.dtype)
        gate2 = jnp.sum(gates * mask2, axis=-1)
        denom = gate1 + gate2 + 1e-09
        w1 = gate1 / denom
        w2 = gate2 / denom
        p1 = jnp.cumsum(mask1, axis=0) - mask1
        pos1 = jnp.sum(p1 * mask1, axis=-1).astype(jnp.int32)
        off = jnp.sum(mask1, axis=0)
        p2 = jnp.cumsum(mask2, axis=0) - mask2 + off[None, :]
        pos2 = jnp.sum(p2 * mask2, axis=-1).astype(jnp.int32)
        keep1 = (pos1 < C).astype(xt.dtype)
        keep2 = (pos2 < C).astype(xt.dtype)
        pos1 = jnp.clip(pos1, 0, C - 1)
        pos2 = jnp.clip(pos2, 0, C - 1)
        xe = jnp.zeros((e, C, d), dtype=xt.dtype)
        xe = xe.at[idx1, pos1].add(xt * keep1[:, None])
        xe = xe.at[idx2, pos2].add(xt * keep2[:, None])
        h = jax.nn.gelu(jnp.einsum('ecd,edf->ecf', xe, W1) + b1[:, None, :], approximate=False)
        ye = jnp.einsum('ecf,efd->ecd', h, W2) + b2[:, None, :]
        out = ye[idx1, pos1] * (w1 * keep1)[:, None] + ye[idx2, pos2] * (w2 * keep2)[:, None]
        return out.reshape(b, s, d)
    h = _L0_tok_ref(x, L0_tok_W)
    h = jnp.concatenate([h, txt], axis=1)
    h = h + _L0_attn_ref(_layernorm(h, axis=-1), L0_attn_Wq, L0_attn_Wk, L0_attn_Wv, L0_attn_gq, L0_attn_gk, L0_attn_Wo, L0_attn_bo, L0_attn_ln_w, L0_attn_ln_b)
    h = h + _L0_ffn_ref(_layernorm(h, axis=-1), L0_ffn_Wg, L0_ffn_W1, L0_ffn_b1, L0_ffn_W2, L0_ffn_b2)
    return h

_drawn_inputs = setup_inputs


def setup_inputs(seed=0):
    import zlib

    import numpy as np

    out = dict(_drawn_inputs(seed))
    spreads = {'L0_attn_ln_w': (1.0, 0.6),
     'L0_attn_ln_b': (0.0, 0.794),
     'L0_ffn_b1': (0.0, 0.305),
     'L0_ffn_b2': (0.0, 0.1)}
    factors = {}
    for name, (base, spread) in spreads.items():
        noise = np.random.default_rng([zlib.crc32(name.encode()), seed]).standard_normal(out[name].shape)
        drawn = base * np.exp(spread * noise) if base else spread * noise
        out[name] = jnp.asarray(drawn.astype(out[name].dtype))
    for name, factor in factors.items():
        out[name] = (out[name] * factor).astype(out[name].dtype)
    return out
```

```python
from contextlib import ExitStack

import numpy as np

import concourse.bass as bass
from concourse import mybir

F32 = mybir.dt.float32
BF16 = mybir.dt.bfloat16
I32 = mybir.dt.int32
U32 = mybir.dt.uint32
ALU = mybir.AluOpType
ACT = mybir.ActivationFunctionType
AX = mybir.AxisListType

P = 128
B, C_IN, IMG, PATCH = 64, 3, 84, 16
GRID = IMG // PATCH
N_PATCH = GRID * GRID
N_TXT = 77
N = N_PATCH + N_TXT
D = 256
KC = D // P
FLAT = C_IN * PATCH * PATCH
FLATC = FLAT // P
TOKENS = B * N
HEADS, HD = 16, 16
THRESH, SHARP = 0.29514, 15.0
LN_EPS, NORM_EPS = 1e-05, 1e-12
E, F = 8, 1024
FC = F // P
CAP = 2 * 2 * TOKENS // E
PAIR = 2
SLOTS = B // PAIR
HALF = HEADS // 2
QKV = 2 * D + D + 2 * HEADS
WCH = 1024
WCHUNKS = 2 * E * KC
TILE, PARTS = 256, 2
TILES = 2 * TOKENS // TILE + E - 1
CENTRE = TOKENS
ROWS = 2 * TOKENS
RSQRT_GUESS = float(0x5F3759DF)
NEWTON_ROUNDS = 3
NQK, NV2, NV1, NR2, NCOLS = 0, 2 * PAIR * HEADS, 2 * PAIR * HEADS + PAIR, 2 * PAIR * HEADS + 2 * PAIR, 2 * PAIR * HEADS + 3 * PAIR


class Steps:

    def __init__(self, eng, sem):
        self.eng, self.sem, self.n, self.base = eng, sem, 0, 0

    def mark(self, ins):
        self.n += 1
        return ins.then_inc(self.sem, 1)

    def settle(self):
        self.eng.wait_ge(self.sem, self.base + self.n)

    def do(self, ins):
        self.mark(ins)
        self.settle()


def slots(eng, steps, slot, full_from, loop_from, unroll, rounds, total):
    def known(s):
        return lambda lag, count: 0 <= s - lag < count
    per_slot = 0
    for s in range(loop_from):
        before = steps.n if steps else 0
        slot(s, s % unroll, known(s))
        per_slot = (steps.n if steps else 0) - before
    at = steps.n if steps else 0
    with eng.Fori(0, rounds) as it:
        for k in range(unroll):
            if steps:
                steps.base = it * (per_slot * unroll)
            slot(it * unroll + (loop_from + k), (loop_from + k) % unroll, lambda lag, count: True)
    if steps:
        assert steps.n - at == per_slot * unroll, (steps.n - at, per_slot)
        steps.base, steps.n = 0, at + per_slot * unroll * rounds
    for s in range(loop_from + unroll * rounds, total):
        slot(s, s % unroll, known(s))


def wait_before_dma(eng, past, *waits):
    values = [v if isinstance(v, int) else eng.to_reg(v) for _, v in waits]
    eng.wait_ge(*past)
    for (sem, _), value in zip(waits, values):
        eng.wait_ge(sem, value)


def inverse_sqrt(nc, steps, done, y, x, t):
    steps.do(nc.vector.tensor_scalar(y.bitcast(I32), x.bitcast(I32), -0.5, RSQRT_GUESS, ALU.mult, ALU.add))
    for n in range(NEWTON_ROUNDS):
        steps.do(nc.vector.tensor_tensor(t, y, y, ALU.mult))
        steps.do(nc.vector.scalar_tensor_tensor(out=t, in0=t, scalar=-0.5, in1=x, op0=ALU.mult, op1=ALU.mult))
        last = nc.vector.scalar_tensor_tensor(out=y, in0=t, scalar=1.5, in1=y, op0=ALU.add, op1=ALU.mult)
        if n < NEWTON_ROUNDS - 1:
            steps.do(last)
    last.then_inc(done, 1)


def prepare_and_tokenise(nc, m, dram):
    CHUNK, GROUP = 200, 100
    PER = CHUNK // GROUP
    with ExitStack() as ctx:
        sb = lambda n, s, d: ctx.enter_context(nc.sbuf_tensor(n, s, d))
        sem = lambda n: ctx.enter_context(nc.semaphore(n))
        w_tok = sb("w_tok", [P, FLATC, D], F32)
        w_tok_hi = sb("w_tok_hi", [P, FLATC, D], BF16)
        w_tok_lo = sb("w_tok_lo", [P, FLATC, D], BF16)
        w_all = sb("w_all", [P, KC, QKV], F32)
        w_raw = sb("w_raw", [P, KC, 2 * D], F32)
        w_out = sb("w_out", [P, KC, D], F32)
        w_gate = sb("w_gate", [P, KC, E], F32)
        gated = sb("gated", [P, KC, 2 * D], F32)
        ln_w = sb("ln_w", [P, KC], F32)
        ln_b = sb("ln_b", [P, KC], F32)
        ln_b_cols = sb("ln_b_cols", [P, KC, P], F32)
        g_row = sb("g_row", [P, 2, HD], F32)
        pat = sb("pat", [P, 2, FLATC, CHUNK], F32)
        pat_hi = sb("pat_hi", [P, 2, FLATC, CHUNK], BF16)
        pat_lo = sb("pat_lo", [P, 2, FLATC, CHUNK], BF16)
        tok = sb("tok", [P, 2, D], F32)
        bias = sb("bias", [P, (E + 1) * D // P], F32)
        bias_rest = sb("bias_rest", [P, (E + 1) * D // P], F32)
        bias_parts = sb("bias_parts", [P, 3, (E + 1) * D // P], BF16)
        ps_tok = [ctx.enter_context(nc.psum_tensor(f"ps_tok{i}", [P, 512], F32)) for i in range(2)]
        ps_bias = ctx.enter_context(nc.psum_tensor("ps_bias", [P, 512], F32))

        consts_in = sem("consts_in")
        w_tok_in = sem("w_tok_in")
        w_in = sem("w_in")
        pat_in = [sem(f"pat_in{i}") for i in range(2)]
        dve_steps = sem("dve_steps1")
        w_tok_ready = sem("w_tok_ready")
        hi_ready = sem("pat_hi_ready")
        lo_ready = sem("pat_lo_ready")
        group_done = sem("group_done")
        group_copied = sem("group_copied")
        tok_out = [sem(f"tok_out{i}") for i in range(2)]
        ln_b_ready = sem("ln_b_ready")
        bias_done = sem("bias_done")
        bias_split = sem("bias_split")
        bias_out = sem("bias_out")
        block = ctx.enter_context(nc.Block())
        LOADS = B * N_PATCH // CHUNK

        @block.sync
        def _(sp):
            sp.dma_start(w_tok[:], dram["w_tok"]).then_inc(w_tok_in, 16)
            for c in range(2):
                sp.dma_start(pat[:, c], dram["patches"][:, :, CHUNK * c:CHUNK * (c + 1)]).then_inc(pat_in[c], 16)
            for dst, src in ((m.consts[:], dram["consts"]), (m.b1[:], dram["b1"]), (m.bo[:], dram["bo"].partition_broadcast(P))):
                sp.dma_start(dst, src).then_inc(consts_in, 16)
            for dst, src in ((w_raw[:], dram["w_qk"]), (w_all[:, :, 2 * D:3 * D], dram["w_v"]), (w_out[:], dram["w_o"]),
                             (bias[:], dram["biases"]), (w_gate[:], dram["w_g"]), (ln_w[:], dram["ln_w"]), (ln_b[:], dram["ln_b"]),
                             (g_row[:, 0, :], dram["gq"].partition_broadcast(P)),
                             (g_row[:, 1, :], dram["gk"].partition_broadcast(P))):
                sp.dma_start(dst, src).then_inc(w_in, 16)
            for i in range(3):
                if i == 0:
                    sp.wait_ge(bias_split, 1)
                sp.dma_start(dram["bias_parts"][i].rearrange("(p c) -> p c", p=P), bias_parts[:, i]).then_inc(bias_out, 16)
            for c in range(2, LOADS):
                sp.wait_ge(hi_ready, c - 1)
                sp.wait_ge(lo_ready, c - 1)
                sp.dma_start(pat[:, c % 2], dram["patches"][:, :, CHUNK * c:CHUNK * (c + 1)]).then_inc(pat_in[c % 2], 16)
            sp.wait_ge(bias_out, 48)
            sp.wait_ge(tok_out[0], 16 * LOADS * PER // 2)
            sp.wait_ge(tok_out[1], 16 * LOADS * PER // 2)

        def copy_groups(act, c):
            for j in range(PER):
                n = PER * c + j
                act.wait_ge(group_done, n + 1)
                if n >= 2:
                    act.wait_ge(tok_out[n % 2], 16 * (n // 2))
                nc.scalar.copy(tok[0:GROUP, n % 2], ps_tok[n % 2][0:GROUP, 0:D]).then_inc(group_copied, 1)
                act.wait_ge(group_copied, n + 1)
                act.dma_start(dram["tok"][GROUP * n:GROUP * (n + 1), :], tok[0:GROUP, n % 2]).then_inc(tok_out[n % 2], 16)

        @block.scalar
        def _(act):
            for c in range(LOADS):
                act.wait_ge(pat_in[c % 2], 16 * (c // 2 + 1))
                if c >= 2:
                    act.wait_ge(group_done, PER * (c - 1))
                nc.scalar.copy(pat_hi[:, c % 2], pat[:, c % 2]).then_inc(hi_ready, 1)
                if c >= 1:
                    copy_groups(act, c - 1)
            copy_groups(act, LOADS - 1)

        @block.tensor
        def _(pe):
            pe.wait_ge(w_tok_ready, 1)
            for c in range(LOADS):
                pe.wait_ge(hi_ready, c + 1)
                pe.wait_ge(lo_ready, c + 1)
                for j in range(PER):
                    n = PER * c + j
                    if n >= 2:
                        pe.wait_ge(group_copied, n - 1)
                    cols = slice(GROUP * j, GROUP * (j + 1))
                    parts = [(x, w, f) for f in range(FLATC) for x, w in ((pat_hi, w_tok_hi), (pat_lo, w_tok_hi), (pat_hi, w_tok_lo))]
                    for i, (x, w, f) in enumerate(parts):
                        mm = nc.tensor.matmul(ps_tok[n % 2][0:GROUP, 0:D], x[:, c % 2, f, cols], w[:, f, :],
                                              start=i == 0, stop=i == len(parts) - 1)
                    mm.then_inc(group_done, 1)
                if c == 0:
                    pe.wait_ge(ln_b_ready, 1)
                    for kc in range(KC):
                        mm = nc.tensor.matmul(ps_bias[:, :], ln_b_cols[:, kc, :], w_raw[:, kc, :], start=kc == 0, stop=kc == KC - 1)
                    mm.then_inc(bias_done, 1)

        @block.vector
        def _(dve):
            st = Steps(dve, dve_steps)
            dve.wait_ge(w_tok_in, 16)
            st.do(nc.vector.tensor_copy(w_tok_hi[:], w_tok[:]))
            nc.vector.tensor_tensor(w_tok_lo[:], w_tok[:], w_tok_hi[:], ALU.subtract).then_inc(w_tok_ready, 1)
            for c in range(LOADS):
                dve.wait_ge(hi_ready, c + 1)
                if c >= 2:
                    dve.wait_ge(group_done, PER * (c - 1))
                nc.vector.tensor_tensor(pat_lo[:, c % 2], pat[:, c % 2], pat_hi[:, c % 2], ALU.subtract).then_inc(lo_ready, 1)
                if c == 0:
                    dve.wait_ge(w_in, 16 * 9)
                    dve.wait_ge(consts_in, 16 * 3)
                    for i in range(3):
                        rest = bias if i == 0 else bias_rest
                        ins = nc.vector.tensor_copy(bias_parts[:, i], rest[:])
                        if i < 2:
                            st.do(ins)
                            st.do(nc.vector.tensor_tensor(bias_rest[:], rest[:], bias_parts[:, i], ALU.subtract))
                    ins.then_inc(bias_split, 1)
                    for kc in range(KC):
                        st.mark(nc.vector.tensor_scalar(w_all[:, kc, 0:2 * D], w_raw[:, kc, :], ln_w[:, kc:kc + 1], None, ALU.mult))
                    nc.vector.tensor_copy(ln_b_cols[:], ln_b[:].unsqueeze(2).to_broadcast([P, KC, P])).then_inc(ln_b_ready, 1)
                    st.mark(nc.vector.tensor_copy(m.ident[:], m.ident_f))
                    st.mark(nc.vector.tensor_copy(m.tri[:], m.tri_f))
                    st.mark(nc.vector.tensor_copy(m.token_id[:], m.first_tokens))
                    st.mark(nc.vector.tensor_copy(m.w_out_hi[:], w_out[:]))
                    st.mark(nc.vector.tensor_copy(m.w_gate_hi[:], w_gate[:]))
                    st.mark(nc.vector.memset(m.ones[:], 1.0))
                    st.settle()
                    st.mark(nc.vector.tensor_tensor(m.w_out_lo[:], w_out[:], m.w_out_hi[:], ALU.subtract))
                    st.mark(nc.vector.tensor_tensor(m.w_gate_lo[:], w_gate[:], m.w_gate_hi[:], ALU.subtract))
                    for kc in range(KC):
                        for i in range(2):
                            st.mark(nc.vector.tensor_tensor(
                                gated[:, kc, i * D:(i + 1) * D].rearrange("p (h d) -> p h d", d=HD),
                                w_all[:, kc, i * D:(i + 1) * D].rearrange("p (h d) -> p h d", d=HD),
                                g_row[:, i, :].unsqueeze(1).to_broadcast([P, HEADS, HD]), ALU.mult))
                    st.settle()
                    for kc in range(KC):
                        st.mark(nc.vector.tensor_reduce(w_all[:, kc, 3 * D:QKV], gated[:, kc, :].rearrange("p (h d) -> p h d", d=HD), AX.X, ALU.add))
                    st.settle()
                    st.do(nc.vector.tensor_copy(m.w_hi[:], w_all[:]))
                    st.mark(nc.vector.tensor_tensor(m.w_lo[:], w_all[:], m.w_hi[:], ALU.subtract))
            dve.wait_ge(bias_done, 1)
            st.do(nc.vector.tensor_copy(m.bias_qk[:], ps_bias[:, :]))
            for i in range(2):
                st.mark(nc.vector.tensor_tensor(
                    gated[:, 0, i * D:(i + 1) * D].rearrange("p (h d) -> p h d", d=HD),
                    m.bias_qk[:, i * D:(i + 1) * D].rearrange("p (h d) -> p h d", d=HD),
                    g_row[:, i, :].unsqueeze(1).to_broadcast([P, HEADS, HD]), ALU.mult))
            st.settle()
            st.mark(nc.vector.tensor_reduce(m.bias_gate[:], gated[:, 0, :].rearrange("p (h d) -> p h d", d=HD), AX.X, ALU.add))
            st.mark(nc.vector.memset(m.placed[:], 0.0))
            st.settle()


def fusion_attention(nc, m, dram):
    PROJ, ATT, OUT, ROUTE, PLACE = 1, 2, 3, 4, 5
    TOTAL = SLOTS + PLACE
    RING = 4
    with ExitStack() as ctx:
        sb = lambda n, s, d: ctx.enter_context(nc.sbuf_tensor(n, s, d))
        sem = lambda n: ctx.enter_context(nc.semaphore(n))
        pb = lambda n: ctx.enter_context(nc.psum_tensor(n, [P, 512], F32))
        h = sb("h", [P, RING, PAIR, D], F32)
        stats = sb("stats", [P, 2, PAIR, 6], F32)
        mv = sb("mv", [P, 2, PAIR, 2], F32)
        squares = sb("squares", [P, NCOLS], F32)
        inv = sb("inv", [P, 2, NCOLS], F32)
        inv_t = sb("inv_t", [P, NCOLS], F32)
        x12 = sb("x12", [P, 2, PAIR, D], F32)
        x1, x2, qk_sq = x12[:, 0], x12[:, 1], x12[:].rearrange("p i b d -> p (i b d)").rearrange("p (b c) -> p b c", b=PAIR)
        x1s = sb("x1s", [P, PAIR, 2, D], BF16)
        x1T = sb("x1T", [P, PAIR, 2, KC, N], BF16)
        qk = sb("qk", [P, PAIR, 2 * D], F32)
        qks = sb("qks", [P, PAIR, 2 * HEADS, 4, HD], BF16)
        qT = sb("qT", [P, PAIR, HALF, N], BF16)
        kT = sb("kT", [P, PAIR, HALF, N], BF16)
        sig = sb("sig", [P, 2, 2, HALF // 2, N], F32)
        vg = sb("vg", [P, PAIR, D + 2 * HEADS], F32)
        gate = sb("gate", [P, PAIR, 2 * HEADS], F32)
        gate_q = sb("gate_q", [P, PAIR, HEADS, HD], F32)
        v_pad = sb("v_pad", [P, PAIR, HEADS, 2 * HD], F32)
        cT = sb("cT", [P, KC, N], F32)
        cTs = sb("cTs", [P, PAIR, 2, KC, N], BF16)
        h2 = sb("h2", [P, PAIR, D], F32)
        x2s = sb("x2s", [P, PAIR, 2, D], BF16)
        x2T = sb("x2T", [P, PAIR, 2, KC, N], BF16)
        w_stage = sb("w_stage", [P, WCH], F32)
        lg = sb("lg", [P, PAIR, 5, E], F32)
        sg = sb("sg", [P, PAIR, 2, E], F32)
        top = sb("top", [P, PAIR, 8], F32)
        masks = sb("masks", [P, PAIR, 2, E], BF16)
        places = sb("places", [P, PAIR, 2, E], F32)
        entry = sb("entry", [P, PAIR, 2, 2], F32)
        slot_f = sb("slot_f", [P, PAIR, 2], F32)
        slot_i = sb("slot_i", [P, PAIR, 2], U32)
        sum12 = sb("sum12", [P, 2 * E], F32)
        zeros = sb("zeros", [P, 128], F32)
        sig_bias = sb("sig_bias", [P, 1], F32)
        bT, bQK0, bQK1, bV, bKT, bS0, bS1, bC = [pb(n) for n in ("bT", "bQK0", "bQK1", "bV", "bKT", "bS0", "bS1", "bC")]
        bQK, bS = [bQK0, bQK1], [bS0, bS1]
        xT_ps = bT[:, :].bitcast(BF16)[:, 0:PAIR * 2 * KC * N].rearrange("p (b s k n) -> p b s k n", b=PAIR, s=2, k=KC)
        kt_ps = bKT[:, :].bitcast(BF16)[:, 0:HALF * N].rearrange("p (j n) -> p j n", j=HALF)

        names = """x1_ready x1_hi x1_lo x1T_done x1T_ready qk_done qk_ready v_done v_copied sq_ready inv_ready
            qn_ready qk_hi qk_lo qT_done qT_ready kT_done kT_ready score_done sig_ready vgate_ready col_done c_ready
            wo_done h2_ready out_stored x2_ready x2_hi x2_lo xln_stored x2T_done x2T_ready lg_done lg_read masks_ready
            pos_done pos_read entry_ready scattered bo_added w_loaded w_hi_ready w_lo_ready table_zero dve_steps2
            zero_ready pad_zero bias_set ex_ready sg_ready""".split()
        q = {n: sem(n) for n in names}
        h_loaded = [sem(f"h_loaded{i}") for i in range(RING)]
        block = ctx.enter_context(nc.Block())

        def run(eng, steps, slot):
            slots(eng, steps, slot, PLACE, 8, RING, 6, TOTAL)

        def tok_of(s):
            v = dram["tok"].rearrange("(g b n) d -> g n b d", b=PAIR, n=N_PATCH)
            return v[bass.ds(s, 1)].rearrange("o n b d -> (o n) b d")

        def txt_of(s):
            v = dram["txt"].rearrange("(g b) n d -> g n b d", b=PAIR)
            return v[bass.ds(s, 1)].rearrange("o n b d -> (o n) b d")

        def rows_of(t, s):
            v = t[0:TOKENS, :].rearrange("(g b n) d -> g n b d", b=PAIR, n=N)
            return v[bass.ds(s, 1)].rearrange("o n b d -> (o n) b d")

        @block.sync
        def _(sp):
            sp.wait_ge(q["zero_ready"], 1)
            sp.dma_start(dram["table"].rearrange("(p r) c -> p (r c)", p=P).rearrange("p (a c) -> p a c", c=102),
                         zeros[:, 0:102].unsqueeze(1).to_broadcast([P, E * ROWS * 2 // P // 102, 102])).then_inc(q["table_zero"], 16)
            sp.dma_start(dram["out"][TOKENS:TOKENS + P, :].rearrange("p (a c) -> p a c", c=128),
                         zeros[:, :].unsqueeze(1).to_broadcast([P, 2, 128])).then_inc(q["table_zero"], 16)

            def slot(s, k, ok):
                if ok(0, SLOTS):
                    if not isinstance(s, int) or s >= RING:
                        sp.wait_ge(q["h2_ready"], s - RING + 1)
                    sp.dma_start(h[0:N_PATCH, k], tok_of(s)).then_inc(h_loaded[k], 16)
                    sp.dma_start(h[N_PATCH:N, k], txt_of(s)).then_inc(h_loaded[k], 16)
                    if not isinstance(s, int) or s >= 1:
                        sp.wait_ge(q["w_hi_ready"], s)
                        sp.wait_ge(q["w_lo_ready"], s)
                    sp.dma_start(w_stage[:], dram["w_ffn"][bass.ds(s, 1)].rearrange("o p c -> p (o c)")).then_inc(q["w_loaded"], 16)
                if ok(OUT, SLOTS):
                    o = s - OUT
                    sp.wait_ge(q["h2_ready"], o + 1)
                    sp.dma_start(rows_of(dram["out"], o), h2[0:N]).then_inc(q["out_stored"], 16)
                    sp.wait_ge(q["x2_lo"], o + 1)
                    sp.wait_ge(q["x2_hi"], o + 1)
                    sp.dma_start(rows_of(dram["xln"], o), x2s[0:N].rearrange("n b s d -> n b (s d)")).then_inc(q["xln_stored"], 16)

            run(sp, None, slot)
            sp.wait_ge(q["out_stored"], 16 * SLOTS)
            sp.wait_ge(q["xln_stored"], 16 * SLOTS)
            sp.wait_ge(q["table_zero"], 32)

        @block.tensor
        def _(pe):
            def transposes(src, done):
                for b in range(PAIR):
                    for part in range(2):
                        for kc in range(KC):
                            mm = nc.tensor.transpose(xT_ps[:, b, part, kc, :], src[0:N, b, part, kc * P:(kc + 1) * P], m.ident[0:N, 0:N])
                mm.then_inc(done, 1)

            def product(out, xT, b, hi, lo, cols, first=True):
                parts = [(x, w, kc) for kc in range(KC) for x, w in ((0, hi), (1, hi), (0, lo))]
                for i, (x, w, kc) in enumerate(parts):
                    mm = nc.tensor.matmul(out, xT[:, b, x, kc, :], w[:, kc, cols], start=i == 0, stop=i == len(parts) - 1)
                return mm

            def slot(s, k, ok):
                p, a, o, r, c = s - PROJ, s - ATT, s - OUT, s - ROUTE, s - PLACE
                has_p, has_a, has_o = ok(PROJ, SLOTS), ok(ATT, SLOTS), ok(OUT, SLOTS)
                late = lambda x, n: not isinstance(x, int) or x >= n

                if ok(PLACE, SLOTS):
                    pe.wait_ge(q["masks_ready"], c + 1)
                    pe.wait_ge(q["lg_read"], c + 1)
                    mk = masks[0:N].rearrange("n b c e -> n (b c e)")
                    W = 2 * E
                    nc.tensor.matmul(bT[:, 0:PAIR * W], m.tri[0:N, :], mk, start=True, stop=False, skip_group_check=True)
                    nc.tensor.matmul(bT[:, W:2 * W], m.ones[0:N, :], mk[:, 0:W], start=False, stop=True, skip_group_check=True)
                    nc.tensor.matmul(bT[:, 2 * W:3 * W], m.ones[0:N, :], mk[:, 0:W], start=True, stop=False, skip_group_check=True)
                    nc.tensor.matmul(bT[:, 2 * W:3 * W], m.ones[0:N, :], mk[:, W:2 * W], start=False, stop=True,
                                     skip_group_check=True).then_inc(q["pos_done"], 1)
                if has_p:
                    pe.wait_ge(q["x1_hi"], p + 1)
                    pe.wait_ge(q["x1_lo"], p + 1)
                    if ok(ROUTE + 1, SLOTS):
                        pe.wait_ge(q["pos_read"], c + 1)
                    transposes(x1s, q["x1T_done"])

                def turn(b, which, done):
                    n = 2 * a + b
                    if which == 0:
                        pe.wait_ge(q["qk_hi"], a + 1)
                        pe.wait_ge(q["qk_lo"], a + 1)
                        if late(n, 1):
                            pe.wait_ge(q["kT_ready"], n)
                    else:
                        pe.wait_ge(q["qT_ready"], n + 1)
                    for j in range(HALF):
                        mm = nc.tensor.transpose(kt_ps[:, j, :], qks[0:N, b, which * HEADS + 2 * j:which * HEADS + 2 * j + 2].rearrange("n h c d -> n (h c d)"),
                                                 m.ident[0:N, 0:N])
                    mm.then_inc(done, 1)

                def scores(b, half):
                    n = 8 * a + 4 * b + 2 * half
                    if half == 0:
                        pe.wait_ge(q["qT_ready"], 2 * a + b + 1)
                        pe.wait_ge(q["kT_ready"], 2 * a + b + 1)
                    for u in range(2):
                        if late(n + u, 2):
                            pe.wait_ge(q["sig_ready"], n + u - 1)
                    for j in range(HALF // 2):
                        for u in range(2):
                            rows = slice(64 * u, 64 * u + 64)
                            mm = nc.tensor.matmul(bS[u][0:N, j * N:(j + 1) * N], kT[rows, b, half * 4 + j, :], qT[rows, b, half * 4 + j, :],
                                                  start=True, stop=True)
                            if j == HALF // 2 - 1:
                                mm.then_inc(q["score_done"], 1)

                def collapse(b):
                    n = 2 * a + b
                    pe.wait_ge(q["vgate_ready"], a + 1)
                    if late(n, 1):
                        pe.wait_ge(q["c_ready"], n)
                    for half in range(2):
                        pe.wait_ge(q["sig_ready"], 8 * a + 4 * b + 2 * half + 2)
                        for j in range(4):
                            for u in range(2):
                                mm = nc.tensor.matmul(bC[32 * j:32 * j + 32, half * N:(half + 1) * N], v_pad[0:N, b, 2 * (4 * half + j) + u, :],
                                                      sig[0:N, half, u, j, :], start=u == 0, stop=u == 1, skip_group_check=True)
                        mm.then_inc(q["col_done"], 1)
                    for kc in range(KC):
                        mm = nc.tensor.matmul(bC[:, (2 + kc) * N:(3 + kc) * N], gate_q[0:N, b].rearrange("n h d -> n (h d)")[:, kc * P:(kc + 1) * P],
                                              m.ident_f[0:N, 0:N], start=True, stop=True, skip_group_check=True)
                    mm.then_inc(q["col_done"], 1)

                def project_qk(b):
                    if b == 0:
                        pe.wait_ge(q["x1T_ready"], p + 1)
                    if late(p, 1):
                        pe.wait_ge(q["qk_ready"], 2 * p + b - 1)
                    product(bQK[b][0:N, :], x1T, b, m.w_hi, m.w_lo, slice(0, 2 * D)).then_inc(q["qk_done"], 1)

                def project_v(b):
                    n = 2 * p + b
                    if late(n, 1):
                        pe.wait_ge(q["v_copied"], n)
                    if b == 0 and ok(OUT + 1, SLOTS):
                        pe.wait_ge(q["h2_ready"], o)
                    if b == 1 and has_o:
                        pe.wait_ge(q["h2_ready"], o + 1)
                    product(bV[0:N, 0:D + 2 * HEADS], x1T, b, m.w_hi, m.w_lo, slice(2 * D, QKV)).then_inc(q["v_done"], 1)

                if has_a:
                    turn(0, 0, q["qT_done"])
                if has_p:
                    project_qk(0)
                if has_a:
                    turn(0, 1, q["kT_done"])
                if has_p:
                    project_v(0)
                if has_a:
                    scores(0, 0)
                if has_p:
                    project_qk(1)
                if has_a:
                    scores(0, 1)
                if has_o:
                    pe.wait_ge(q["c_ready"], 2 * o + 2)
                    if has_p:
                        pe.wait_ge(q["v_copied"], 2 * p + 1)
                    else:
                        pe.wait_ge(q["v_copied"], 2 * SLOTS)
                        pe.wait_ge(q["h2_ready"], o)
                    for b in range(PAIR):
                        mm = product(bV[0:N, b * D:(b + 1) * D], cTs, b, m.w_out_hi, m.w_out_lo, slice(0, D))
                    mm.then_inc(q["wo_done"], 1)
                if has_a:
                    turn(1, 0, q["qT_done"])
                    collapse(0)
                    turn(1, 1, q["kT_done"])
                if has_p:
                    project_v(1)
                if has_a:
                    scores(1, 0)
                if ok(ROUTE, SLOTS):
                    pe.wait_ge(q["x2_hi"], r + 1)
                    pe.wait_ge(q["x2_lo"], r + 1)
                    if has_p:
                        pe.wait_ge(q["x1T_ready"], p + 1)
                    elif ok(ROUTE + 1, SLOTS):
                        pe.wait_ge(q["pos_read"], c + 1)
                    transposes(x2s, q["x2T_done"])
                if has_a:
                    scores(1, 1)
                if ok(ROUTE, SLOTS):
                    pe.wait_ge(q["x2T_ready"], r + 1)
                    for b in range(PAIR):
                        mm = product(bT[0:N, b * E:(b + 1) * E], x2T, b, m.w_gate_hi, m.w_gate_lo, slice(0, E))
                    mm.then_inc(q["lg_done"], 1)
                if has_a:
                    collapse(1)

            run(pe, None, slot)

        @block.scalar
        def _(act):
            def slot(s, k, ok):
                p, a, o = s - PROJ, s - ATT, s - OUT
                has_p, has_a, has_o = ok(PROJ, SLOTS), ok(ATT, SLOTS), ok(OUT, SLOTS)
                late = lambda x, n: not isinstance(x, int) or x >= n

                def keep_qT(b):
                    n = 2 * a + b
                    act.wait_ge(q["qT_done"], n + 1)
                    if late(n, 2):
                        act.wait_ge(q["score_done"], 4 * n - 4)
                    nc.scalar.copy(qT[:, b], kt_ps).then_inc(q["qT_ready"], 1)

                def keep_v(b):
                    n = 2 * p + b
                    act.wait_ge(q["v_done"], n + 1)
                    if late(p, 1):
                        act.wait_ge(q["vgate_ready"], p)
                    nc.scalar.copy(vg[0:N, b], bV[0:N, 0:D + 2 * HEADS]).then_inc(q["v_copied"], 1)

                def resonance(b, half):
                    for u in range(2):
                        n = 8 * a + 4 * b + 2 * half + u
                        act.wait_ge(q["score_done"], n + 1)
                        if late(2 * a + b, 1):
                            act.wait_ge(q["col_done"], 3 * (2 * a + b - 1) + half + 1)
                        nc.scalar.activation(sig[0:N, half, u], bS[u][0:N, 0:4 * N].rearrange("n (j t) -> n j t", j=4), ACT.Sigmoid,
                                             bias=sig_bias[0:N, :], scale=SHARP).then_inc(q["sig_ready"], 1)

                if has_a:
                    keep_qT(0)
                if has_p:
                    keep_v(0)
                if has_a:
                    resonance(0, 0)
                if has_p:
                    act.wait_ge(q["qk_ready"], 2 * p + 2)
                    if late(p, 1):
                        act.wait_ge(q["inv_ready"], s)
                    act.wait_ge(q["x1_lo"], p + 1)
                    act.wait_ge(q["x1_hi"], p + 1)
                    if ok(OUT + 1, SLOTS):
                        act.wait_ge(q["x2_lo"], o)
                        act.wait_ge(q["x2_hi"], o)
                    nc.scalar.activation(qk_sq[0:N], qk[0:N], ACT.Square).then_inc(q["sq_ready"], 1)
                if has_a:
                    resonance(0, 1)
                    keep_qT(1)
                if has_p:
                    keep_v(1)
                if has_a:
                    resonance(1, 0)
                    resonance(1, 1)
                if ok(0, SLOTS):
                    act.wait_ge(q["w_loaded"], 16 * (s + 1))
                    nc.scalar.copy(m.w_ffn_hi[:, bass.ds(s, 1)].rearrange("p o c -> p (o c)"), w_stage[:]).then_inc(q["w_hi_ready"], 1)
                    act.wait_ge(q["x1_ready"], s + 1)
                    if late(s, 1):
                        act.wait_ge(q["x1T_done"], s)
                    nc.scalar.copy(x1s[0:N, :, 0, :], x1[0:N]).then_inc(q["x1_hi"], 1)
                if has_o:
                    act.wait_ge(q["x2_ready"], o + 1)
                    if late(o, 1):
                        act.wait_ge(q["x2T_done"], o)
                        act.wait_ge(q["xln_stored"], 16 * o)
                    nc.scalar.copy(x2s[0:N, :, 0, :], x2[0:N]).then_inc(q["x2_hi"], 1)
                if has_p:
                    act.wait_ge(q["qn_ready"], p + 1)
                    if late(p, 1):
                        act.wait_ge(q["kT_done"], 2 * p)
                    for b in range(PAIR):
                        for i, step in enumerate((2, 1)):
                            dst = qks[0:N, b, i * HEADS:(i + 1) * HEADS, 0:step + 1:step, :]
                            src = qk[0:N, b, i * D:(i + 1) * D].rearrange("n (h d) -> n h d", d=HD).unsqueeze(2).to_broadcast([N, HEADS, 2, HD])
                            ins = nc.scalar.copy(dst, src)
                    ins.then_inc(q["qk_hi"], 1)
                if ok(ROUTE, SLOTS):
                    act.wait_ge(q["ex_ready"], s - ROUTE + 1)
                    if late(s - ROUTE, 1):
                        act.wait_ge(q["entry_ready"], s - ROUTE)
                    nc.scalar.activation(sg[0:N, :, 0, :], lg[0:N, :, 3, :], ACT.Sigmoid)
                    nc.scalar.activation(sg[0:N, :, 1, :], lg[0:N, :, 3, :], ACT.Sigmoid, scale=-1.0).then_inc(q["sg_ready"], 1)

            act.wait_ge(q["bias_set"], 1)
            run(act, None, slot)

        @block.gpsimd
        def _(pool):
            nc.gpsimd.memset(zeros[:], 0.0).then_inc(q["zero_ready"], 1)
            nc.gpsimd.memset(sig_bias[:], -THRESH * SHARP).then_inc(q["bias_set"], 1)
            nc.gpsimd.memset(v_pad[:], 0.0).then_inc(q["pad_zero"], 1)
            nc.gpsimd.memset(qks[:, :, :, 3, :], 0.0).then_inc(q["pad_zero"], 1)
            pool.wait_ge(q["table_zero"], 32)

            def slot(s, k, ok):
                p, o, c = s - PROJ, s - OUT, s - PLACE
                late = lambda x, n: not isinstance(x, int) or x >= n
                if ok(PLACE, SLOTS):
                    wait_before_dma(pool, (q["table_zero"], 32), (q["entry_ready"], c + 1))
                    for b in range(PAIR):
                        for i in range(2):
                            nc.gpsimd.indirect_dma_start(dram["table"], bass.IndirectOffsetOnAxis(ap=slot_i[0:N, b, i:i + 1], axis=0),
                                                         entry[0:N, b, i, :], None).then_inc(q["scattered"], 16)
                if ok(0, SLOTS):
                    pool.wait_ge(q["x1_ready"], s + 1)
                    nc.gpsimd.tensor_tensor(h[0:N, k], h[0:N, k], m.bo[0:N].unsqueeze(1).to_broadcast([N, PAIR, D]), ALU.add).then_inc(q["bo_added"], 1)
                if ok(PROJ, SLOTS):
                    pool.wait_ge(q["inv_ready"], s + 1)
                    nc.gpsimd.tensor_tensor(qk[0:N].rearrange("n b (h d) -> n (b h) d", d=HD), qk[0:N].rearrange("n b (h d) -> n (b h) d", d=HD),
                                            inv[0:N, k % 2, NQK:NV2].unsqueeze(2).to_broadcast([N, PAIR * 2 * HEADS, HD]), ALU.mult).then_inc(q["qn_ready"], 1)
                if ok(0, SLOTS):
                    pool.wait_ge(q["x1_hi"], s + 1)
                    nc.gpsimd.tensor_tensor(x1s[0:N, :, 1, :], x1[0:N], x1s[0:N, :, 0, :], ALU.subtract).then_inc(q["x1_lo"], 1)
                    pool.wait_ge(q["w_hi_ready"], s + 1)
                    nc.gpsimd.tensor_tensor(m.w_ffn_lo[:, bass.ds(s, 1)].rearrange("p o c -> p (o c)"), w_stage[:],
                                            m.w_ffn_hi[:, bass.ds(s, 1)].rearrange("p o c -> p (o c)"), ALU.subtract).then_inc(q["w_lo_ready"], 1)
                if ok(OUT, SLOTS):
                    pool.wait_ge(q["x2_hi"], o + 1)
                    nc.gpsimd.tensor_tensor(x2s[0:N, :, 1, :], x2[0:N], x2s[0:N, :, 0, :], ALU.subtract).then_inc(q["x2_lo"], 1)

            run(pool, None, slot)
            pool.wait_ge(q["scattered"], 16 * 4 * SLOTS)

        @block.vector
        def _(dve):
            st = Steps(dve, q["dve_steps2"])
            v = nc.vector
            st.mark(v.memset(squares[:], 1.0))
            st.mark(v.memset(inv[:], 1.0))
            dve.wait_ge(q["pad_zero"], 2)
            st.settle()

            def slot(s, k, ok):
                p, a, o, r, c = s - PROJ, s - ATT, s - OUT, s - ROUTE, s - PLACE
                has_p, has_a, has_o = ok(PROJ, SLOTS), ok(ATT, SLOTS), ok(OUT, SLOTS)
                late = lambda x, n: not isinstance(x, int) or x >= n
                now, was = inv[0:N, k % 2], inv[0:N, (k + 1) % 2]

                if ok(PLACE, SLOTS):
                    dve.wait_ge(q["pos_done"], c + 1)
                    W = 2 * E
                    placed = m.placed[:]
                    st.mark(v.tensor_tensor(places[0:N].rearrange("n b c e -> n b (c e)"), bT[0:N, 0:PAIR * W].rearrange("n (b w) -> n b w", w=W),
                                            placed[0:N].unsqueeze(1).to_broadcast([N, PAIR, W]), ALU.add))
                    v.tensor_copy(sum12[:], bT[:, 2 * W:3 * W]).then_inc(q["pos_read"], 1)
                    st.settle()
                    dve.wait_ge(q["pos_read"], c + 1)
                    st.mark(v.tensor_tensor(m.placed[:], placed, sum12[:], ALU.add))
                    st.mark(v.tensor_tensor(places[0:N], places[0:N], m.sign[0:N].rearrange('p (c e) -> p c e', c=2).unsqueeze(1).to_broadcast([N, PAIR, 2, E]), ALU.mult))
                    st.settle()
                    st.do(v.tensor_tensor(places[0:N], places[0:N], m.centre[0:N].rearrange('p (c e) -> p c e', c=2).unsqueeze(1).to_broadcast([N, PAIR, 2, E]), ALU.add))
                    st.do(v.tensor_tensor(places[0:N], places[0:N], masks[0:N], ALU.mult))
                    if late(c, 1):
                        dve.wait_ge(q["scattered"], 64 * c)
                    st.mark(v.tensor_reduce(slot_f[0:N], places[0:N], AX.X, ALU.add))
                    dve.wait_ge(q["sg_ready"], c + 1)
                    col = lambda i: top[0:N, :, i:i + 1]
                    M2, EX = lg[0:N, :, 2, :], lg[0:N, :, 3, :]
                    st.do(v.reciprocal(EX, sg[0:N, :, 1, :]))
                    st.do(v.tensor_tensor(EX, EX, sg[0:N, :, 0, :], ALU.mult))
                    st.mark(v.tensor_reduce(col(2), EX, AX.X, ALU.add))
                    st.do(v.tensor_tensor(EX, EX, M2, ALU.mult))
                    st.mark(v.tensor_reduce(col(3), EX, AX.X, ALU.add))
                    st.do(v.reciprocal(col(2), col(2)))
                    st.do(v.tensor_tensor(col(3), col(3), col(2), ALU.mult))
                    st.do(v.tensor_scalar(col(6), col(2), 1e-9, None, ALU.add))
                    st.do(v.tensor_tensor(col(6), col(6), col(3), ALU.add))
                    st.do(v.reciprocal(col(6), col(6)))
                    st.mark(v.tensor_tensor(col(4), col(2), col(6), ALU.mult))
                    st.do(v.tensor_tensor(col(5), col(3), col(6), ALU.mult))
                    st.mark(v.tensor_copy(entry[0:N, :, :, 0], m.token_id[0:N].unsqueeze(2).to_broadcast([N, PAIR, 2])))
                    st.mark(v.tensor_copy(entry[0:N, :, :, 1], top[0:N, :, 4:6]))
                    st.settle()
                    v.tensor_copy(slot_i[0:N], slot_f[0:N]).then_inc(q["entry_ready"], 1)
                    st.mark(v.tensor_scalar(m.token_id[0:N], m.token_id[0:N], float(PAIR * N), None, ALU.add))
                if has_p:
                    dve.wait_ge(q["x1T_done"], p + 1)
                    if late(p, 1):
                        dve.wait_ge(q["v_done"], 2 * p)
                    v.tensor_copy(x1T[:], xT_ps).then_inc(q["x1T_ready"], 1)

                def scaled_qk(b):
                    dve.wait_ge(q["qk_done"], 2 * p + b + 1)
                    if late(p, 1) and b == 0:
                        dve.wait_ge(q["qk_hi"], p)
                        dve.wait_ge(q["qk_lo"], p)
                    v.scalar_tensor_tensor(out=qk[0:N, b], in0=bQK[b][0:N, :], scalar=was[:, NR2 + b:NR2 + b + 1], in1=m.bias_qk[0:N],
                                           op0=ALU.mult, op1=ALU.add).then_inc(q["qk_ready"], 1)

                def keep_kT(b):
                    n = 2 * a + b
                    dve.wait_ge(q["kT_done"], n + 1)
                    if late(n, 2):
                        dve.wait_ge(q["score_done"], 4 * n - 4)
                    v.tensor_copy(kT[:, b], kt_ps).then_inc(q["kT_ready"], 1)

                def gate_and_split(b):
                    n = 2 * a + b
                    dve.wait_ge(q["col_done"], 3 * n + 3)
                    if b == 0 and late(a, 1):
                        dve.wait_ge(q["wo_done"], a)
                    st.do(v.tensor_copy(cT[:], bC[:, 2 * N:4 * N].rearrange("p (k n) -> p k n", n=N)))
                    st.do(v.tensor_tensor(cT[:], bC[:, 0:2 * N].rearrange("p (k n) -> p k n", n=N), cT[:], ALU.mult))
                    st.do(v.tensor_copy(cTs[:, b, 0], cT[:]))
                    v.tensor_tensor(cTs[:, b, 1], cT[:], cTs[:, b, 0], ALU.subtract).then_inc(q["c_ready"], 1)

                if has_p:
                    scaled_qk(0)
                if has_a:
                    keep_kT(0)
                if has_p:
                    scaled_qk(1)
                if has_o:
                    dve.wait_ge(q["wo_done"], o + 1)
                    dve.wait_ge(q["bo_added"], o + 1)
                    if late(o, 1):
                        dve.wait_ge(q["out_stored"], 16 * o)
                    ins = v.tensor_tensor(h2[0:N], bV[0:N, :].rearrange("n (b d) -> n b d", b=PAIR), h[0:N, (k - OUT) % RING], ALU.add)
                    ins.then_inc(q["h2_ready"], 1)
                if has_a:
                    keep_kT(1)
                    gate_and_split(0)
                if ok(0, SLOTS):
                    dve.wait_ge(h_loaded[k], (s - k) * (32 // RING) + 32)
                    for b in range(PAIR):
                        st.mark(v.bn_stats(stats[0:N, 0, b], h[0:N, k, b]))
                if has_o:
                    dve.wait_ge(q["h2_ready"], o + 1)
                    for b in range(PAIR):
                        st.mark(v.bn_stats(stats[0:N, 1, b], h2[0:N, b]))
                if ok(0, SLOTS) or has_o:
                    st.settle()
                if has_p:
                    dve.wait_ge(q["sq_ready"], p + 1)
                    st.mark(v.tensor_reduce(squares[0:N, NQK:NV2], qk_sq[0:N].rearrange("n b (h d) -> n (b h) d", d=HD), AX.X, ALU.add))
                if ok(0, SLOTS):
                    for b in range(PAIR):
                        st.mark(v.bn_aggr(mv[0:N, 0, b], stats[0:N, 0, b]))
                if has_o:
                    for b in range(PAIR):
                        st.mark(v.bn_aggr(mv[0:N, 1, b], stats[0:N, 1, b]))
                st.settle()
                if has_p:
                    st.mark(v.tensor_scalar(squares[0:N, NQK:NV2], squares[0:N, NQK:NV2], NORM_EPS * NORM_EPS, None, ALU.max))
                if has_o:
                    st.mark(v.tensor_scalar(squares[0:N, NV2:NV1], mv[0:N, 1, :, 1], LN_EPS, None, ALU.add))
                if ok(0, SLOTS):
                    st.do(v.tensor_scalar(squares[0:N, NV1:NR2], mv[0:N, 0, :, 1], LN_EPS, None, ALU.add))
                    st.do(v.reciprocal(squares[0:N, NR2:NCOLS], squares[0:N, NV1:NR2]))
                    st.do(v.tensor_tensor(squares[0:N, NR2:NCOLS], squares[0:N, NR2:NCOLS], mv[0:N, 0, :, 1], ALU.mult))
                    st.mark(v.tensor_scalar(squares[0:N, NR2:NCOLS], squares[0:N, NR2:NCOLS], LN_EPS, None, ALU.add))
                if ok(0, SLOTS) or has_p or has_o:
                    if late(s, 3):
                        dve.wait_ge(q["qn_ready"], s - 2)
                    st.settle()
                    inverse_sqrt(nc, st, q["inv_ready"], now, squares[0:N], inv_t[0:N])
                    dve.wait_ge(q["inv_ready"], s + 1)
                if ok(0, SLOTS):
                    if late(s, 1):
                        dve.wait_ge(q["x1_hi"], s)
                        dve.wait_ge(q["x1_lo"], s)
                    for b in range(PAIR):
                        ins = v.tensor_scalar(x1[0:N, b], h[0:N, k, b], mv[0:N, 0, b, 0:1], now[:, NV1 + b:NV1 + b + 1], ALU.subtract, ALU.mult)
                    ins.then_inc(q["x1_ready"], 1)
                if has_o:
                    if late(o, 1):
                        dve.wait_ge(q["x2_hi"], o)
                        dve.wait_ge(q["x2_lo"], o)
                    for b in range(PAIR):
                        ins = v.tensor_scalar(x2[0:N, b], h2[0:N, b], mv[0:N, 1, b, 0:1], now[:, NV2 + b:NV2 + b + 1], ALU.subtract, ALU.mult)
                    ins.then_inc(q["x2_ready"], 1)
                if ok(ROUTE, SLOTS):
                    dve.wait_ge(q["x2T_done"], r + 1)
                    if late(r, 1):
                        dve.wait_ge(q["lg_done"], r)
                    v.tensor_copy(x2T[:], xT_ps).then_inc(q["x2T_ready"], 1)
                if has_a:
                    gate_and_split(1)
                if has_p:
                    dve.wait_ge(q["v_copied"], 2 * p + 2)
                    for b in range(PAIR):
                        st.mark(v.scalar_tensor_tensor(out=gate[0:N, b], in0=vg[0:N, b, D:], scalar=was[:, NR2 + b:NR2 + b + 1], in1=m.bias_gate[0:N],
                                                       op0=ALU.mult, op1=ALU.add))
                    st.settle()
                    st.do(v.tensor_tensor(gate[0:N], gate[0:N], now[:, NQK:NV2].rearrange("n (b h) -> n b h", b=PAIR), ALU.mult))
                    st.mark(v.tensor_copy(gate_q[0:N], gate[0:N, :, 0:HEADS].unsqueeze(3).to_broadcast([N, PAIR, HEADS, HD])))
                    for b in range(PAIR):
                        for u in range(2):
                            ins = v.tensor_tensor(v_pad[0:N, b].rearrange("n (j u) c -> n j u c", u=2)[:, :, u, u * HD:(u + 1) * HD],
                                                  vg[0:N, b, 0:D].rearrange("n (j u d) -> n j u d", u=2, d=HD)[:, :, u, :],
                                                  gate[0:N, b, HEADS:].rearrange("n (j u) -> n j u", u=2)[:, :, u:u + 1].to_broadcast([N, HALF, HD]), ALU.mult)
                            if b == 1 and u == 1:
                                ins.then_inc(q["vgate_ready"], 1)
                            else:
                                st.mark(ins)
                if ok(ROUTE, SLOTS):
                    dve.wait_ge(q["lg_done"], r + 1)
                    if late(r, 1):
                        dve.wait_ge(q["pos_done"], r)
                    L, M1, M2, EX, T1 = [lg[0:N, :, i, :] for i in range(5)]
                    wide = lambda ap: ap.to_broadcast([N, PAIR, E])
                    col = lambda i: top[0:N, :, i:i + 1]
                    iota = m.rev_e[0:N].unsqueeze(1).to_broadcast([N, PAIR, E])
                    v.tensor_copy(L, bT[0:N, 0:PAIR * E].rearrange("n (b e) -> n b e", e=E)).then_inc(q["lg_read"], 1)
                    dve.wait_ge(q["lg_read"], r + 1)

                    def choose(x, mask, best):
                        st.do(v.tensor_reduce(col(best), x, AX.X, ALU.max))
                        st.do(v.tensor_tensor(mask, x, wide(col(best)), ALU.is_equal))
                        st.do(v.tensor_tensor(mask, mask, iota, ALU.mult))
                        st.do(v.tensor_reduce(col(2), mask, AX.X, ALU.max))
                        st.do(v.tensor_tensor(mask, mask, wide(col(2)), ALU.is_equal))

                    choose(L, M1, 0)
                    st.do(v.scalar_tensor_tensor(out=T1, in0=M1, scalar=-3.0e38, in1=L, op0=ALU.mult, op1=ALU.add))
                    choose(T1, M2, 1)
                    st.mark(v.tensor_copy(masks[0:N, :, 0, :], M1))
                    v.tensor_copy(masks[0:N, :, 1, :], M2).then_inc(q["masks_ready"], 1)
                    v.tensor_tensor(EX, L, wide(col(0)), ALU.subtract).then_inc(q["ex_ready"], 1)
                if has_p:
                    dve.wait_ge(q["qk_hi"], p + 1)
                    for i in range(2):
                        ins = v.tensor_tensor(qks[0:N, :, i * HEADS:(i + 1) * HEADS, 1 + i, :],
                                              qk[0:N, :, i * D:(i + 1) * D].rearrange("n b (h d) -> n b h d", d=HD),
                                              qks[0:N, :, i * HEADS:(i + 1) * HEADS, 0, :], ALU.subtract)
                        if i == 0:
                            st.mark(ins)
                    ins.then_inc(q["qk_lo"], 1)

            run(dve, st, slot)
            st.settle()


def plan_tiles(nc, m):
    with ExitStack() as ctx:
        sb = lambda n, s: ctx.enter_context(nc.sbuf_tensor(n, s, F32))
        first, second, count, tiles, begin, end, v_start, v_left = [sb(n, [P, E]) for n in (
            "first", "second", "count", "tiles", "begin", "end", "v_start", "v_left")]
        tiles_i = ctx.enter_context(nc.sbuf_tensor("tiles_i", [P, E], I32))
        before = sb("before", [P, E, E])
        own, other = sb("own", [P, TILES, E]), sb("other", [P, TILES, E])
        any_, expert, start, left, rows = [sb(n, [P, TILES]) for n in ("any", "expert", "start", "left", "rows")]
        dve_steps = ctx.enter_context(nc.semaphore("dve_steps3"))
        block = ctx.enter_context(nc.Block())

        @block.vector
        def _(dve):
            st = Steps(dve, dve_steps)
            v = nc.vector
            n1, n2 = m.placed[:, 0:E], m.placed[:, E:2 * E]
            st.do(v.tensor_scalar(first[:], n1, float(CAP), None, ALU.min))
            st.do(v.tensor_scalar(second[:], n1, -1.0, float(CAP), ALU.mult, ALU.add))
            st.do(v.tensor_tensor(second[:], second[:], n2, ALU.min))
            st.do(v.tensor_scalar(second[:], second[:], 0.0, None, ALU.max))
            st.do(v.tensor_tensor(count[:], first[:], second[:], ALU.add))
            st.do(v.tensor_scalar(tiles_i[:], count[:], float(TILE - 1), None, ALU.add))
            st.do(v.tensor_scalar(tiles_i[:], tiles_i[:], TILE.bit_length() - 1, None, ALU.arith_shift_right))
            st.do(v.tensor_copy(tiles[:], tiles_i[:]))
            st.do(v.tensor_tensor(before[:], m.below.rearrange("p (a b) -> p a b", a=E), tiles[:].unsqueeze(1).to_broadcast([P, E, E]), ALU.mult))
            st.do(v.tensor_reduce(begin[:], before[:], AX.X, ALU.add))
            st.do(v.tensor_tensor(end[:], begin[:], tiles[:], ALU.add))
            t_of = m.tile_no.unsqueeze(2).to_broadcast([P, TILES, E])
            over = lambda ap: ap.unsqueeze(1).to_broadcast([P, TILES, E])
            st.do(v.tensor_tensor(own[:], t_of, over(begin[:]), ALU.is_ge))
            st.do(v.tensor_tensor(other[:], t_of, over(end[:]), ALU.is_ge))
            st.do(v.tensor_tensor(own[:], own[:], other[:], ALU.subtract))
            st.do(v.scalar_tensor_tensor(out=v_start[:], in0=begin[:], scalar=float(-TILE), in1=m.centre_e, op0=ALU.mult, op1=ALU.add))
            st.do(v.tensor_tensor(v_start[:], v_start[:], first[:], ALU.subtract))
            st.do(v.scalar_tensor_tensor(out=v_left[:], in0=begin[:], scalar=float(TILE), in1=count[:], op0=ALU.mult, op1=ALU.add))
            st.do(v.tensor_reduce(any_[:], own[:], AX.X, ALU.add))
            for value, out in ((m.index_e, expert), (v_start[:], start), (v_left[:], left)):
                st.do(v.tensor_tensor(other[:], own[:], over(value), ALU.mult))
                st.do(v.tensor_reduce(out[:], other[:], AX.X, ALU.add))
            st.do(v.tensor_tensor(rows[:], m.tile_no, any_[:], ALU.mult))
            st.do(v.tensor_scalar(rows[:], rows[:], float(TILE), None, ALU.mult))
            st.do(v.tensor_tensor(start[:], start[:], rows[:], ALU.add))
            st.do(v.tensor_tensor(left[:], left[:], rows[:], ALU.subtract))
            for h in range(PARTS):
                st.do(v.tensor_tensor(m.valid[:, :, h], left[:], m.pos_p[:, h:h + 1].to_broadcast([P, TILES]), ALU.is_gt))
            st.do(v.tensor_copy(m.tile_info[:, 0, :], expert[:]))
            st.do(v.tensor_copy(m.tile_info[:, 1, :], start[:]))


def expert_tiles(nc, m, dram):
    UP, DOWN = 1, 2
    TOTAL = TILES + DOWN
    LOOP_FROM, UNROLL = 4, 2
    with ExitStack() as ctx:
        sb = lambda n, s, d: ctx.enter_context(nc.sbuf_tensor(n, s, d))
        sem = lambda n: ctx.enter_context(nc.semaphore(n))
        pb = lambda n: ctx.enter_context(nc.psum_tensor(n, [P, 512], F32))
        b2_rows = sb("b2_rows", [P, E, D], BF16)
        tab = sb("tab", [P, 2, PARTS, 2], F32)
        away = sb("away", [P, PARTS, 2], F32)
        kept = sb("kept", [P, 2, PARTS, 2], F32)
        from_id = sb("from_id", [P, 2, PARTS], U32)
        to_id = sb("to_id", [P, 2, PARTS], U32)
        weight = sb("weight", [P, 2, PARTS], F32)
        x = sb("x", [P, 2, PARTS, 2 * D], BF16)
        xT = sb("xT", [P, 2, 4, TILE], BF16)
        act_f = sb("act_f", [P, FC, TILE], F32)
        act_hi = sb("act_hi", [P, 2, FC, TILE], BF16)
        act_lo = sb("act_lo", [P, 2, FC, TILE], BF16)
        y = sb("y", [P, 2, PARTS, D], F32)
        bX = pb("bX")
        bH = [pb(f"bH{i}") for i in range(FC // 2)]
        bY = [pb(f"bY{i}") for i in range(2)]
        x_ps = bX[:, :].bitcast(BF16).rearrange("p (c n) -> p c n", c=4)
        names = """b2_in b2_zero ids_ready weight_ready gathered0 gathered1 turned turned_kept up_done gelu_ready act_ready
            down_done y_ready added dve_steps4 tab_in0 tab_in1""".split()
        q = {n: sem(n) for n in names}
        tab_in = [q["tab_in0"], q["tab_in1"]]
        gathered = [q["gathered0"], q["gathered1"]]
        block = ctx.enter_context(nc.Block())
        late = lambda v, n: not isinstance(v, int) or v >= n

        def run(eng, steps, slot):
            slots(eng, steps, slot, DOWN, LOOP_FROM, UNROLL, (TILES - LOOP_FROM) // UNROLL, TOTAL)

        def info(eng, which, t, top):
            return eng.value_load(m.tile_info[0:1, which, bass.ds(t, 1)], min_val=0, max_val=top)

        def uses(s, k, each):
            return (s - k % 2) * (each // 2) + each

        @block.sync
        def _(sp):
            sp.wait_ge(q["b2_zero"], 1)
            sp.dma_start(b2_rows[0:3].rearrange("p e d -> p (e d)"), dram["bias_parts"][:, D:]).then_inc(q["b2_in"], 16)

            def slot(s, k, ok):
                if ok(0, TILES):
                    if late(s, 2):
                        sp.wait_ge(q["ids_ready"], s - 1)
                    start = info(sp, 1, s, E * ROWS - TILE)
                    sp.dma_start(tab[:, k % 2], dram["table"][bass.ds(start, TILE), :].rearrange("(h p) c -> p h c", p=P)).then_inc(tab_in[k % 2], 16)

            run(sp, None, slot)
            sp.wait_ge(q["added"], 16 * PARTS * TILES)

        @block.gpsimd
        def _(pool):
            nc.gpsimd.memset(b2_rows[:], 0.0).then_inc(q["b2_zero"], 1)

            def add(d, k, h):
                before = [(q["added"], 16 * (PARTS * d + h))] if h or late(d, 1) else []
                wait_before_dma(pool, (q["b2_zero"], 1), *([] if h else [(q["y_ready"], d + 1)]), *before)
                nc.gpsimd.indirect_dma_start(dram["out"], bass.IndirectOffsetOnAxis(ap=to_id[:, k % 2, h:h + 1], axis=0),
                                             y[:, k % 2, h], None, compute_op=ALU.add).then_inc(q["added"], 16)

            def slot(s, k, ok):
                d = s - DOWN
                if ok(0, TILES):
                    wait_before_dma(pool, (q["b2_zero"], 1), (q["ids_ready"], s + 1), *([(q["turned"], s - 1)] if late(s, 2) else []))
                    for h in range(PARTS):
                        nc.gpsimd.indirect_dma_start(x[:, k % 2, h], None, dram["xln"], bass.IndirectOffsetOnAxis(ap=from_id[:, k % 2, h:h + 1], axis=0)
                                                     ).then_inc(gathered[k % 2], 16)
                if ok(DOWN, TILES):
                    for h in range(PARTS):
                        add(d, k, h)

            run(pool, None, slot)

        @block.tensor
        def _(pe):
            pe.wait_ge(q["b2_in"], 16)

            def slot(s, k, ok):
                u, d = s - UP, s - DOWN
                if ok(DOWN, TILES):
                    e_down = info(pe, 0, d, E - 1)
                if ok(UP, TILES):
                    e_up = info(pe, 0, u, E - 1)
                    pe.wait_ge(gathered[(k - UP) % 2], uses(u, k - UP, 16 * PARTS))
                    if late(u, 1):
                        pe.wait_ge(q["turned_kept"], u)
                    for c in range(4):
                        for h in range(PARTS):
                            mm = nc.tensor.transpose(x_ps[:, c, h * P:(h + 1) * P], x[:, (k - UP) % 2, h, c * P:(c + 1) * P], m.ident[:])
                    mm.then_inc(q["turned"], 1)
                if ok(DOWN, TILES):
                    at = k % 2
                    if late(d, 2):
                        pe.wait_ge(q["y_ready"], d - 1)
                    for h in range(PARTS):
                        rows = slice(h * P, (h + 1) * P)
                        out = bY[at][:, h * D:(h + 1) * D]
                        nc.tensor.matmul(out, m.ones[:], b2_rows[:, bass.ds(e_down, 1), :].rearrange("p o d -> p (o d)"), start=True, stop=False)
                        for f in range(FC):
                            if h == 0 and f % 2 == 0:
                                pe.wait_ge(q["act_ready"], (FC // 2) * d + f // 2 + 1)
                            for a, w in ((act_hi, m.w_ffn_hi), (act_lo, m.w_ffn_hi), (act_hi, m.w_ffn_lo)):
                                rhs = w[:, bass.ds(2 * e_down + (2 * E + f // 4), 1), (f % 4) * D:(f % 4 + 1) * D].rearrange("p o d -> p (o d)")
                                mm = nc.tensor.matmul(out, a[:, at, f, rows], rhs, start=False, stop=f == FC - 1 and w is m.w_ffn_lo)
                    mm.then_inc(q["down_done"], 1)
                if ok(UP, TILES):
                    at = (k - UP) % 2
                    pe.wait_ge(q["turned_kept"], u + 1)
                    for b in range(FC // 2):
                        if late(u, 1):
                            pe.wait_ge(q["gelu_ready"], (FC // 2) * (u - 1) + b + 1)
                        for f in range(2):
                            parts = [(p, w, kc) for kc in range(KC) for p, w in ((0, m.w_ffn_hi), (1, m.w_ffn_hi), (0, m.w_ffn_lo))]
                            for i, (p, w, kc) in enumerate(parts):
                                lhs = w[:, bass.ds(2 * e_up + kc, 1), (2 * b + f) * P:(2 * b + f + 1) * P].rearrange("p o d -> p (o d)")
                                mm = nc.tensor.matmul(bH[b][:, f * TILE:(f + 1) * TILE], lhs, xT[:, at, 2 * p + kc, :],
                                                      start=i == 0, stop=i == len(parts) - 1)
                        mm.then_inc(q["up_done"], 1)

            run(pe, None, slot)

        @block.scalar
        def _(act):
            def slot(s, k, ok):
                u = s - UP
                if ok(UP, TILES):
                    at = (k - UP) % 2
                    e = info(act, 0, u, E - 1)
                    act.wait_ge(q["turned"], u + 1)
                    if late(u, 2):
                        act.wait_ge(q["up_done"], (FC // 2) * (u - 1))
                    nc.scalar.copy(xT[:, at], x_ps).then_inc(q["turned_kept"], 1)
                    for b in range(FC // 2):
                        act.wait_ge(q["up_done"], (FC // 2) * u + b + 1)
                        if late(u, 1):
                            act.wait_ge(q["act_ready"], (FC // 2) * (u - 1) + b + 1)
                        for f in range(2):
                            ins = nc.scalar.activation(act_f[:, 2 * b + f, :], bH[b][:, f * TILE:(f + 1) * TILE], ACT.Gelu,
                                                       bias=m.b1[:, bass.ds(e * FC + (2 * b + f), 1)])
                        ins.then_inc(q["gelu_ready"], 1)

            run(act, None, slot)

        @block.vector
        def _(dve):
            st = Steps(dve, q["dve_steps4"])
            v = nc.vector

            def slot(s, k, ok):
                u, d = s - UP, s - DOWN
                if ok(DOWN, TILES):
                    at = k % 2
                    if late(d, 2):
                        dve.wait_ge(q["added"], 16 * PARTS * (d - 1))
                    st.mark(v.tensor_tensor(to_id[:, at], kept[:, at, :, 0], m.away.rearrange("p (h c) -> p h c", c=2)[:, :, 0], ALU.add))
                    st.do(v.tensor_copy(weight[:, at], kept[:, at, :, 1]))
                if ok(0, TILES):
                    at = k % 2
                    dve.wait_ge(tab_in[at], uses(s, k, 16))
                    if late(s, 2):
                        dve.wait_ge(gathered[at], uses(s, k, 16 * PARTS) - 16 * PARTS)
                    st.mark(v.tensor_copy(from_id[:, at], tab[:, at, :, 0]))
                    st.do(v.tensor_tensor(away[:], tab[:, at], m.away.rearrange("p (h c) -> p h c", c=2), ALU.subtract))
                    v.tensor_tensor(kept[:, at], away[:], m.valid[:, bass.ds(s, 1), :].rearrange("p o h -> p h o").to_broadcast([P, PARTS, 2]),
                                    ALU.mult).then_inc(q["ids_ready"], 1)
                    dve.wait_ge(q["ids_ready"], s + 1)
                if ok(UP, TILES):
                    at = (k - UP) % 2
                    for b in range(FC // 2):
                        part = slice(2 * b, 2 * b + 2)
                        dve.wait_ge(q["gelu_ready"], (FC // 2) * u + b + 1)
                        if late(u, 2):
                            dve.wait_ge(q["down_done"], u - 1)
                        st.do(v.tensor_copy(act_hi[:, at, part], act_f[:, part]))
                        v.tensor_tensor(act_lo[:, at, part], act_f[:, part], act_hi[:, at, part], ALU.subtract).then_inc(q["act_ready"], 1)
                        if b == 0 and ok(DOWN, TILES):
                            weigh(d, k % 2)
                elif ok(DOWN, TILES):
                    weigh(d, k % 2)

            def weigh(d, at):
                dve.wait_ge(q["down_done"], d + 1)
                for h in range(PARTS):
                    ins = v.tensor_scalar(y[:, at, h], bY[at][:, h * D:(h + 1) * D], weight[:, at, h:h + 1], None, ALU.mult)
                    if h == 0:
                        st.mark(ins)
                ins.then_inc(q["y_ready"], 1)

            run(dve, st, slot)
            st.settle()


CONSTS = {"ident_f": P, "tri_f": P, "rev_e": E, "index_e": E, "sign": 2 * E, "centre": 2 * E, "centre_e": E,
          "first_tokens": PAIR, "pos_p": PARTS, "away": 2 * PARTS, "below": E * E, "tile_no": TILES}


def constants():
    p, e = np.arange(P), np.arange(E)
    wide = lambda x: np.broadcast_to(np.asarray(x).reshape(1, -1), (P, np.size(x)))
    tables = {
        "ident_f": np.eye(P),
        "tri_f": p[:, None] < p[None, :],
        "rev_e": wide(E - e),
        "index_e": wide(e),
        "sign": wide(np.repeat([-1, 1], E)),
        "centre": wide(np.concatenate([e * ROWS + CENTRE - 1, e * ROWS + CENTRE])),
        "centre_e": wide(e * ROWS + CENTRE),
        "first_tokens": np.arange(PAIR)[None, :] * N + p[:, None],
        "pos_p": np.stack([p + h * P for h in range(PARTS)], axis=1),
        "away": np.stack([TOKENS + p, 0 * p] * PARTS, axis=1),
        "below": wide(e[None, :] < e[:, None]),
        "tile_no": wide(np.arange(TILES)),
    }
    return np.concatenate([tables[n].astype(np.float32) for n in CONSTS], axis=1)


class Kept:

    def __init__(self, nc, ctx):
        sb = lambda n, s, d: ctx.enter_context(nc.sbuf_tensor(n, s, d))
        self.w_ffn_hi = sb("w_ffn_hi", [P, WCHUNKS, WCH], BF16)
        self.w_ffn_lo = sb("w_ffn_lo", [P, WCHUNKS, WCH], BF16)
        self.w_hi = sb("w_hi", [P, KC, QKV], BF16)
        self.w_lo = sb("w_lo", [P, KC, QKV], BF16)
        self.w_out_hi = sb("w_out_hi", [P, KC, D], BF16)
        self.w_out_lo = sb("w_out_lo", [P, KC, D], BF16)
        self.w_gate_hi = sb("w_gate_hi", [P, KC, E], BF16)
        self.w_gate_lo = sb("w_gate_lo", [P, KC, E], BF16)
        self.bias_qk = sb("bias_qk", [P, 2 * D], F32)
        self.bias_gate = sb("bias_gate", [P, 2 * HEADS], F32)
        self.bo = sb("bo", [P, D], F32)
        self.b1 = sb("b1", [P, E * FC], F32)
        self.ident = sb("ident", [P, P], BF16)
        self.tri = sb("tri", [P, P], BF16)
        self.ones = sb("ones", [P, P], BF16)
        self.token_id = sb("token_id", [P, PAIR], F32)
        self.placed = sb("placed", [P, 2 * E], F32)
        self.valid = sb("valid", [P, TILES, PARTS], F32)
        self.tile_info = sb("tile_info", [P, 2, TILES], I32)
        self.consts = sb("consts", [P, sum(CONSTS.values())], F32)
        at = {}
        col = 0
        for name, width in CONSTS.items():
            at[name] = self.consts[:, col:col + width]
            col += width
        self.ident_f, self.tri_f, self.rev_e, self.index_e = at["ident_f"], at["tri_f"], at["rev_e"], at["index_e"]
        self.sign, self.centre, self.centre_e = at["sign"], at["centre"], at["centre_e"]
        self.first_tokens, self.pos_p, self.away = at["first_tokens"], at["pos_p"], at["away"]
        self.below, self.tile_no = at["below"], at["tile_no"]


def build(nc, dram):
    dram = dict(dram)
    dram["tok"] = nc.dram_tensor("tok_rows", [B * N_PATCH, D], F32, kind="Internal").ap()
    dram["bias_parts"] = nc.dram_tensor("bias_part_rows", [3, (E + 1) * D], BF16, kind="Internal").ap()
    dram["xln"] = nc.dram_tensor("xln_rows", [TOKENS, 2 * D], BF16, kind="Internal").ap()
    dram["table"] = nc.dram_tensor("table_rows", [E * ROWS, 2], F32, kind="Internal").ap()
    with ExitStack() as ctx:
        m = Kept(nc, ctx)
        prepare_and_tokenise(nc, m, dram)
        fusion_attention(nc, m, dram)
        plan_tiles(nc, m)
        expert_tiles(nc, m, dram)


def kernel(**inputs):
    import concourse.bacc as bacc
    from concourse.bass_utils import run_bass_kernel_spmd

    a = {k: np.asarray(v) for k, v in inputs.items()}
    img = a["x"][:, :, :GRID * PATCH, :GRID * PATCH].reshape(B, C_IN, GRID, PATCH, GRID, PATCH)
    patches = img.transpose(0, 1, 3, 5, 2, 4).reshape(B * N_PATCH, FLATC, P).transpose(2, 1, 0)
    rows = lambda w: w.reshape(KC, P, -1).transpose(1, 0, 2)
    w1 = a["L0_ffn_W1"].reshape(E * KC, P, F)
    w2 = a["L0_ffn_W2"].reshape(E * 2, 4, P, D).transpose(0, 2, 1, 3).reshape(E * 2, P, 4 * D)
    arrays = {
        "patches": patches,
        "txt": a["txt"],
        "w_tok": a["L0_tok_W"].reshape(FLATC, P, D).transpose(1, 0, 2),
        "w_qk": np.concatenate([rows(a["L0_attn_Wq"]), rows(a["L0_attn_Wk"])], axis=2),
        "w_v": rows(a["L0_attn_Wv"]),
        "w_o": rows(a["L0_attn_Wo"]),
        "w_g": rows(a["L0_ffn_Wg"]),
        "ln_w": a["L0_attn_ln_w"].reshape(KC, P).T,
        "ln_b": a["L0_attn_ln_b"].reshape(KC, P).T,
        "gq": a["L0_attn_gq"],
        "gk": a["L0_attn_gk"],
        "bo": a["L0_attn_bo"],
        "w_ffn": np.concatenate([w1, w2], axis=0),
        "b1": a["L0_ffn_b1"].reshape(E * FC, P).T,
        "biases": np.concatenate([a["L0_attn_bo"], a["L0_ffn_b2"].reshape(E * D)]).reshape(P, -1),
        "consts": constants(),
    }
    arrays = {"in_" + k: np.ascontiguousarray(v) for k, v in arrays.items()}
    nc = bacc.Bacc("TRN2", target_bir_lowering=False, num_devices=1)
    dram = {k[3:]: nc.dram_tensor(k, v.shape, mybir.dt.from_np(v.dtype), kind="ExternalInput").ap() for k, v in arrays.items()}
    dram["out"] = nc.dram_tensor("out_rows", (TOKENS + P, D), F32, kind="ExternalOutput").ap()
    build(nc, dram)
    r = run_bass_kernel_spmd(nc, [arrays], core_ids=[0])
    return r.results[0]["out_rows"][:TOKENS].reshape(B, N, D)
```

```python
from contextlib import ExitStack

import numpy as np

import concourse.bass as bass
from concourse import mybir

F32 = mybir.dt.float32
BF16 = mybir.dt.bfloat16
I32 = mybir.dt.int32
U32 = mybir.dt.uint32
ALU = mybir.AluOpType
ACT = mybir.ActivationFunctionType
AX = mybir.AxisListType

P = 128
B, C_IN, IMG, PATCH = 64, 3, 84, 16
GRID = IMG // PATCH
N_PATCH = GRID * GRID
N_TXT = 77
N = N_PATCH + N_TXT
D = 256
KC = D // P
FLAT = C_IN * PATCH * PATCH
FLATC = FLAT // P
TOKENS = B * N
HEADS, HD = 16, 16
THRESH, SHARP = 0.29514, 15.0
LN_EPS, NORM_EPS = 1e-05, 1e-12
E, F = 8, 1024
FC = F // P
CAP = 2 * 2 * TOKENS // E
PAIR = 2
SLOTS = B // PAIR
GROUP = 4
GB = GROUP * PAIR
HALF = HEADS // 2
QKV = 2 * D + D + 2 * HEADS
WCH = 1024
WCHUNKS = 2 * E * KC
TILE, PARTS = 256, 2
TILES = 2 * TOKENS // TILE + E - 1
CENTRE = TOKENS
ROWS = 2 * TOKENS
RSQRT_GUESS = float(0x5F3759DF)
NEWTON_ROUNDS = 3
ATTENTION_STEPS, FFN_STEPS = 159, 18
NQK, NV2, NV1, NR2, NCOLS = 0, 2 * PAIR * HEADS, 2 * PAIR * HEADS + PAIR, 2 * PAIR * HEADS + 2 * PAIR, 2 * PAIR * HEADS + 3 * PAIR


class Steps:

    def __init__(self, eng, sem, per_round=0):
        self.eng, self.sem, self.n, self.base, self.per_round = eng, sem, 0, 0, per_round

    def mark(self, ins):
        self.n += 1
        return ins.then_inc(self.sem, 1)

    def settle(self):
        self.eng.wait_ge(self.sem, self.base + self.n)

    def do(self, ins):
        self.mark(ins)
        self.settle()


def slots(eng, steps, slot, loop_from, unroll, rounds, total):
    def known(s):
        return lambda lag, count: 0 <= s - lag < count
    for s in range(loop_from):
        slot(s, s % unroll, known(s))
    at = steps.n if steps else 0
    with eng.Fori(0, rounds) as it:
        if steps:
            steps.base = it * steps.per_round
        for k in range(unroll):
            slot(it * unroll + (loop_from + k), (loop_from + k) % unroll, lambda lag, count: True)
    if steps:
        assert steps.n - at == steps.per_round, steps.n - at
        steps.base, steps.n = 0, at + steps.per_round * rounds
    for s in range(loop_from + unroll * rounds, total):
        slot(s, s % unroll, known(s))


def wait_before_dma(eng, past, *waits):
    values = [v if isinstance(v, int) else eng.to_reg(v) for _, v in waits]
    eng.wait_ge(*past)
    for (sem, _), value in zip(waits, values):
        eng.wait_ge(sem, value)


def inverse_sqrt(nc, steps, done, y, x, t):
    steps.do(nc.vector.tensor_scalar(y.bitcast(I32), x.bitcast(I32), -0.5, RSQRT_GUESS, ALU.mult, ALU.add))
    for n in range(NEWTON_ROUNDS):
        steps.do(nc.vector.tensor_tensor(t, y, y, ALU.mult))
        steps.do(nc.vector.scalar_tensor_tensor(out=t, in0=t, scalar=-0.5, in1=x, op0=ALU.mult, op1=ALU.mult))
        last = nc.vector.scalar_tensor_tensor(out=y, in0=t, scalar=1.5, in1=y, op0=ALU.add, op1=ALU.mult)
        if n < NEWTON_ROUNDS - 1:
            steps.do(last)
    last.then_inc(done, 1)


def prepare_and_tokenise(nc, m, dram):
    CHUNK, GROUP = 200, 100
    PER = CHUNK // GROUP
    with ExitStack() as ctx:
        sb = lambda n, s, d: ctx.enter_context(nc.sbuf_tensor(n, s, d))
        sem = lambda n: ctx.enter_context(nc.semaphore(n))
        w_tok = sb("w_tok", [P, FLATC, D], F32)
        w_tok_hi = sb("w_tok_hi", [P, FLATC, D], BF16)
        w_tok_lo = sb("w_tok_lo", [P, FLATC, D], BF16)
        w_all = sb("w_all", [P, KC, QKV], F32)
        w_raw = sb("w_raw", [P, KC, 2 * D], F32)
        w_out = sb("w_out", [P, KC, D], F32)
        w_gate = sb("w_gate", [P, KC, E], F32)
        gated = sb("gated", [P, KC, 2 * D], F32)
        ln_w = sb("ln_w", [P, KC], F32)
        ln_b = sb("ln_b", [P, KC], F32)
        ln_b_cols = sb("ln_b_cols", [P, KC, P], F32)
        g_row = sb("g_row", [P, 2, HD], F32)
        pat = sb("pat", [P, 2, FLATC, CHUNK], F32)
        pat_hi = sb("pat_hi", [P, 2, FLATC, CHUNK], BF16)
        pat_lo = sb("pat_lo", [P, 2, FLATC, CHUNK], BF16)
        tok = sb("tok", [P, 2, D], F32)
        bias = sb("bias", [P, (E + 1) * D // P], F32)
        bias_rest = sb("bias_rest", [P, (E + 1) * D // P], F32)
        bias_parts = sb("bias_parts", [P, 3, (E + 1) * D // P], BF16)
        zeros = sb("zeros", [P, E * ROWS * 2 // P], F32)
        ps_tok = [ctx.enter_context(nc.psum_tensor(f"ps_tok{i}", [P, 512], F32)) for i in range(2)]
        ps_bias = ctx.enter_context(nc.psum_tensor("ps_bias", [P, 512], F32))

        consts_in = sem("consts_in")
        w_tok_in = sem("w_tok_in")
        w_in = sem("w_in")
        pat_in = [sem(f"pat_in{i}") for i in range(2)]
        dve_steps = sem("dve_steps1")
        w_tok_ready = sem("w_tok_ready")
        hi_ready = sem("pat_hi_ready")
        lo_ready = sem("pat_lo_ready")
        group_done = sem("group_done")
        group_copied = sem("group_copied")
        tok_out = [sem(f"tok_out{i}") for i in range(2)]
        ln_b_ready = sem("ln_b_ready")
        bias_done = sem("bias_done")
        bias_split = sem("bias_split")
        bias_out = sem("bias_out")
        zero_ready = sem("zero_ready")
        bo_in = sem("bo_in")
        rows_zero = sem("rows_zero")
        block = ctx.enter_context(nc.Block())
        LOADS = B * N_PATCH // CHUNK

        @block.sync
        def _(sp):
            sp.dma_start(w_tok[:], dram["w_tok"]).then_inc(w_tok_in, 16)
            for c in range(2):
                sp.dma_start(pat[:, c], dram["patches"][:, :, CHUNK * c:CHUNK * (c + 1)]).then_inc(pat_in[c], 16)
            for dst, src in ((m.consts[:], dram["consts"]), (m.b1[:], dram["b1"])):
                sp.dma_start(dst, src).then_inc(consts_in, 16)
            for dst, src in ((w_raw[:], dram["w_qk"]), (w_all[:, :, 2 * D:3 * D], dram["w_v"]), (w_out[:], dram["w_o"]),
                             (bias[:], dram["biases"]), (w_gate[:], dram["w_g"]), (ln_w[:], dram["ln_w"]), (ln_b[:], dram["ln_b"]),
                             (g_row[:, 0, :], dram["gq"].partition_broadcast(P)),
                             (g_row[:, 1, :], dram["gk"].partition_broadcast(P))):
                sp.dma_start(dst, src).then_inc(w_in, 16)
            for i in range(3):
                if i == 0:
                    sp.wait_ge(bias_split, 1)
                sp.dma_start(dram["bias_parts"][i].rearrange("(p c) -> p c", p=P), bias_parts[:, i]).then_inc(bias_out, 16)
            for c in range(2, LOADS):
                sp.wait_ge(hi_ready, c - 1)
                sp.wait_ge(lo_ready, c - 1)
                sp.dma_start(pat[:, c % 2], dram["patches"][:, :, CHUNK * c:CHUNK * (c + 1)]).then_inc(pat_in[c % 2], 16)
            sp.wait_ge(bias_out, 48)
            sp.wait_ge(zero_ready, 2)
            sp.dma_start(m.bo_rows[0:3], dram["bias_parts"][:, 0:D]).then_inc(bo_in, 16)
            sp.dma_start(dram["table"].rearrange("(p r) c -> p (r c)", p=P), zeros[:]).then_inc(rows_zero, 16)
            sp.dma_start(dram["out"][TOKENS:TOKENS + P, :], zeros[:, 0:D]).then_inc(rows_zero, 16)
            sp.wait_ge(bo_in, 16)
            sp.wait_ge(rows_zero, 32)
            sp.wait_ge(tok_out[0], 16 * LOADS * PER // 2)
            sp.wait_ge(tok_out[1], 16 * LOADS * PER // 2)

        @block.gpsimd
        def _(pool):
            nc.gpsimd.memset(m.bo_rows[:], 0.0).then_inc(zero_ready, 1)
            nc.gpsimd.memset(zeros[:], 0.0).then_inc(zero_ready, 1)

        def copy_groups(act, c):
            for j in range(PER):
                n = PER * c + j
                act.wait_ge(group_done, n + 1)
                if n >= 2:
                    act.wait_ge(tok_out[n % 2], 16 * (n // 2))
                nc.scalar.copy(tok[0:GROUP, n % 2], ps_tok[n % 2][0:GROUP, 0:D]).then_inc(group_copied, 1)
                act.wait_ge(group_copied, n + 1)
                act.dma_start(dram["tok"][GROUP * n:GROUP * (n + 1), :], tok[0:GROUP, n % 2]).then_inc(tok_out[n % 2], 16)

        @block.scalar
        def _(act):
            for c in range(LOADS):
                act.wait_ge(pat_in[c % 2], 16 * (c // 2 + 1))
                if c >= 2:
                    act.wait_ge(group_done, PER * (c - 1))
                nc.scalar.copy(pat_hi[:, c % 2], pat[:, c % 2]).then_inc(hi_ready, 1)
                if c >= 1:
                    copy_groups(act, c - 1)
            copy_groups(act, LOADS - 1)

        @block.tensor
        def _(pe):
            pe.wait_ge(w_tok_ready, 1)
            for c in range(LOADS):
                pe.wait_ge(hi_ready, c + 1)
                pe.wait_ge(lo_ready, c + 1)
                for j in range(PER):
                    n = PER * c + j
                    if n >= 2:
                        pe.wait_ge(group_copied, n - 1)
                    cols = slice(GROUP * j, GROUP * (j + 1))
                    parts = [(x, w, f) for f in range(FLATC) for x, w in ((pat_hi, w_tok_hi), (pat_lo, w_tok_hi), (pat_hi, w_tok_lo))]
                    for i, (x, w, f) in enumerate(parts):
                        mm = nc.tensor.matmul(ps_tok[n % 2][0:GROUP, 0:D], x[:, c % 2, f, cols], w[:, f, :],
                                              start=i == 0, stop=i == len(parts) - 1)
                    mm.then_inc(group_done, 1)
                if c == 0:
                    pe.wait_ge(ln_b_ready, 1)
                    for kc in range(KC):
                        mm = nc.tensor.matmul(ps_bias[:, :], ln_b_cols[:, kc, :], w_raw[:, kc, :], start=kc == 0, stop=kc == KC - 1)
                    mm.then_inc(bias_done, 1)

        @block.vector
        def _(dve):
            st = Steps(dve, dve_steps)
            dve.wait_ge(w_tok_in, 16)
            st.do(nc.vector.tensor_copy(w_tok_hi[:], w_tok[:]))
            nc.vector.tensor_tensor(w_tok_lo[:], w_tok[:], w_tok_hi[:], ALU.subtract).then_inc(w_tok_ready, 1)
            for c in range(LOADS):
                dve.wait_ge(hi_ready, c + 1)
                if c >= 2:
                    dve.wait_ge(group_done, PER * (c - 1))
                nc.vector.tensor_tensor(pat_lo[:, c % 2], pat[:, c % 2], pat_hi[:, c % 2], ALU.subtract).then_inc(lo_ready, 1)
                if c == 0:
                    dve.wait_ge(w_in, 16 * 9)
                    dve.wait_ge(consts_in, 16 * 2)
                    for i in range(3):
                        rest = bias if i == 0 else bias_rest
                        ins = nc.vector.tensor_copy(bias_parts[:, i], rest[:])
                        if i < 2:
                            st.do(ins)
                            st.do(nc.vector.tensor_tensor(bias_rest[:], rest[:], bias_parts[:, i], ALU.subtract))
                    ins.then_inc(bias_split, 1)
                    for kc in range(KC):
                        st.mark(nc.vector.tensor_scalar(w_all[:, kc, 0:2 * D], w_raw[:, kc, :], ln_w[:, kc:kc + 1], None, ALU.mult))
                    nc.vector.tensor_copy(ln_b_cols[:], ln_b[:].unsqueeze(2).to_broadcast([P, KC, P])).then_inc(ln_b_ready, 1)
                    st.mark(nc.vector.tensor_copy(m.ident[:], m.ident_f))
                    st.mark(nc.vector.tensor_copy(m.tri[:], m.tri_f))
                    st.mark(nc.vector.tensor_copy(m.token_id[:], m.first_tokens))
                    st.mark(nc.vector.tensor_copy(m.w_out_hi[:], w_out[:]))
                    st.mark(nc.vector.tensor_copy(m.w_gate_hi[:], w_gate[:]))
                    st.mark(nc.vector.memset(m.ones[:], 1.0))
                    st.settle()
                    st.mark(nc.vector.tensor_tensor(m.w_out_lo[:], w_out[:], m.w_out_hi[:], ALU.subtract))
                    st.mark(nc.vector.tensor_tensor(m.w_gate_lo[:], w_gate[:], m.w_gate_hi[:], ALU.subtract))
                    for kc in range(KC):
                        for i in range(2):
                            st.mark(nc.vector.tensor_tensor(
                                gated[:, kc, i * D:(i + 1) * D].rearrange("p (h d) -> p h d", d=HD),
                                w_all[:, kc, i * D:(i + 1) * D].rearrange("p (h d) -> p h d", d=HD),
                                g_row[:, i, :].unsqueeze(1).to_broadcast([P, HEADS, HD]), ALU.mult))
                    st.settle()
                    for kc in range(KC):
                        st.mark(nc.vector.tensor_reduce(w_all[:, kc, 3 * D:QKV], gated[:, kc, :].rearrange("p (h d) -> p h d", d=HD), AX.X, ALU.add))
                    st.settle()
                    st.do(nc.vector.tensor_copy(m.w_hi[:], w_all[:]))
                    st.mark(nc.vector.tensor_tensor(m.w_lo[:], w_all[:], m.w_hi[:], ALU.subtract))
            dve.wait_ge(bias_done, 1)
            st.do(nc.vector.tensor_copy(m.bias_qk[:], ps_bias[:, :]))
            for i in range(2):
                st.mark(nc.vector.tensor_tensor(
                    gated[:, 0, i * D:(i + 1) * D].rearrange("p (h d) -> p h d", d=HD),
                    m.bias_qk[:, i * D:(i + 1) * D].rearrange("p (h d) -> p h d", d=HD),
                    g_row[:, i, :].unsqueeze(1).to_broadcast([P, HEADS, HD]), ALU.mult))
            st.settle()
            st.mark(nc.vector.tensor_reduce(m.bias_gate[:], gated[:, 0, :].rearrange("p (h d) -> p h d", d=HD), AX.X, ALU.add))
            st.mark(nc.vector.memset(m.placed[:], 0.0))
            st.settle()


def fusion_attention(nc, m, dram):
    PROJ, ATT, OUT, ROUTE, PLACE = 1, 2, 3, 4, 8
    TOTAL = SLOTS + PLACE
    RING = GROUP
    ROUNDS = (SLOTS - 1 - PLACE) // RING
    with ExitStack() as ctx:
        sb = lambda n, s, d: ctx.enter_context(nc.sbuf_tensor(n, s, d))
        sem = lambda n: ctx.enter_context(nc.semaphore(n))
        pb = lambda n: ctx.enter_context(nc.psum_tensor(n, [P, 512], F32))
        h = sb("h", [P, RING, PAIR, D], F32)
        stats = sb("stats", [P, 2, PAIR, 6], F32)
        mv = sb("mv", [P, 2, PAIR, 2], F32)
        squares = sb("squares", [P, NCOLS], F32)
        inv = sb("inv", [P, 2, NCOLS], F32)
        inv_t = sb("inv_t", [P, NCOLS], F32)
        x12 = sb("x12", [P, 2, PAIR, D], F32)
        x1, x2, qk_sq = x12[:, 0], x12[:, 1], x12[:].rearrange("p i b d -> p (i b d)").rearrange("p (b c) -> p b c", b=PAIR)
        x1s = sb("x1s", [P, PAIR, 2, D], BF16)
        x1T = sb("x1T", [P, PAIR, 2, KC, N], BF16)
        qk = sb("qk", [P, PAIR, 2 * D], F32)
        qks = sb("qks", [P, PAIR, 2 * HEADS, 4, HD], BF16)
        qT = sb("qT", [P, PAIR, HALF, N], BF16)
        kT = sb("kT", [P, PAIR, HALF, N], BF16)
        sig = sb("sig", [P, 2, 2, HALF // 2, N], F32)
        vg = sb("vg", [P, PAIR, D + 2 * HEADS], F32)
        gate = sb("gate", [P, PAIR, 2 * HEADS], F32)
        gate_q = sb("gate_q", [P, PAIR, HEADS, HD], F32)
        v_pad = sb("v_pad", [P, PAIR, HEADS, 2 * HD], F32)
        cT = sb("cT", [P, KC, N], F32)
        cTs = sb("cTs", [P, PAIR, 2, KC, N], BF16)
        h2 = sb("h2", [P, PAIR, D], F32)
        x2s = sb("x2s", [P, PAIR, 2, D], BF16)
        x2T = sb("x2T", [P, PAIR, 2, KC, N], BF16)
        w_stage = sb("w_stage", [P, WCH], F32)
        logits = sb("logits", [P, GB, E], F32)
        mask1 = sb("mask1", [P, GB, E], F32)
        mask2 = sb("mask2", [P, GB, E], F32)
        ex = sb("ex", [P, GB, E], F32)
        sg = sb("sg", [P, 2, GB, E], F32)
        top = sb("top", [P, GB, 8], F32)
        masks = sb("masks", [P, GB, 2, E], BF16)
        places = sb("places", [P, GB, 2, E], F32)
        entry = sb("entry", [P, GB, 2, 2], F32)
        slot_f = sb("slot_f", [P, GB, 2], F32)
        slot_i = sb("slot_i", [P, GB, 2], U32)
        sums = sb("sums", [P, 2 * E], F32)
        sig_bias = sb("sig_bias", [P, 1], F32)
        bT, bQK0, bQK1, bV, bKT, bS0, bS1, bC = [pb(n) for n in ("bT", "bQK0", "bQK1", "bV", "bKT", "bS0", "bS1", "bC")]
        bQK, bS = [bQK0, bQK1], [bS0, bS1]
        xT_ps = bT[:, :].bitcast(BF16)[:, 0:PAIR * 2 * KC * N].rearrange("p (b s k n) -> p b s k n", b=PAIR, s=2, k=KC)
        kt_ps = bKT[:, :].bitcast(BF16)[:, 0:HALF * N].rearrange("p (j n) -> p j n", j=HALF)
        lg_ps = bT[:, 4 * N:4 * N + PAIR * E]
        W = 2 * E
        rank_ps, count_ps = bV[:, 0:GB * W], bV[:, GB * W:(GB + 1) * W]

        names = """x1_ready x1_hi x1_lo x1T_done x1T_ready qk_done qk_ready v_done v_copied sq_ready inv_ready
            qn_ready qk_hi qk_lo qT_done qT_ready kT_done kT_ready score_done sig_ready gate_ready gate_q_ready vgate_ready
            col_done cg_ready c_ready wo_done h2_ready out_stored x2_ready x2_hi x2_lo xln_stored x2T_done x2T_ready lg_done
            lg_read masks_ready pos_done pos_read entry_ready scattered w_loaded w_hi_ready w_lo_ready dve_steps2
            pad_zero bias_set ex_ready sg_ready""".split()
        q = {n: sem(n) for n in names}
        h_loaded = [sem(f"h_loaded{i}") for i in range(RING)]
        block = ctx.enter_context(nc.Block())
        late = lambda x, n: not isinstance(x, int) or x >= n

        def run(eng, steps, slot):
            slots(eng, steps, slot, PLACE, RING, ROUNDS, TOTAL)

        def tok_of(s):
            v = dram["tok"].rearrange("(g b n) d -> g n b d", b=PAIR, n=N_PATCH)
            return v[bass.ds(s, 1)].rearrange("o n b d -> (o n) b d")

        def txt_of(s):
            v = dram["txt"].rearrange("(g b) n d -> g n b d", b=PAIR)
            return v[bass.ds(s, 1)].rearrange("o n b d -> (o n) b d")

        def rows_of(t, s):
            v = t[0:TOKENS, :].rearrange("(g b n) d -> g n b d", b=PAIR, n=N)
            return v[bass.ds(s, 1)].rearrange("o n b d -> (o n) b d")

        @block.sync
        def _(sp):
            def load_h(g, k):
                sp.dma_start(h[0:N_PATCH, k], tok_of(g)).then_inc(h_loaded[k], 16)
                sp.dma_start(h[N_PATCH:N, k], txt_of(g)).then_inc(h_loaded[k], 16)

            load_h(0, 0)

            def slot(s, k, ok):
                o = s - OUT
                if ok(0, SLOTS):
                    if late(s, 1):
                        sp.wait_ge(q["w_hi_ready"], s)
                        sp.wait_ge(q["w_lo_ready"], s)
                    sp.dma_start(w_stage[:], dram["w_ffn"][bass.ds(s, 1)].rearrange("o p c -> p (o c)")).then_inc(q["w_loaded"], 16)
                if ok(OUT, SLOTS):
                    sp.wait_ge(q["h2_ready"], o + 1)
                    sp.dma_start(rows_of(dram["out"], o), h2[0:N]).then_inc(q["out_stored"], 16)
                if ok(-1, SLOTS):
                    load_h(s + 1, (k + 1) % RING)
                if ok(OUT, SLOTS):
                    sp.wait_ge(q["x2_lo"], o + 1)
                    sp.wait_ge(q["x2_hi"], o + 1)
                    sp.dma_start(rows_of(dram["xln"], o), x2s[0:N].rearrange("n b s d -> n b (s d)")).then_inc(q["xln_stored"], 16)

            run(sp, None, slot)
            sp.wait_ge(q["out_stored"], 16 * SLOTS)
            sp.wait_ge(q["xln_stored"], 16 * SLOTS)

        @block.tensor
        def _(pe):
            def transposes(src, done):
                for b in range(PAIR):
                    for part in range(2):
                        for kc in range(KC):
                            mm = nc.tensor.transpose(xT_ps[:, b, part, kc, :], src[0:N, b, part, kc * P:(kc + 1) * P], m.ident[0:N, 0:N])
                mm.then_inc(done, 1)

            def product(out, xT, b, hi, lo, cols, first=True):
                parts = [(x, w, kc) for kc in range(KC) for x, w in ((0, hi), (1, hi), (0, lo))]
                for i, (x, w, kc) in enumerate(parts):
                    mm = nc.tensor.matmul(out, xT[:, b, x, kc, :], w[:, kc, cols], start=first and i == 0, stop=i == len(parts) - 1,
                                          skip_group_check=not first)
                return mm

            def ranks():
                mk = masks[0:N].rearrange("n b c e -> n (b c e)")
                add = lambda out, lhs, rhs, first, last: nc.tensor.matmul(out, lhs, rhs, start=first, stop=last, skip_group_check=True)
                add(rank_ps, m.tri[0:N, :], mk, True, False)
                for back in range(1, GB):
                    add(rank_ps[:, back * W:], m.ones[0:N, :], mk[:, 0:(GB - back) * W], False, back == GB - 1)
                for b in range(GB):
                    mm = add(count_ps, m.ones[0:N, :], mk[:, b * W:(b + 1) * W], b == 0, b == GB - 1)
                mm.then_inc(q["pos_done"], GROUP)

            def slot(s, k, ok):
                p, a, o, r = s - PROJ, s - ATT, s - OUT, s - ROUTE
                has_p, has_a, has_o, has_r = ok(PROJ, SLOTS), ok(ATT, SLOTS), ok(OUT, SLOTS), ok(ROUTE, SLOTS)

                def turn(b, which, done):
                    n = 2 * a + b
                    if which == 0:
                        if b == 0:
                            pe.wait_ge(q["qk_hi"], a + 1)
                            pe.wait_ge(q["qk_lo"], a + 1)
                        if late(n, 1):
                            pe.wait_ge(q["kT_ready"], n)
                    else:
                        pe.wait_ge(q["qT_ready"], n + 1)
                    for j in range(HALF):
                        mm = nc.tensor.transpose(kt_ps[:, j, :], qks[0:N, b, which * HEADS + 2 * j:which * HEADS + 2 * j + 2].rearrange("n h c d -> n (h c d)"),
                                                 m.ident[0:N, 0:N])
                    mm.then_inc(done, 1)

                def scores(b, half):
                    n = 8 * a + 4 * b + 2 * half
                    if half == 0:
                        pe.wait_ge(q["kT_ready"], 2 * a + b + 1)
                    for u in range(2):
                        if late(n + u, 2):
                            pe.wait_ge(q["sig_ready"], n + u - 1)
                    for j in range(HALF // 2):
                        for u in range(2):
                            rows = slice(64 * u, 64 * u + 64)
                            mm = nc.tensor.matmul(bS[u][0:N, j * N:(j + 1) * N], kT[rows, b, half * 4 + j, :], qT[rows, b, half * 4 + j, :],
                                                  start=True, stop=True)
                            if j == HALF // 2 - 1:
                                mm.then_inc(q["score_done"], 1)

                def collapse(b):
                    n = 2 * a + b
                    if b == 0:
                        pe.wait_ge(q["gate_q_ready"], a + 1)
                    if late(n, 1):
                        pe.wait_ge(q["c_ready"], n)
                    for kc in range(KC):
                        mm = nc.tensor.matmul(bC[:, (2 + kc) * N:(3 + kc) * N], gate_q[0:N, b].rearrange("n h d -> n (h d)")[:, kc * P:(kc + 1) * P],
                                              m.ident_f[0:N, 0:N], start=True, stop=True, skip_group_check=True)
                    mm.then_inc(q["col_done"], 1)
                    if b == 0:
                        pe.wait_ge(q["vgate_ready"], a + 1)
                    for half in range(2):
                        pe.wait_ge(q["sig_ready"], 8 * a + 4 * b + 2 * half + 2)
                        for j in range(4):
                            for u in range(2):
                                mm = nc.tensor.matmul(bC[32 * j:32 * j + 32, half * N:(half + 1) * N], v_pad[0:N, b, 2 * (4 * half + j) + u, :],
                                                      sig[0:N, half, u, j, :], start=u == 0, stop=u == 1, skip_group_check=True)
                        mm.then_inc(q["col_done"], 1)

                def project_qk(b):
                    if b == 0:
                        pe.wait_ge(q["x1T_ready"], p + 1)
                    if late(p, 1):
                        pe.wait_ge(q["qk_ready"], 2 * p + b - 1)
                    product(bQK[b][0:N, :], x1T, b, m.w_hi, m.w_lo, slice(0, 2 * D)).then_inc(q["qk_done"], 1)

                def project_v(b):
                    n = 2 * p + b
                    if late(n, 1):
                        pe.wait_ge(q["v_copied"], n)
                    if b == 0 and has_o:
                        pe.wait_ge(q["h2_ready"], o + 1)
                    product(bV[0:N, 0:D + 2 * HEADS], x1T, b, m.w_hi, m.w_lo, slice(2 * D, QKV)).then_inc(q["v_done"], 1)

                if has_p:
                    pe.wait_ge(q["x1_hi"], p + 1)
                    pe.wait_ge(q["x1_lo"], p + 1)
                    if ok(ROUTE + 1, SLOTS):
                        pe.wait_ge(q["lg_read"], r)
                    transposes(x1s, q["x1T_done"])
                if has_a:
                    turn(0, 0, q["qT_done"])
                if has_o:
                    pe.wait_ge(q["v_copied"], 2 * p if has_p else 2 * SLOTS)
                    if late(o, 1):
                        pe.wait_ge(q["h2_ready"], o)
                    if k == 1 and ok(PLACE + 1, SLOTS):
                        pe.wait_ge(q["pos_read"], s - 1 - ROUTE)
                    nc.tensor.matmul(bV[0:N, :], m.ones[:, 0:N], m.bo_rows[:].unsqueeze(1).to_broadcast([P, PAIR, D]), start=True, stop=False,
                                     skip_group_check=True)
                    pe.wait_ge(q["c_ready"], 2 * o + 2)
                    for b in range(PAIR):
                        mm = product(bV[0:N, b * D:(b + 1) * D], cTs, b, m.w_out_hi, m.w_out_lo, slice(0, D), first=False)
                    mm.then_inc(q["wo_done"], 1)
                if has_p:
                    project_qk(0)
                if has_r:
                    pe.wait_ge(q["x2_hi"], r + 1)
                    pe.wait_ge(q["x2_lo"], r + 1)
                    if has_p:
                        pe.wait_ge(q["x1T_ready"], p + 1)
                    elif ok(ROUTE + 1, SLOTS):
                        pe.wait_ge(q["lg_read"], r)
                    transposes(x2s, q["x2T_done"])
                if has_a:
                    turn(0, 1, q["kT_done"])
                if has_p:
                    project_qk(1)
                if has_a:
                    scores(0, 0)
                if has_p:
                    project_v(0)
                if has_a:
                    scores(0, 1)
                    turn(1, 0, q["qT_done"])
                if has_r:
                    pe.wait_ge(q["x2T_ready"], r + 1)
                    for b in range(PAIR):
                        mm = product(lg_ps[0:N, b * E:(b + 1) * E], x2T, b, m.w_gate_hi, m.w_gate_lo, slice(0, E))
                    mm.then_inc(q["lg_done"], 1)
                if has_p:
                    project_v(1)
                if has_a:
                    turn(1, 1, q["kT_done"])
                    collapse(0)
                    scores(1, 0)
                if k == 0 and ok(PLACE, SLOTS):
                    pe.wait_ge(q["masks_ready"], s - ROUTE)
                    pe.wait_ge(q["v_copied"], 2 * p + 2 if has_p else 2 * SLOTS)
                    if has_o and not has_p:
                        pe.wait_ge(q["h2_ready"], o + 1)
                    ranks()
                if has_a:
                    scores(1, 1)
                    collapse(1)

            run(pe, None, slot)

        @block.scalar
        def _(act):
            def slot(s, k, ok):
                p, a, o = s - PROJ, s - ATT, s - OUT
                has_p, has_a, has_o = ok(PROJ, SLOTS), ok(ATT, SLOTS), ok(OUT, SLOTS)

                def keep_qT(b):
                    n = 2 * a + b
                    act.wait_ge(q["qT_done"], n + 1)
                    if late(n, 2):
                        act.wait_ge(q["score_done"], 4 * n - 4)
                    nc.scalar.copy(qT[:, b], kt_ps).then_inc(q["qT_ready"], 1)

                def keep_v(b):
                    n = 2 * p + b
                    act.wait_ge(q["v_done"], n + 1)
                    if late(p, 1) and b == 0:
                        act.wait_ge(q["vgate_ready"], p)
                    nc.scalar.copy(vg[0:N, b], bV[0:N, 0:D + 2 * HEADS]).then_inc(q["v_copied"], 1)

                def resonance(b, half):
                    for u in range(2):
                        n = 8 * a + 4 * b + 2 * half + u
                        act.wait_ge(q["score_done"], n + 1)
                        if late(2 * a + b, 1):
                            act.wait_ge(q["col_done"], 3 * (2 * a + b - 1) + half + 2)
                        nc.scalar.activation(sig[0:N, half, u], bS[u][0:N, 0:4 * N].rearrange("n (j t) -> n j t", j=4), ACT.Sigmoid,
                                             bias=sig_bias[0:N, :], scale=SHARP).then_inc(q["sig_ready"], 1)

                def keep_gates(b):
                    n = 2 * a + b
                    act.wait_ge(q["col_done"], 3 * n + 3)
                    if late(n, 1):
                        act.wait_ge(q["c_ready"], n)
                    nc.scalar.copy(cT[:], bC[:, 2 * N:4 * N].rearrange("p (k n) -> p k n", n=N)).then_inc(q["cg_ready"], 1)

                def squares_of(b):
                    act.wait_ge(q["qk_ready"], 2 * p + b + 1)
                    if b == 0:
                        if late(p, 1):
                            act.wait_ge(q["inv_ready"], s)
                        act.wait_ge(q["x1_lo"], p + 1)
                        act.wait_ge(q["x1_hi"], p + 1)
                    elif ok(OUT + 1, SLOTS):
                        act.wait_ge(q["x2_lo"], o)
                        act.wait_ge(q["x2_hi"], o)
                    nc.scalar.activation(qk_sq[0:N, b], qk[0:N, b], ACT.Square).then_inc(q["sq_ready"], 1)

                if has_a:
                    keep_qT(0)
                if has_p:
                    squares_of(0)
                    squares_of(1)
                if has_a:
                    resonance(0, 0)
                if has_p:
                    keep_v(0)
                if has_a:
                    resonance(0, 1)
                    keep_qT(1)
                if has_p:
                    keep_v(1)
                if has_a:
                    keep_gates(0)
                if k == 0 and ok(PLACE, SLOTS):
                    act.wait_ge(q["ex_ready"], s - ROUTE)
                    nc.scalar.activation(sg[0:N, 0], ex[0:N], ACT.Sigmoid)
                    nc.scalar.activation(sg[0:N, 1], ex[0:N], ACT.Sigmoid, scale=-1.0).then_inc(q["sg_ready"], GROUP)
                if has_a:
                    resonance(1, 0)
                if ok(0, SLOTS):
                    act.wait_ge(q["x1_ready"], s + 1)
                    if late(s, 1):
                        act.wait_ge(q["x1T_done"], s)
                    nc.scalar.copy(x1s[0:N, :, 0, :], x1[0:N]).then_inc(q["x1_hi"], 1)
                if has_a:
                    resonance(1, 1)
                if has_p:
                    act.wait_ge(q["qn_ready"], p + 1)
                    if late(p, 1):
                        act.wait_ge(q["kT_done"], 2 * p)
                    for b in range(PAIR):
                        for i, step in enumerate((2, 1)):
                            dst = qks[0:N, b, i * HEADS:(i + 1) * HEADS, 0:step + 1:step, :]
                            src = qk[0:N, b, i * D:(i + 1) * D].rearrange("n (h d) -> n h d", d=HD).unsqueeze(2).to_broadcast([N, HEADS, 2, HD])
                            ins = nc.scalar.copy(dst, src)
                    ins.then_inc(q["qk_hi"], 1)
                if has_o:
                    act.wait_ge(q["x2_ready"], o + 1)
                    if late(o, 1):
                        act.wait_ge(q["x2T_done"], o)
                        act.wait_ge(q["xln_stored"], 16 * o)
                    nc.scalar.copy(x2s[0:N, :, 0, :], x2[0:N]).then_inc(q["x2_hi"], 1)
                if has_a:
                    keep_gates(1)
                if ok(0, SLOTS):
                    act.wait_ge(q["w_loaded"], 16 * (s + 1))
                    nc.scalar.copy(m.w_ffn_hi[:, bass.ds(s, 1)].rearrange("p o c -> p (o c)"), w_stage[:]).then_inc(q["w_hi_ready"], 1)

            act.wait_ge(q["bias_set"], 1)
            run(act, None, slot)

        @block.gpsimd
        def _(pool):
            nc.gpsimd.memset(sig_bias[:], -THRESH * SHARP).then_inc(q["bias_set"], 1)
            nc.gpsimd.memset(v_pad[:], 0.0).then_inc(q["pad_zero"], 1)
            nc.gpsimd.memset(qks[:, :, :, 3, :], 0.0).then_inc(q["pad_zero"], 1)
            pool.wait_ge(q["pad_zero"], 2)

            def slot(s, k, ok):
                p, a, o, c = s - PROJ, s - ATT, s - OUT, s - PLACE
                if ok(ATT, SLOTS):
                    pool.wait_ge(q["gate_ready"], a + 1)
                    if late(a, 1):
                        pool.wait_ge(q["col_done"], 6 * a)
                    for b in range(PAIR):
                        for u in range(2):
                            ins = nc.gpsimd.tensor_tensor(
                                v_pad[0:N, b].rearrange("n (j u) c -> n j u c", u=2)[:, :, u, u * HD:(u + 1) * HD],
                                vg[0:N, b, 0:D].rearrange("n (j u d) -> n j u d", u=2, d=HD)[:, :, u, :],
                                gate[0:N, b, HEADS:].rearrange("n (j u) -> n j u", u=2)[:, :, u:u + 1].to_broadcast([N, HALF, HD]), ALU.mult)
                    ins.then_inc(q["vgate_ready"], 1)
                if ok(PROJ, SLOTS):
                    pool.wait_ge(q["inv_ready"], s + 1)
                    nc.gpsimd.tensor_tensor(qk[0:N].rearrange("n b (h d) -> n (b h) d", d=HD), qk[0:N].rearrange("n b (h d) -> n (b h) d", d=HD),
                                            inv[0:N, k % 2, NQK:NV2].unsqueeze(2).to_broadcast([N, PAIR * 2 * HEADS, HD]), ALU.mult).then_inc(q["qn_ready"], 1)
                if ok(0, SLOTS):
                    pool.wait_ge(q["x1_hi"], s + 1)
                    nc.gpsimd.tensor_tensor(x1s[0:N, :, 1, :], x1[0:N], x1s[0:N, :, 0, :], ALU.subtract).then_inc(q["x1_lo"], 1)
                if ok(PLACE, SLOTS):
                    first = (k - PLACE) % RING
                    wait_before_dma(pool, (q["pad_zero"], 2), (q["entry_ready"], c + (GROUP - first)))
                    for b in range(PAIR):
                        for i in range(2):
                            nc.gpsimd.indirect_dma_start(dram["table"], bass.IndirectOffsetOnAxis(ap=slot_i[0:N, PAIR * first + b, i:i + 1], axis=0),
                                                         entry[0:N, PAIR * first + b, i, :], None).then_inc(q["scattered"], 16)
                if ok(OUT, SLOTS):
                    pool.wait_ge(q["x2_hi"], o + 1)
                    nc.gpsimd.tensor_tensor(x2s[0:N, :, 1, :], x2[0:N], x2s[0:N, :, 0, :], ALU.subtract).then_inc(q["x2_lo"], 1)
                if ok(0, SLOTS):
                    pool.wait_ge(q["w_hi_ready"], s + 1)
                    nc.gpsimd.tensor_tensor(m.w_ffn_lo[:, bass.ds(s, 1)].rearrange("p o c -> p (o c)"), w_stage[:],
                                            m.w_ffn_hi[:, bass.ds(s, 1)].rearrange("p o c -> p (o c)"), ALU.subtract).then_inc(q["w_lo_ready"], 1)

            run(pool, None, slot)
            pool.wait_ge(q["scattered"], 16 * 4 * SLOTS)

        @block.vector
        def _(dve):
            st = Steps(dve, q["dve_steps2"], ATTENTION_STEPS)
            v = nc.vector
            st.mark(v.memset(squares[:], 1.0))
            st.mark(v.memset(inv[:], 1.0))
            st.settle()
            wide = lambda ap: ap.to_broadcast([N, GB, E])
            col = lambda i: top[0:N, :, i:i + 1]

            def choose(x, mask, best):
                iota = m.rev_e[0:N].unsqueeze(1).to_broadcast([N, GB, E])
                st.do(v.tensor_reduce(col(best), x, AX.X, ALU.max))
                st.do(v.tensor_tensor(mask, x, wide(col(best)), ALU.is_equal))
                st.do(v.tensor_tensor(mask, mask, iota, ALU.mult))
                st.do(v.tensor_reduce(col(2), mask, AX.X, ALU.max))
                st.do(v.tensor_tensor(mask, mask, wide(col(2)), ALU.is_equal))

            def route():
                L, M1, M2, X = logits[0:N], mask1[0:N], mask2[0:N], ex[0:N]
                choose(L, M1, 0)
                st.do(v.scalar_tensor_tensor(out=X, in0=M1, scalar=-3.0e38, in1=L, op0=ALU.mult, op1=ALU.add))
                choose(X, M2, 1)
                st.mark(v.tensor_copy(masks[0:N, :, 0, :], M1))
                v.tensor_copy(masks[0:N, :, 1, :], M2).then_inc(q["masks_ready"], GROUP)
                v.tensor_tensor(X, L, wide(col(0)), ALU.subtract).then_inc(q["ex_ready"], GROUP)

            def place(s):
                done = s - ROUTE
                both = lambda ap: ap.rearrange("p (c e) -> p c e", c=2).unsqueeze(1).to_broadcast([N, GB, 2, E])
                M2, EX = mask2[0:N], ex[0:N]
                dve.wait_ge(q["pos_done"], done)
                st.mark(v.tensor_copy(sums[:], count_ps))
                v.tensor_tensor(places[0:N].rearrange("n b c e -> n b (c e)"), rank_ps[0:N, :].rearrange("n (b w) -> n b w", w=W),
                                m.placed[0:N].unsqueeze(1).to_broadcast([N, GB, W]), ALU.add).then_inc(q["pos_read"], GROUP)
                dve.wait_ge(q["sg_ready"], done)
                st.mark(v.reciprocal(EX, sg[0:N, 1]))
                dve.wait_ge(q["pos_read"], done)
                st.settle()
                st.mark(v.tensor_tensor(m.placed[:], m.placed[:], sums[:], ALU.add))
                st.mark(v.tensor_tensor(places[0:N], places[0:N], both(m.sign[0:N]), ALU.mult))
                st.do(v.tensor_tensor(EX, EX, sg[0:N, 0], ALU.mult))
                st.mark(v.tensor_tensor(places[0:N], places[0:N], both(m.centre[0:N]), ALU.add))
                st.do(v.tensor_reduce(col(2), EX, AX.X, ALU.add))
                st.mark(v.tensor_tensor(EX, EX, M2, ALU.mult))
                st.do(v.tensor_tensor(places[0:N], places[0:N], masks[0:N], ALU.mult))
                if late(s, PLACE + GROUP):
                    dve.wait_ge(q["scattered"], 64 * (s - PLACE))
                st.mark(v.tensor_reduce(col(3), EX, AX.X, ALU.add))
                st.mark(v.reciprocal(col(2), col(2)))
                st.do(v.tensor_reduce(slot_f[0:N], places[0:N], AX.X, ALU.add))
                st.mark(v.tensor_copy(slot_i[0:N], slot_f[0:N]))
                st.mark(v.tensor_scalar(col(6), col(2), 1e-9, None, ALU.add))
                st.do(v.tensor_tensor(col(3), col(3), col(2), ALU.mult))
                st.mark(v.tensor_copy(entry[0:N, :, :, 0], m.token_id[0:N].unsqueeze(2).to_broadcast([N, GB, 2])))
                st.do(v.tensor_tensor(col(6), col(6), col(3), ALU.add))
                st.do(v.reciprocal(col(6), col(6)))
                st.mark(v.tensor_scalar(m.token_id[0:N], m.token_id[0:N], float(GB * N), None, ALU.add))
                v.tensor_tensor(entry[0:N, :, :, 1], top[0:N, :, 2:4], col(6).to_broadcast([N, GB, 2]), ALU.mult).then_inc(q["entry_ready"], GROUP)

            def slot(s, k, ok):
                p, a, o, r = s - PROJ, s - ATT, s - OUT, s - ROUTE
                has_p, has_a, has_o, has_r = ok(PROJ, SLOTS), ok(ATT, SLOTS), ok(OUT, SLOTS), ok(ROUTE, SLOTS)
                now, was = inv[0:N, k % 2], inv[0:N, (k + 1) % 2]

                def scaled_qk(b):
                    dve.wait_ge(q["qk_done"], 2 * p + b + 1)
                    if late(p, 1) and b == 0:
                        dve.wait_ge(q["qk_hi"], p)
                        dve.wait_ge(q["qk_lo"], p)
                    v.scalar_tensor_tensor(out=qk[0:N, b], in0=bQK[b][0:N, :], scalar=was[:, NR2 + b:NR2 + b + 1], in1=m.bias_qk[0:N],
                                           op0=ALU.mult, op1=ALU.add).then_inc(q["qk_ready"], 1)

                def keep_kT(b):
                    n = 2 * a + b
                    dve.wait_ge(q["kT_done"], n + 1)
                    if late(n, 2):
                        dve.wait_ge(q["score_done"], 4 * n - 4)
                    v.tensor_copy(kT[:, b], kt_ps).then_inc(q["kT_ready"], 1)

                def sum_squares(b):
                    dve.wait_ge(q["sq_ready"], 2 * p + b + 1)
                    at = NQK + b * 2 * HEADS
                    st.mark(v.tensor_reduce(squares[0:N, at:at + 2 * HEADS], qk_sq[0:N, b].rearrange("n (h d) -> n h d", d=HD), AX.X, ALU.add))

                def gate_and_split(b):
                    n = 2 * a + b
                    dve.wait_ge(q["cg_ready"], n + 1)
                    if b == 0 and late(a, 1):
                        dve.wait_ge(q["wo_done"], a)
                    st.do(v.tensor_tensor(cT[:], bC[:, 0:2 * N].rearrange("p (k n) -> p k n", n=N), cT[:], ALU.mult))
                    st.do(v.tensor_copy(cTs[:, b, 0], cT[:]))
                    v.tensor_tensor(cTs[:, b, 1], cT[:], cTs[:, b, 0], ALU.subtract).then_inc(q["c_ready"], 1)

                if has_p:
                    dve.wait_ge(q["x1T_done"], p + 1)
                    if late(p, 1):
                        dve.wait_ge(q["v_done"], 2 * p)
                    v.tensor_copy(x1T[:], xT_ps).then_inc(q["x1T_ready"], 1)
                if has_a:
                    dve.wait_ge(q["v_copied"], 2 * a + 2)
                    for b in range(PAIR):
                        st.mark(v.scalar_tensor_tensor(out=gate[0:N, b], in0=vg[0:N, b, D:], scalar=now[:, NR2 + b:NR2 + b + 1], in1=m.bias_gate[0:N],
                                                       op0=ALU.mult, op1=ALU.add))
                    st.settle()
                    v.tensor_tensor(gate[0:N], gate[0:N], was[:, NQK:NV2].rearrange("n (b h) -> n b h", b=PAIR), ALU.mult).then_inc(q["gate_ready"], 1)
                if ok(0, SLOTS):
                    dve.wait_ge(h_loaded[k], (s - k) * (32 // RING) + 32)
                    for b in range(PAIR):
                        st.mark(v.bn_stats(stats[0:N, 0, b], h[0:N, k, b]))
                if has_a:
                    dve.wait_ge(q["gate_ready"], a + 1)
                    v.tensor_copy(gate_q[0:N], gate[0:N, :, 0:HEADS].unsqueeze(3).to_broadcast([N, PAIR, HEADS, HD])).then_inc(q["gate_q_ready"], 1)
                if has_o:
                    dve.wait_ge(q["wo_done"], o + 1)
                    if late(o, 1):
                        dve.wait_ge(q["out_stored"], 16 * o)
                    v.tensor_tensor(h2[0:N], bV[0:N, :].rearrange("n (b d) -> n b d", b=PAIR), h[0:N, (k - OUT) % RING],
                                    ALU.add).then_inc(q["h2_ready"], 1)
                if has_p:
                    scaled_qk(0)
                if has_a:
                    keep_kT(0)
                if has_o:
                    dve.wait_ge(q["h2_ready"], o + 1)
                    for b in range(PAIR):
                        st.mark(v.bn_stats(stats[0:N, 1, b], h2[0:N, b]))
                if has_p:
                    scaled_qk(1)
                if has_r:
                    dve.wait_ge(q["x2T_done"], r + 1)
                    if late(r, 1):
                        dve.wait_ge(q["lg_done"], r)
                    v.tensor_copy(x2T[:], xT_ps).then_inc(q["x2T_ready"], 1)
                st.settle()
                if has_p:
                    sum_squares(0)
                if ok(0, SLOTS):
                    for b in range(PAIR):
                        st.mark(v.bn_aggr(mv[0:N, 0, b], stats[0:N, 0, b]))
                if has_o:
                    for b in range(PAIR):
                        st.mark(v.bn_aggr(mv[0:N, 1, b], stats[0:N, 1, b]))
                st.settle()
                if ok(0, SLOTS):
                    st.do(v.tensor_scalar(squares[0:N, NV1:NR2], mv[0:N, 0, :, 1], LN_EPS, None, ALU.add))
                    st.mark(v.reciprocal(squares[0:N, NR2:NCOLS], squares[0:N, NV1:NR2]))
                if has_o:
                    st.mark(v.tensor_scalar(squares[0:N, NV2:NV1], mv[0:N, 1, :, 1], LN_EPS, None, ALU.add))
                if has_p:
                    sum_squares(1)
                st.settle()
                if has_p:
                    st.mark(v.tensor_scalar(squares[0:N, NQK:NV2], squares[0:N, NQK:NV2], NORM_EPS * NORM_EPS, None, ALU.max))
                if ok(0, SLOTS):
                    st.do(v.tensor_tensor(squares[0:N, NR2:NCOLS], squares[0:N, NR2:NCOLS], mv[0:N, 0, :, 1], ALU.mult))
                    st.mark(v.tensor_scalar(squares[0:N, NR2:NCOLS], squares[0:N, NR2:NCOLS], LN_EPS, None, ALU.add))
                if ok(0, SLOTS) or has_p or has_o:
                    if late(s, 3):
                        dve.wait_ge(q["qn_ready"], s - 2)
                    st.settle()
                    inverse_sqrt(nc, st, q["inv_ready"], now, squares[0:N], inv_t[0:N])
                    dve.wait_ge(q["inv_ready"], s + 1)
                if ok(0, SLOTS):
                    if late(s, 1):
                        dve.wait_ge(q["x1_hi"], s)
                        dve.wait_ge(q["x1_lo"], s)
                    for b in range(PAIR):
                        ins = v.tensor_scalar(x1[0:N, b], h[0:N, k, b], mv[0:N, 0, b, 0:1], now[:, NV1 + b:NV1 + b + 1], ALU.subtract, ALU.mult)
                    ins.then_inc(q["x1_ready"], 1)
                if has_a:
                    keep_kT(1)
                if has_o:
                    if late(o, 1):
                        dve.wait_ge(q["x2_hi"], o)
                        dve.wait_ge(q["x2_lo"], o)
                    for b in range(PAIR):
                        ins = v.tensor_scalar(x2[0:N, b], h2[0:N, b], mv[0:N, 1, b, 0:1], now[:, NV2 + b:NV2 + b + 1], ALU.subtract, ALU.mult)
                    ins.then_inc(q["x2_ready"], 1)
                if has_r:
                    dve.wait_ge(q["lg_done"], r + 1)
                    at = slice(PAIR * k, PAIR * (k + 1))
                    v.tensor_copy(logits[0:N, at], lg_ps[0:N, :].rearrange("n (b e) -> n b e", e=E)).then_inc(q["lg_read"], 1)
                if has_a:
                    gate_and_split(0)
                if k == GROUP - 1 and has_r:
                    dve.wait_ge(q["lg_read"], r + 1)
                    route()
                if k == 0 and ok(PLACE, SLOTS):
                    place(s)
                if has_p:
                    dve.wait_ge(q["qk_hi"], p + 1)
                    for i in range(2):
                        ins = v.tensor_tensor(qks[0:N, :, i * HEADS:(i + 1) * HEADS, 1 + i, :],
                                              qk[0:N, :, i * D:(i + 1) * D].rearrange("n b (h d) -> n b h d", d=HD),
                                              qks[0:N, :, i * HEADS:(i + 1) * HEADS, 0, :], ALU.subtract)
                        if i == 0:
                            st.mark(ins)
                    ins.then_inc(q["qk_lo"], 1)
                if has_a:
                    gate_and_split(1)

            run(dve, st, slot)
            st.settle()


def plan_tiles(nc, m):
    with ExitStack() as ctx:
        sb = lambda n, s: ctx.enter_context(nc.sbuf_tensor(n, s, F32))
        first, second, count, tiles, begin, end, v_start, v_left = [sb(n, [P, E]) for n in (
            "first", "second", "count", "tiles", "begin", "end", "v_start", "v_left")]
        tiles_i = ctx.enter_context(nc.sbuf_tensor("tiles_i", [P, E], I32))
        before = sb("before", [P, E, E])
        own, other = sb("own", [P, TILES, E]), sb("other", [P, TILES, E])
        any_, expert, start, left, rows = [sb(n, [P, TILES]) for n in ("any", "expert", "start", "left", "rows")]
        dve_steps = ctx.enter_context(nc.semaphore("dve_steps3"))
        block = ctx.enter_context(nc.Block())

        @block.vector
        def _(dve):
            st = Steps(dve, dve_steps)
            v = nc.vector
            n1, n2 = m.placed[:, 0:E], m.placed[:, E:2 * E]
            st.do(v.tensor_scalar(first[:], n1, float(CAP), None, ALU.min))
            st.do(v.tensor_scalar(second[:], n1, -1.0, float(CAP), ALU.mult, ALU.add))
            st.do(v.tensor_tensor(second[:], second[:], n2, ALU.min))
            st.do(v.tensor_scalar(second[:], second[:], 0.0, None, ALU.max))
            st.do(v.tensor_tensor(count[:], first[:], second[:], ALU.add))
            st.do(v.tensor_scalar(tiles_i[:], count[:], float(TILE - 1), None, ALU.add))
            st.do(v.tensor_scalar(tiles_i[:], tiles_i[:], TILE.bit_length() - 1, None, ALU.arith_shift_right))
            st.do(v.tensor_copy(tiles[:], tiles_i[:]))
            st.do(v.tensor_tensor(before[:], m.below.rearrange("p (a b) -> p a b", a=E), tiles[:].unsqueeze(1).to_broadcast([P, E, E]), ALU.mult))
            st.do(v.tensor_reduce(begin[:], before[:], AX.X, ALU.add))
            st.do(v.tensor_tensor(end[:], begin[:], tiles[:], ALU.add))
            t_of = m.tile_no.unsqueeze(2).to_broadcast([P, TILES, E])
            over = lambda ap: ap.unsqueeze(1).to_broadcast([P, TILES, E])
            st.do(v.tensor_tensor(own[:], t_of, over(begin[:]), ALU.is_ge))
            st.do(v.tensor_tensor(other[:], t_of, over(end[:]), ALU.is_ge))
            st.do(v.tensor_tensor(own[:], own[:], other[:], ALU.subtract))
            st.do(v.scalar_tensor_tensor(out=v_start[:], in0=begin[:], scalar=float(-TILE), in1=m.centre_e, op0=ALU.mult, op1=ALU.add))
            st.do(v.tensor_tensor(v_start[:], v_start[:], first[:], ALU.subtract))
            st.do(v.scalar_tensor_tensor(out=v_left[:], in0=begin[:], scalar=float(TILE), in1=count[:], op0=ALU.mult, op1=ALU.add))
            st.do(v.tensor_reduce(any_[:], own[:], AX.X, ALU.add))
            for value, out in ((m.index_e, expert), (v_start[:], start), (v_left[:], left)):
                st.do(v.tensor_tensor(other[:], own[:], over(value), ALU.mult))
                st.do(v.tensor_reduce(out[:], other[:], AX.X, ALU.add))
            st.do(v.tensor_tensor(rows[:], m.tile_no, any_[:], ALU.mult))
            st.do(v.tensor_scalar(rows[:], rows[:], float(TILE), None, ALU.mult))
            st.do(v.tensor_tensor(start[:], start[:], rows[:], ALU.add))
            st.do(v.tensor_tensor(left[:], left[:], rows[:], ALU.subtract))
            for h in range(PARTS):
                st.do(v.tensor_tensor(m.valid[:, :, h], left[:], m.pos_p[:, h:h + 1].to_broadcast([P, TILES]), ALU.is_gt))
            st.do(v.tensor_copy(m.tile_info[:, 0, :], expert[:]))
            st.do(v.tensor_copy(m.tile_info[:, 1, :], start[:]))


def expert_tiles(nc, m, dram):
    UP, DOWN = 1, 2
    TOTAL = TILES + DOWN
    LOOP_FROM, UNROLL = 4, 2
    with ExitStack() as ctx:
        sb = lambda n, s, d: ctx.enter_context(nc.sbuf_tensor(n, s, d))
        sem = lambda n: ctx.enter_context(nc.semaphore(n))
        pb = lambda n: ctx.enter_context(nc.psum_tensor(n, [P, 512], F32))
        b2_rows = sb("b2_rows", [P, E, D], BF16)
        tab = sb("tab", [P, 2, PARTS, 2], F32)
        away = sb("away", [P, PARTS, 2], F32)
        kept = sb("kept", [P, 2, PARTS, 2], F32)
        from_id = sb("from_id", [P, 2, PARTS], U32)
        to_id = sb("to_id", [P, 2, PARTS], U32)
        weight = sb("weight", [P, 2, PARTS], F32)
        x = sb("x", [P, 2, PARTS, 2 * D], BF16)
        xT = sb("xT", [P, 2, 4, TILE], BF16)
        act_f = sb("act_f", [P, FC, TILE], F32)
        act_hi = sb("act_hi", [P, 2, FC, TILE], BF16)
        act_lo = sb("act_lo", [P, 2, FC, TILE], BF16)
        y = sb("y", [P, 2, PARTS, D], F32)
        bX = pb("bX")
        bH = [pb(f"bH{i}") for i in range(FC // 2)]
        bY = [pb(f"bY{i}") for i in range(2)]
        x_ps = bX[:, :].bitcast(BF16).rearrange("p (c n) -> p c n", c=4)
        names = """b2_in b2_zero ids_ready weight_ready gathered0 gathered1 turned turned_kept up_done gelu_ready act_ready
            down_done y_ready added dve_steps4 tab_in0 tab_in1""".split()
        q = {n: sem(n) for n in names}
        tab_in = [q["tab_in0"], q["tab_in1"]]
        gathered = [q["gathered0"], q["gathered1"]]
        block = ctx.enter_context(nc.Block())
        late = lambda v, n: not isinstance(v, int) or v >= n

        def run(eng, steps, slot):
            slots(eng, steps, slot, LOOP_FROM, UNROLL, (TILES - LOOP_FROM) // UNROLL, TOTAL)

        def info(eng, which, t, top):
            return eng.value_load(m.tile_info[0:1, which, bass.ds(t, 1)], min_val=0, max_val=top)

        def uses(s, k, each):
            return (s - k % 2) * (each // 2) + each

        @block.sync
        def _(sp):
            sp.wait_ge(q["b2_zero"], 1)
            sp.dma_start(b2_rows[0:3].rearrange("p e d -> p (e d)"), dram["bias_parts"][:, D:]).then_inc(q["b2_in"], 16)

            def slot(s, k, ok):
                if ok(0, TILES):
                    if late(s, 2):
                        sp.wait_ge(q["ids_ready"], s - 1)
                    start = info(sp, 1, s, E * ROWS - TILE)
                    sp.dma_start(tab[:, k % 2], dram["table"][bass.ds(start, TILE), :].rearrange("(h p) c -> p h c", p=P)).then_inc(tab_in[k % 2], 16)

            run(sp, None, slot)
            sp.wait_ge(q["added"], 16 * PARTS * TILES)

        @block.gpsimd
        def _(pool):
            nc.gpsimd.memset(b2_rows[:], 0.0).then_inc(q["b2_zero"], 1)

            def add(d, k, h):
                before = [(q["added"], 16 * (PARTS * d + h))] if h or late(d, 1) else []
                wait_before_dma(pool, (q["b2_zero"], 1), *([] if h else [(q["y_ready"], d + 1)]), *before)
                nc.gpsimd.indirect_dma_start(dram["out"], bass.IndirectOffsetOnAxis(ap=to_id[:, k % 2, h:h + 1], axis=0),
                                             y[:, k % 2, h], None, compute_op=ALU.add).then_inc(q["added"], 16)

            def slot(s, k, ok):
                d = s - DOWN
                if ok(0, TILES):
                    wait_before_dma(pool, (q["b2_zero"], 1), (q["ids_ready"], s + 1), *([(q["turned"], s - 1)] if late(s, 2) else []))
                    for h in range(PARTS):
                        nc.gpsimd.indirect_dma_start(x[:, k % 2, h], None, dram["xln"], bass.IndirectOffsetOnAxis(ap=from_id[:, k % 2, h:h + 1], axis=0)
                                                     ).then_inc(gathered[k % 2], 16)
                if ok(DOWN, TILES):
                    for h in range(PARTS):
                        add(d, k, h)

            run(pool, None, slot)

        @block.tensor
        def _(pe):
            pe.wait_ge(q["b2_in"], 16)

            def slot(s, k, ok):
                u, d = s - UP, s - DOWN
                if ok(DOWN, TILES):
                    e_down = info(pe, 0, d, E - 1)
                if ok(UP, TILES):
                    e_up = info(pe, 0, u, E - 1)
                    pe.wait_ge(gathered[(k - UP) % 2], uses(u, k - UP, 16 * PARTS))
                    if late(u, 1):
                        pe.wait_ge(q["turned_kept"], u)
                    for c in range(4):
                        for h in range(PARTS):
                            mm = nc.tensor.transpose(x_ps[:, c, h * P:(h + 1) * P], x[:, (k - UP) % 2, h, c * P:(c + 1) * P], m.ident[:])
                    mm.then_inc(q["turned"], 1)
                if ok(DOWN, TILES):
                    at = k % 2
                    if late(d, 2):
                        pe.wait_ge(q["y_ready"], d - 1)
                    for h in range(PARTS):
                        rows = slice(h * P, (h + 1) * P)
                        out = bY[at][:, h * D:(h + 1) * D]
                        nc.tensor.matmul(out, m.ones[:], b2_rows[:, bass.ds(e_down, 1), :].rearrange("p o d -> p (o d)"), start=True, stop=False)
                        for f in range(FC):
                            if h == 0 and f % 2 == 0:
                                pe.wait_ge(q["act_ready"], (FC // 2) * d + f // 2 + 1)
                            for a, w in ((act_hi, m.w_ffn_hi), (act_lo, m.w_ffn_hi), (act_hi, m.w_ffn_lo)):
                                rhs = w[:, bass.ds(2 * e_down + (2 * E + f // 4), 1), (f % 4) * D:(f % 4 + 1) * D].rearrange("p o d -> p (o d)")
                                mm = nc.tensor.matmul(out, a[:, at, f, rows], rhs, start=False, stop=f == FC - 1 and w is m.w_ffn_lo)
                    mm.then_inc(q["down_done"], 1)
                if ok(UP, TILES):
                    at = (k - UP) % 2
                    pe.wait_ge(q["turned_kept"], u + 1)
                    for b in range(FC // 2):
                        if late(u, 1):
                            pe.wait_ge(q["gelu_ready"], (FC // 2) * (u - 1) + b + 1)
                        for f in range(2):
                            parts = [(p, w, kc) for kc in range(KC) for p, w in ((0, m.w_ffn_hi), (1, m.w_ffn_hi), (0, m.w_ffn_lo))]
                            for i, (p, w, kc) in enumerate(parts):
                                lhs = w[:, bass.ds(2 * e_up + kc, 1), (2 * b + f) * P:(2 * b + f + 1) * P].rearrange("p o d -> p (o d)")
                                mm = nc.tensor.matmul(bH[b][:, f * TILE:(f + 1) * TILE], lhs, xT[:, at, 2 * p + kc, :],
                                                      start=i == 0, stop=i == len(parts) - 1)
                        mm.then_inc(q["up_done"], 1)

            run(pe, None, slot)

        @block.scalar
        def _(act):
            def slot(s, k, ok):
                u = s - UP
                if ok(UP, TILES):
                    at = (k - UP) % 2
                    e = info(act, 0, u, E - 1)
                    act.wait_ge(q["turned"], u + 1)
                    if late(u, 2):
                        act.wait_ge(q["up_done"], (FC // 2) * (u - 1))
                    nc.scalar.copy(xT[:, at], x_ps).then_inc(q["turned_kept"], 1)
                    for b in range(FC // 2):
                        act.wait_ge(q["up_done"], (FC // 2) * u + b + 1)
                        if late(u, 1):
                            act.wait_ge(q["act_ready"], (FC // 2) * (u - 1) + b + 1)
                        for f in range(2):
                            ins = nc.scalar.activation(act_f[:, 2 * b + f, :], bH[b][:, f * TILE:(f + 1) * TILE], ACT.Gelu,
                                                       bias=m.b1[:, bass.ds(e * FC + (2 * b + f), 1)])
                        ins.then_inc(q["gelu_ready"], 1)

            run(act, None, slot)

        @block.vector
        def _(dve):
            st = Steps(dve, q["dve_steps4"], FFN_STEPS)
            v = nc.vector

            def slot(s, k, ok):
                u, d = s - UP, s - DOWN
                if ok(DOWN, TILES):
                    at = k % 2
                    if late(d, 2):
                        dve.wait_ge(q["added"], 16 * PARTS * (d - 1))
                    st.mark(v.tensor_tensor(to_id[:, at], kept[:, at, :, 0], m.away.rearrange("p (h c) -> p h c", c=2)[:, :, 0], ALU.add))
                    st.do(v.tensor_copy(weight[:, at], kept[:, at, :, 1]))
                if ok(0, TILES):
                    at = k % 2
                    dve.wait_ge(tab_in[at], uses(s, k, 16))
                    if late(s, 2):
                        dve.wait_ge(gathered[at], uses(s, k, 16 * PARTS) - 16 * PARTS)
                    st.mark(v.tensor_copy(from_id[:, at], tab[:, at, :, 0]))
                    st.do(v.tensor_tensor(away[:], tab[:, at], m.away.rearrange("p (h c) -> p h c", c=2), ALU.subtract))
                    v.tensor_tensor(kept[:, at], away[:], m.valid[:, bass.ds(s, 1), :].rearrange("p o h -> p h o").to_broadcast([P, PARTS, 2]),
                                    ALU.mult).then_inc(q["ids_ready"], 1)
                    dve.wait_ge(q["ids_ready"], s + 1)
                if ok(UP, TILES):
                    at = (k - UP) % 2
                    for b in range(FC // 2):
                        part = slice(2 * b, 2 * b + 2)
                        dve.wait_ge(q["gelu_ready"], (FC // 2) * u + b + 1)
                        if late(u, 2):
                            dve.wait_ge(q["down_done"], u - 1)
                        st.do(v.tensor_copy(act_hi[:, at, part], act_f[:, part]))
                        v.tensor_tensor(act_lo[:, at, part], act_f[:, part], act_hi[:, at, part], ALU.subtract).then_inc(q["act_ready"], 1)
                        if b == 0 and ok(DOWN, TILES):
                            weigh(d, k % 2)
                elif ok(DOWN, TILES):
                    weigh(d, k % 2)

            def weigh(d, at):
                dve.wait_ge(q["down_done"], d + 1)
                for h in range(PARTS):
                    ins = v.tensor_scalar(y[:, at, h], bY[at][:, h * D:(h + 1) * D], weight[:, at, h:h + 1], None, ALU.mult)
                    if h == 0:
                        st.mark(ins)
                ins.then_inc(q["y_ready"], 1)

            run(dve, st, slot)
            st.settle()


CONSTS = {"ident_f": P, "tri_f": P, "rev_e": E, "index_e": E, "sign": 2 * E, "centre": 2 * E, "centre_e": E,
          "first_tokens": GB, "pos_p": PARTS, "away": 2 * PARTS, "below": E * E, "tile_no": TILES}


def constants():
    p, e = np.arange(P), np.arange(E)
    wide = lambda x: np.broadcast_to(np.asarray(x).reshape(1, -1), (P, np.size(x)))
    tables = {
        "ident_f": np.eye(P),
        "tri_f": p[:, None] < p[None, :],
        "rev_e": wide(E - e),
        "index_e": wide(e),
        "sign": wide(np.repeat([-1, 1], E)),
        "centre": wide(np.concatenate([e * ROWS + CENTRE - 1, e * ROWS + CENTRE])),
        "centre_e": wide(e * ROWS + CENTRE),
        "first_tokens": np.arange(GB)[None, :] * N + p[:, None],
        "pos_p": np.stack([p + h * P for h in range(PARTS)], axis=1),
        "away": np.stack([TOKENS + p, 0 * p] * PARTS, axis=1),
        "below": wide(e[None, :] < e[:, None]),
        "tile_no": wide(np.arange(TILES)),
    }
    return np.concatenate([tables[n].astype(np.float32) for n in CONSTS], axis=1)


class Kept:

    def __init__(self, nc, ctx):
        sb = lambda n, s, d: ctx.enter_context(nc.sbuf_tensor(n, s, d))
        self.w_ffn_hi = sb("w_ffn_hi", [P, WCHUNKS, WCH], BF16)
        self.w_ffn_lo = sb("w_ffn_lo", [P, WCHUNKS, WCH], BF16)
        self.w_hi = sb("w_hi", [P, KC, QKV], BF16)
        self.w_lo = sb("w_lo", [P, KC, QKV], BF16)
        self.w_out_hi = sb("w_out_hi", [P, KC, D], BF16)
        self.w_out_lo = sb("w_out_lo", [P, KC, D], BF16)
        self.w_gate_hi = sb("w_gate_hi", [P, KC, E], BF16)
        self.w_gate_lo = sb("w_gate_lo", [P, KC, E], BF16)
        self.bias_qk = sb("bias_qk", [P, 2 * D], F32)
        self.bias_gate = sb("bias_gate", [P, 2 * HEADS], F32)
        self.bo_rows = sb("bo_rows", [P, D], BF16)
        self.b1 = sb("b1", [P, E * FC], F32)
        self.ident = sb("ident", [P, P], BF16)
        self.tri = sb("tri", [P, P], BF16)
        self.ones = sb("ones", [P, P], BF16)
        self.token_id = sb("token_id", [P, GB], F32)
        self.placed = sb("placed", [P, 2 * E], F32)
        self.valid = sb("valid", [P, TILES, PARTS], F32)
        self.tile_info = sb("tile_info", [P, 2, TILES], I32)
        self.consts = sb("consts", [P, sum(CONSTS.values())], F32)
        at = {}
        col = 0
        for name, width in CONSTS.items():
            at[name] = self.consts[:, col:col + width]
            col += width
        self.ident_f, self.tri_f, self.rev_e, self.index_e = at["ident_f"], at["tri_f"], at["rev_e"], at["index_e"]
        self.sign, self.centre, self.centre_e = at["sign"], at["centre"], at["centre_e"]
        self.first_tokens, self.pos_p, self.away = at["first_tokens"], at["pos_p"], at["away"]
        self.below, self.tile_no = at["below"], at["tile_no"]


def build(nc, dram):
    dram = dict(dram)
    dram["tok"] = nc.dram_tensor("tok_rows", [B * N_PATCH, D], F32, kind="Internal").ap()
    dram["bias_parts"] = nc.dram_tensor("bias_part_rows", [3, (E + 1) * D], BF16, kind="Internal").ap()
    dram["xln"] = nc.dram_tensor("xln_rows", [TOKENS, 2 * D], BF16, kind="Internal").ap()
    dram["table"] = nc.dram_tensor("table_rows", [E * ROWS, 2], F32, kind="Internal").ap()
    with ExitStack() as ctx:
        m = Kept(nc, ctx)
        prepare_and_tokenise(nc, m, dram)
        fusion_attention(nc, m, dram)
        plan_tiles(nc, m)
        expert_tiles(nc, m, dram)


def kernel(**inputs):
    import concourse.bacc as bacc
    from concourse.bass_utils import run_bass_kernel_spmd

    a = {k: np.asarray(v) for k, v in inputs.items()}
    img = a["x"][:, :, :GRID * PATCH, :GRID * PATCH].reshape(B, C_IN, GRID, PATCH, GRID, PATCH)
    patches = img.transpose(0, 1, 3, 5, 2, 4).reshape(B * N_PATCH, FLATC, P).transpose(2, 1, 0)
    rows = lambda w: w.reshape(KC, P, -1).transpose(1, 0, 2)
    w1 = a["L0_ffn_W1"].reshape(E * KC, P, F)
    w2 = a["L0_ffn_W2"].reshape(E * 2, 4, P, D).transpose(0, 2, 1, 3).reshape(E * 2, P, 4 * D)
    arrays = {
        "patches": patches,
        "txt": a["txt"],
        "w_tok": a["L0_tok_W"].reshape(FLATC, P, D).transpose(1, 0, 2),
        "w_qk": np.concatenate([rows(a["L0_attn_Wq"]), rows(a["L0_attn_Wk"])], axis=2),
        "w_v": rows(a["L0_attn_Wv"]),
        "w_o": rows(a["L0_attn_Wo"]),
        "w_g": rows(a["L0_ffn_Wg"]),
        "ln_w": a["L0_attn_ln_w"].reshape(KC, P).T,
        "ln_b": a["L0_attn_ln_b"].reshape(KC, P).T,
        "gq": a["L0_attn_gq"],
        "gk": a["L0_attn_gk"],
        "w_ffn": np.concatenate([w1, w2], axis=0),
        "b1": a["L0_ffn_b1"].reshape(E * FC, P).T,
        "biases": np.concatenate([a["L0_attn_bo"], a["L0_ffn_b2"].reshape(E * D)]).reshape(P, -1),
        "consts": constants(),
    }
    arrays = {"in_" + k: np.ascontiguousarray(v) for k, v in arrays.items()}
    nc = bacc.Bacc("TRN2", target_bir_lowering=False, num_devices=1)
    dram = {k[3:]: nc.dram_tensor(k, v.shape, mybir.dt.from_np(v.dtype), kind="ExternalInput").ap() for k, v in arrays.items()}
    dram["out"] = nc.dram_tensor("out_rows", (TOKENS + P, D), F32, kind="ExternalOutput").ap()
    build(nc, dram)
    r = run_bass_kernel_spmd(nc, [arrays], core_ids=[0])
    return r.results[0]["out_rows"][:TOKENS].reshape(B, N, D)
```

```python
from contextlib import ExitStack

import numpy as np

import concourse.bass as bass
from concourse import mybir

F32 = mybir.dt.float32
BF16 = mybir.dt.bfloat16
I32 = mybir.dt.int32
U32 = mybir.dt.uint32
ALU = mybir.AluOpType
ACT = mybir.ActivationFunctionType
AX = mybir.AxisListType

P = 128
B, C_IN, IMG, PATCH = 64, 3, 84, 16
GRID = IMG // PATCH
N_PATCH = GRID * GRID
N_TXT = 77
N = N_PATCH + N_TXT
D = 256
KC = D // P
FLAT = C_IN * PATCH * PATCH
FLATC = FLAT // P
TOKENS = B * N
HEADS, HD = 16, 16
THRESH, SHARP = 0.29514, 15.0
LN_EPS, NORM_EPS = 1e-05, 1e-12
E, F = 8, 1024
FC = F // P
CAP = 2 * 2 * TOKENS // E
PAIR = 2
SLOTS = B // PAIR
GROUP = 4
GB = GROUP * PAIR
BIAS_PARTS = 3
HALF = HEADS // 2
QKV = 2 * D + D + 2 * HEADS
WCH = 1024
WCHUNKS = 2 * E * KC
TILE, PARTS = 256, 2
TILES = 2 * TOKENS // TILE + E - 1
CENTRE = TOKENS
ROWS = 2 * TOKENS
RSQRT_GUESS = float(0x5F3759DF)
NEWTON_ROUNDS = 3
ATTENTION_STEPS, FFN_STEPS = 155, 18
NQK, NV2, NV1, NR2, NCOLS = 0, 2 * PAIR * HEADS, 2 * PAIR * HEADS + PAIR, 2 * PAIR * HEADS + 2 * PAIR, 2 * PAIR * HEADS + 3 * PAIR


class Steps:

    def __init__(self, eng, sem, per_round=0):
        self.eng, self.sem, self.n, self.base, self.per_round = eng, sem, 0, 0, per_round

    def mark(self, ins):
        self.n += 1
        return ins.then_inc(self.sem, 1)

    def settle(self):
        self.eng.wait_ge(self.sem, self.base + self.n)

    def do(self, ins):
        self.mark(ins)
        self.settle()


def slots(eng, steps, slot, loop_from, unroll, rounds, total):
    def known(s):
        return lambda lag, count: 0 <= s - lag < count
    for s in range(loop_from):
        slot(s, s % unroll, known(s))
    at = steps.n if steps else 0
    with eng.Fori(0, rounds) as it:
        if steps:
            steps.base = it * steps.per_round
        for k in range(unroll):
            slot(it * unroll + (loop_from + k), (loop_from + k) % unroll, lambda lag, count: True)
    if steps:
        assert steps.n - at == steps.per_round, steps.n - at
        steps.base, steps.n = 0, at + steps.per_round * rounds
    for s in range(loop_from + unroll * rounds, total):
        slot(s, s % unroll, known(s))


def wait_before_dma(eng, past, *waits):
    values = [v if isinstance(v, int) else eng.to_reg(v) for _, v in waits]
    eng.wait_ge(*past)
    for (sem, _), value in zip(waits, values):
        eng.wait_ge(sem, value)


def in_turn(steps, *chains):
    left = list(chains)
    while left:
        left = [chain for chain in left if next(chain, None) is not None]
        steps.settle()


def inverse_sqrt(nc, steps, done, y, x, t):
    yield steps.mark(nc.vector.tensor_scalar(y.bitcast(I32), x.bitcast(I32), -0.5, RSQRT_GUESS, ALU.mult, ALU.add))
    for n in range(NEWTON_ROUNDS):
        yield steps.mark(nc.vector.tensor_tensor(t, y, y, ALU.mult))
        yield steps.mark(nc.vector.scalar_tensor_tensor(out=t, in0=t, scalar=-0.5, in1=x, op0=ALU.mult, op1=ALU.mult))
        last = nc.vector.scalar_tensor_tensor(out=y, in0=t, scalar=1.5, in1=y, op0=ALU.add, op1=ALU.mult)
        yield steps.mark(last) if n < NEWTON_ROUNDS - 1 else last.then_inc(done, 1)


def prepare_and_tokenise(nc, m, dram):
    CHUNK, GROUP = 200, 100
    PER = CHUNK // GROUP
    with ExitStack() as ctx:
        sb = lambda n, s, d: ctx.enter_context(nc.sbuf_tensor(n, s, d))
        sem = lambda n: ctx.enter_context(nc.semaphore(n))
        w_tok = sb("w_tok", [P, FLATC, D], F32)
        w_tok_hi = sb("w_tok_hi", [P, FLATC, D], BF16)
        w_tok_lo = sb("w_tok_lo", [P, FLATC, D], BF16)
        w_all = sb("w_all", [P, KC, QKV], F32)
        w_raw = sb("w_raw", [P, KC, 2 * D], F32)
        w_out = sb("w_out", [P, KC, D], F32)
        w_gate = sb("w_gate", [P, KC, E], F32)
        gated = sb("gated", [P, KC, 2 * D], F32)
        ln_w = sb("ln_w", [P, KC], F32)
        ln_b = sb("ln_b", [P, KC], F32)
        ln_b_cols = sb("ln_b_cols", [P, KC, P], F32)
        g_row = sb("g_row", [P, 2, HD], F32)
        pat = sb("pat", [P, 2, FLATC, CHUNK], F32)
        pat_hi = sb("pat_hi", [P, 2, FLATC, CHUNK], BF16)
        pat_lo = sb("pat_lo", [P, 2, FLATC, CHUNK], BF16)
        tok = sb("tok", [P, 2, D], F32)
        bias = sb("bias", [P, (E + 1) * D // P], F32)
        bias_rest = sb("bias_rest", [P, (E + 1) * D // P], F32)
        bias_parts = sb("bias_parts", [P, 3, (E + 1) * D // P], BF16)
        zeros = sb("zeros", [P, E * ROWS * 2 // P], F32)
        ps_tok = [ctx.enter_context(nc.psum_tensor(f"ps_tok{i}", [P, 512], F32)) for i in range(2)]
        ps_bias = ctx.enter_context(nc.psum_tensor("ps_bias", [P, 512], F32))

        consts_in = sem("consts_in")
        w_tok_in = sem("w_tok_in")
        w_in = sem("w_in")
        pat_in = [sem(f"pat_in{i}") for i in range(2)]
        dve_steps = sem("dve_steps1")
        w_tok_ready = sem("w_tok_ready")
        hi_ready = sem("pat_hi_ready")
        lo_ready = sem("pat_lo_ready")
        group_done = sem("group_done")
        group_copied = sem("group_copied")
        tok_out = [sem(f"tok_out{i}") for i in range(2)]
        ln_b_ready = sem("ln_b_ready")
        bias_done = sem("bias_done")
        bias_split = sem("bias_split")
        bias_out = sem("bias_out")
        zero_ready = sem("zero_ready")
        bo_in = sem("bo_in")
        rows_zero = sem("rows_zero")
        block = ctx.enter_context(nc.Block())
        LOADS = B * N_PATCH // CHUNK

        @block.sync
        def _(sp):
            sp.dma_start(w_tok[:], dram["w_tok"]).then_inc(w_tok_in, 16)
            for c in range(2):
                sp.dma_start(pat[:, c], dram["patches"][:, :, CHUNK * c:CHUNK * (c + 1)]).then_inc(pat_in[c], 16)
            for dst, src in ((m.consts[:], dram["consts"]), (m.b1[:], dram["b1"])):
                sp.dma_start(dst, src).then_inc(consts_in, 16)
            for dst, src in ((w_raw[:], dram["w_qk"]), (w_all[:, :, 2 * D:3 * D], dram["w_v"]), (w_out[:], dram["w_o"]),
                             (bias[:], dram["biases"]), (w_gate[:], dram["w_g"]), (ln_w[:], dram["ln_w"]), (ln_b[:], dram["ln_b"]),
                             (g_row[:, 0, :], dram["gq"].partition_broadcast(P)),
                             (g_row[:, 1, :], dram["gk"].partition_broadcast(P))):
                sp.dma_start(dst, src).then_inc(w_in, 16)
            for i in range(3):
                if i == 0:
                    sp.wait_ge(bias_split, 1)
                sp.dma_start(dram["bias_parts"][i].rearrange("(p c) -> p c", p=P), bias_parts[:, i]).then_inc(bias_out, 16)
            for c in range(2, LOADS):
                sp.wait_ge(hi_ready, c - 1)
                sp.wait_ge(lo_ready, c - 1)
                sp.dma_start(pat[:, c % 2], dram["patches"][:, :, CHUNK * c:CHUNK * (c + 1)]).then_inc(pat_in[c % 2], 16)
            sp.wait_ge(bias_out, 48)
            sp.wait_ge(zero_ready, 1)
            sp.dma_start(m.bo_rows[0:BIAS_PARTS], dram["bias_parts"][:, 0:D]).then_inc(bo_in, 16)
            sp.dma_start(dram["table"].rearrange("(p r) c -> p (r c)", p=P), zeros[:]).then_inc(rows_zero, 16)
            sp.dma_start(dram["out"][TOKENS:TOKENS + P, :], zeros[:, 0:D]).then_inc(rows_zero, 16)
            sp.wait_ge(bo_in, 16)
            sp.wait_ge(rows_zero, 32)
            sp.wait_ge(tok_out[0], 16 * LOADS * PER // 2)
            sp.wait_ge(tok_out[1], 16 * LOADS * PER // 2)

        @block.gpsimd
        def _(pool):
            nc.gpsimd.memset(zeros[:], 0.0).then_inc(zero_ready, 1)

        def copy_groups(act, c):
            for j in range(PER):
                n = PER * c + j
                act.wait_ge(group_done, n + 1)
                if n >= 2:
                    act.wait_ge(tok_out[n % 2], 16 * (n // 2))
                nc.scalar.copy(tok[0:GROUP, n % 2], ps_tok[n % 2][0:GROUP, 0:D]).then_inc(group_copied, 1)
                act.wait_ge(group_copied, n + 1)
                act.dma_start(dram["tok"][GROUP * n:GROUP * (n + 1), :], tok[0:GROUP, n % 2]).then_inc(tok_out[n % 2], 16)

        @block.scalar
        def _(act):
            for c in range(LOADS):
                act.wait_ge(pat_in[c % 2], 16 * (c // 2 + 1))
                if c >= 2:
                    act.wait_ge(group_done, PER * (c - 1))
                nc.scalar.copy(pat_hi[:, c % 2], pat[:, c % 2]).then_inc(hi_ready, 1)
                if c >= 1:
                    copy_groups(act, c - 1)
            copy_groups(act, LOADS - 1)

        @block.tensor
        def _(pe):
            pe.wait_ge(w_tok_ready, 1)
            for c in range(LOADS):
                pe.wait_ge(hi_ready, c + 1)
                pe.wait_ge(lo_ready, c + 1)
                for j in range(PER):
                    n = PER * c + j
                    if n >= 2:
                        pe.wait_ge(group_copied, n - 1)
                    cols = slice(GROUP * j, GROUP * (j + 1))
                    parts = [(x, w, f) for f in range(FLATC) for x, w in ((pat_hi, w_tok_hi), (pat_lo, w_tok_hi), (pat_hi, w_tok_lo))]
                    for i, (x, w, f) in enumerate(parts):
                        mm = nc.tensor.matmul(ps_tok[n % 2][0:GROUP, 0:D], x[:, c % 2, f, cols], w[:, f, :],
                                              start=i == 0, stop=i == len(parts) - 1)
                    mm.then_inc(group_done, 1)
                if c == 0:
                    pe.wait_ge(ln_b_ready, 1)
                    for kc in range(KC):
                        mm = nc.tensor.matmul(ps_bias[:, :], ln_b_cols[:, kc, :], w_raw[:, kc, :], start=kc == 0, stop=kc == KC - 1)
                    mm.then_inc(bias_done, 1)

        @block.vector
        def _(dve):
            st = Steps(dve, dve_steps)
            dve.wait_ge(w_tok_in, 16)
            st.do(nc.vector.tensor_copy(w_tok_hi[:], w_tok[:]))
            nc.vector.tensor_tensor(w_tok_lo[:], w_tok[:], w_tok_hi[:], ALU.subtract).then_inc(w_tok_ready, 1)
            for c in range(LOADS):
                dve.wait_ge(hi_ready, c + 1)
                if c >= 2:
                    dve.wait_ge(group_done, PER * (c - 1))
                nc.vector.tensor_tensor(pat_lo[:, c % 2], pat[:, c % 2], pat_hi[:, c % 2], ALU.subtract).then_inc(lo_ready, 1)
                if c == 0:
                    dve.wait_ge(w_in, 16 * 9)
                    dve.wait_ge(consts_in, 16 * 2)
                    for i in range(3):
                        rest = bias if i == 0 else bias_rest
                        ins = nc.vector.tensor_copy(bias_parts[:, i], rest[:])
                        if i < 2:
                            st.do(ins)
                            st.do(nc.vector.tensor_tensor(bias_rest[:], rest[:], bias_parts[:, i], ALU.subtract))
                    ins.then_inc(bias_split, 1)
                    for kc in range(KC):
                        st.mark(nc.vector.tensor_scalar(w_all[:, kc, 0:2 * D], w_raw[:, kc, :], ln_w[:, kc:kc + 1], None, ALU.mult))
                    nc.vector.tensor_copy(ln_b_cols[:], ln_b[:].unsqueeze(2).to_broadcast([P, KC, P])).then_inc(ln_b_ready, 1)
                    st.mark(nc.vector.tensor_copy(m.ident[:], m.ident_f))
                    st.mark(nc.vector.tensor_copy(m.tri[:], m.tri_f))
                    st.mark(nc.vector.tensor_copy(m.token_id[:], m.first_tokens))
                    st.mark(nc.vector.tensor_copy(m.w_out_hi[:], w_out[:]))
                    st.mark(nc.vector.tensor_copy(m.w_gate_hi[:], w_gate[:]))
                    st.mark(nc.vector.memset(m.ones[:], 1.0))
                    st.settle()
                    st.mark(nc.vector.tensor_tensor(m.w_out_lo[:], w_out[:], m.w_out_hi[:], ALU.subtract))
                    st.mark(nc.vector.tensor_tensor(m.w_gate_lo[:], w_gate[:], m.w_gate_hi[:], ALU.subtract))
                    for kc in range(KC):
                        for i in range(2):
                            st.mark(nc.vector.tensor_tensor(
                                gated[:, kc, i * D:(i + 1) * D].rearrange("p (h d) -> p h d", d=HD),
                                w_all[:, kc, i * D:(i + 1) * D].rearrange("p (h d) -> p h d", d=HD),
                                g_row[:, i, :].unsqueeze(1).to_broadcast([P, HEADS, HD]), ALU.mult))
                    st.settle()
                    for kc in range(KC):
                        st.mark(nc.vector.tensor_reduce(w_all[:, kc, 3 * D:QKV], gated[:, kc, :].rearrange("p (h d) -> p h d", d=HD), AX.X, ALU.add))
                    st.settle()
                    st.do(nc.vector.tensor_copy(m.w_hi[:], w_all[:]))
                    st.mark(nc.vector.tensor_tensor(m.w_lo[:], w_all[:], m.w_hi[:], ALU.subtract))
            dve.wait_ge(bias_done, 1)
            st.do(nc.vector.tensor_copy(m.bias_qk[:], ps_bias[:, :]))
            for i in range(2):
                st.mark(nc.vector.tensor_tensor(
                    gated[:, 0, i * D:(i + 1) * D].rearrange("p (h d) -> p h d", d=HD),
                    m.bias_qk[:, i * D:(i + 1) * D].rearrange("p (h d) -> p h d", d=HD),
                    g_row[:, i, :].unsqueeze(1).to_broadcast([P, HEADS, HD]), ALU.mult))
            st.settle()
            st.mark(nc.vector.tensor_reduce(m.bias_gate[:], gated[:, 0, :].rearrange("p (h d) -> p h d", d=HD), AX.X, ALU.add))
            st.mark(nc.vector.memset(m.placed[:], 0.0))
            st.settle()


def plan_tiles(nc, m, st, small, large):
    v = nc.vector
    taken = [0]

    def room(width):
        taken[0] += width
        return small[:, taken[0] - width:taken[0]]

    first, second, count, tiles, begin, end, v_start, v_left = [room(E) for _ in range(8)]
    tiles_i = room(E).bitcast(I32)
    before = room(E * E).rearrange("p (a b) -> p a b", a=E)
    any_, expert, start, left, rows = [room(TILES) for _ in range(5)]
    own, other = [large[:, i * TILES * E:(i + 1) * TILES * E].rearrange("p (t e) -> p t e", e=E) for i in range(2)]
    n1, n2 = m.placed[:, 0:E], m.placed[:, E:2 * E]
    st.do(v.tensor_scalar(first, n1, float(CAP), None, ALU.min))
    st.do(v.tensor_scalar(second, n1, -1.0, float(CAP), ALU.mult, ALU.add))
    st.do(v.tensor_tensor(second, second, n2, ALU.min))
    st.do(v.tensor_scalar(second, second, 0.0, None, ALU.max))
    st.do(v.tensor_tensor(count, first, second, ALU.add))
    st.do(v.tensor_scalar(tiles_i, count, float(TILE - 1), None, ALU.add))
    st.do(v.tensor_scalar(tiles_i, tiles_i, TILE.bit_length() - 1, None, ALU.arith_shift_right))
    st.do(v.tensor_copy(tiles, tiles_i))
    st.do(v.tensor_tensor(before, m.below.rearrange("p (a b) -> p a b", a=E), tiles.unsqueeze(1).to_broadcast([P, E, E]), ALU.mult))
    st.do(v.tensor_reduce(begin, before, AX.X, ALU.add))
    st.do(v.tensor_tensor(end, begin, tiles, ALU.add))
    t_of = m.tile_no.unsqueeze(2).to_broadcast([P, TILES, E])
    over = lambda ap: ap.unsqueeze(1).to_broadcast([P, TILES, E])
    st.do(v.tensor_tensor(own, t_of, over(begin), ALU.is_ge))
    st.do(v.tensor_tensor(other, t_of, over(end), ALU.is_ge))
    st.do(v.tensor_tensor(own, own, other, ALU.subtract))
    st.do(v.scalar_tensor_tensor(out=v_start, in0=begin, scalar=float(-TILE), in1=m.centre_e, op0=ALU.mult, op1=ALU.add))
    st.do(v.tensor_tensor(v_start, v_start, first, ALU.subtract))
    st.do(v.scalar_tensor_tensor(out=v_left, in0=begin, scalar=float(TILE), in1=count, op0=ALU.mult, op1=ALU.add))
    st.do(v.tensor_reduce(any_, own, AX.X, ALU.add))
    for value, out in ((m.index_e, expert), (v_start, start), (v_left, left)):
        st.do(v.tensor_tensor(other, own, over(value), ALU.mult))
        st.do(v.tensor_reduce(out[:], other, AX.X, ALU.add))
    st.do(v.tensor_tensor(rows, m.tile_no, any_, ALU.mult))
    st.do(v.tensor_scalar(rows, rows, float(TILE), None, ALU.mult))
    st.do(v.tensor_tensor(start, start, rows, ALU.add))
    st.do(v.tensor_tensor(left, left, rows, ALU.subtract))
    for h in range(PARTS):
        st.do(v.tensor_tensor(m.valid[:, :, h], left, m.pos_p[:, h:h + 1].to_broadcast([P, TILES]), ALU.is_gt))
    st.do(v.tensor_copy(m.tile_info[:, 0, :], expert))
    st.do(v.tensor_copy(m.tile_info[:, 1, :], start))


def fusion_attention(nc, m, dram):
    PROJ, ATT, OUT, NORM, ROUTE, PLACE = 1, 2, 3, 4, 5, 10
    TOTAL = SLOTS + PLACE
    RING = GROUP
    LOOP_FROM = 3 * RING
    ROUNDS = (SLOTS - 1 - LOOP_FROM) // RING
    CHOOSE_AT, PLACE_AT = (PLACE - 1) % RING, PLACE % RING
    with ExitStack() as ctx:
        sb = lambda n, s, d: ctx.enter_context(nc.sbuf_tensor(n, s, d))
        sem = lambda n: ctx.enter_context(nc.semaphore(n))
        pb = lambda n: ctx.enter_context(nc.psum_tensor(n, [P, 512], F32))
        h = sb("h", [P, RING, PAIR, D], F32)
        stats = sb("stats", [P, 2, PAIR, 6], F32)
        mv = sb("mv", [P, 2, PAIR, 2], F32)
        squares = sb("squares", [P, NCOLS], F32)
        inv = sb("inv", [P, 2, NCOLS], F32)
        inv_t = sb("inv_t", [P, NCOLS], F32)
        x1 = sb("x1", [P, PAIR, D], F32)
        x2 = sb("x2", [P, PAIR, D], F32)
        qk_sq = sb("qk_sq", [P, PAIR, 2 * D], F32)
        x1T = sb("x1T", [P, PAIR, 2, KC, N], BF16)
        qk = sb("qk", [P, PAIR, 2 * D], F32)
        qks = sb("qks", [P, PAIR, 2 * HEADS, 4, HD], BF16)
        qT = sb("qT", [P, PAIR, HALF, N], BF16)
        kT = sb("kT", [P, PAIR, HALF, N], BF16)
        sig = sb("sig", [P, 2, 2, HALF // 2, N], F32)
        vg = sb("vg", [P, PAIR, D + 2 * HEADS], F32)
        gate = sb("gate", [P, PAIR, 2 * HEADS], F32)
        gate_q = sb("gate_q", [P, PAIR, HEADS, HD], F32)
        v_pad = sb("v_pad", [P, PAIR, HEADS, 2 * HD], F32)
        cT = sb("cT", [P, KC, N], F32)
        cTs = sb("cTs", [P, PAIR, 2, KC, N], BF16)
        h2 = sb("h2", [P, PAIR, D], F32)
        x2T = sb("x2T", [P, PAIR, 2, KC, N], BF16)
        w_stage = sb("w_stage", [P, WCH], F32)
        logits = sb("logits", [P, GB, E], F32)
        mask1 = sb("mask1", [P, GB, E], F32)
        mask2 = sb("mask2", [P, GB, E], F32)
        ex = sb("ex", [P, GB, E], F32)
        sg = sb("sg", [P, 2, GB, E], F32)
        top = sb("top", [P, GB, 8], F32)
        masks = sb("masks", [P, GB, 2, E], BF16)
        places = sb("places", [P, GB, 2, E], F32)
        entry = sb("entry", [P, GB, 2, 2], F32)
        slot_f = sb("slot_f", [P, GB, 2], F32)
        slot_i = sb("slot_i", [P, GB, 2], U32)
        sums = sb("sums", [P, 2 * E], F32)
        sig_bias = sb("sig_bias", [P, 1], F32)
        bT, bQK0, bQK1, bV, bKT, bS0, bS1, bC = [pb(n) for n in ("bT", "bQK0", "bQK1", "bV", "bKT", "bS0", "bS1", "bC")]
        bQK, bS = [bQK0, bQK1], [bS0, bS1]
        xT_ps = bT[:, 0:PAIR * KC * N].rearrange("p (b k n) -> p b k n", b=PAIR, k=KC)
        kt_ps = bKT[:, :].bitcast(BF16)[:, 0:HALF * N].rearrange("p (j n) -> p j n", j=HALF)
        lg_ps = bT[:, 4 * N:4 * N + PAIR * E]
        W = 2 * E
        rank_ps, count_ps = bKT[:, 0:GB * W], bKT[:, GB * W:(GB + 1) * W]

        names = """x1_ready x1T_done x1T_hi x1T_lo qk_done qk_ready v_done v_copied sq_ready inv_ready
            qn_q_ready qn_k_ready q_hi k_hi q_lo k_lo qT_done qT_ready kT_done kT_ready score_done sig_ready gate_ready gate_q_ready vgate_ready
            col_done cg_ready c_ready wo_done h2_ready out_stored x2_ready xln_stored x2T_done x2T_hi x2T_lo lg_done
            lg_read masks_ready pos_done pos_read entry_ready scattered w_loaded w_hi_ready w_lo_ready dve_steps2
            pad_zero bias_set ex_ready sg_ready""".split()
        q = {n: sem(n) for n in names}
        h_loaded = [sem(f"h_loaded{i}") for i in range(RING)]
        block = ctx.enter_context(nc.Block())
        late = lambda x, n: not isinstance(x, int) or x >= n

        def run(eng, steps, slot):
            slots(eng, steps, slot, LOOP_FROM, RING, ROUNDS, TOTAL)

        def tok_of(s):
            v = dram["tok"].rearrange("(g b n) d -> g n b d", b=PAIR, n=N_PATCH)
            return v[bass.ds(s, 1)].rearrange("o n b d -> (o n) b d")

        def txt_of(s):
            v = dram["txt"].rearrange("(g b) n d -> g n b d", b=PAIR)
            return v[bass.ds(s, 1)].rearrange("o n b d -> (o n) b d")

        def rows_of(t, s):
            v = t[0:TOKENS, :].rearrange("(g b n) d -> g n b d", b=PAIR, n=N)
            return v[bass.ds(s, 1)].rearrange("o n b d -> (o n) b d")

        def split_rest(engine, i):
            return engine.tensor_tensor(qks[0:N, :, i * HEADS:(i + 1) * HEADS, 1 + i, :],
                                        qk[0:N, :, i * D:(i + 1) * D].rearrange("n b (h d) -> n b h d", d=HD),
                                        qks[0:N, :, i * HEADS:(i + 1) * HEADS, 0, :], ALU.subtract)

        @block.sync
        def _(sp):
            def load_h(g, k):
                sp.dma_start(h[0:N_PATCH, k], tok_of(g)).then_inc(h_loaded[k], 16)
                sp.dma_start(h[N_PATCH:N, k], txt_of(g)).then_inc(h_loaded[k], 16)

            load_h(0, 0)

            def slot(s, k, ok):
                o = s - OUT
                if ok(0, SLOTS):
                    if late(s, 1):
                        sp.wait_ge(q["w_hi_ready"], s)
                        sp.wait_ge(q["w_lo_ready"], s)
                    sp.dma_start(w_stage[:], dram["w_ffn"][bass.ds(s, 1)].rearrange("o p c -> p (o c)")).then_inc(q["w_loaded"], 16)
                if ok(NORM, SLOTS):
                    sp.wait_ge(q["x2_ready"], s - NORM + 1)
                    sp.dma_start(rows_of(dram["xln"], s - NORM), x2[0:N]).then_inc(q["xln_stored"], 16)
                if ok(OUT, SLOTS):
                    sp.wait_ge(q["h2_ready"], o + 1)
                    sp.dma_start(rows_of(dram["out"], o), h2[0:N]).then_inc(q["out_stored"], 16)
                if ok(-1, SLOTS):
                    load_h(s + 1, (k + 1) % RING)

            run(sp, None, slot)
            sp.wait_ge(q["out_stored"], 16 * SLOTS)
            sp.wait_ge(q["xln_stored"], 16 * SLOTS)

        @block.tensor
        def _(pe):
            def transposes(src, done):
                for b in range(PAIR):
                    for kc in range(KC):
                        mm = nc.tensor.transpose(xT_ps[:, b, kc, :], src[0:N, b, kc * P:(kc + 1) * P], m.ident_f[0:N, 0:N])
                mm.then_inc(done, 1)

            def product(out, xT, b, hi, lo, cols, first=True):
                parts = [(x, w, kc) for kc in range(KC) for x, w in ((0, hi), (1, hi), (0, lo))]
                for i, (x, w, kc) in enumerate(parts):
                    mm = nc.tensor.matmul(out, xT[:, b, x, kc, :], w[:, kc, cols], start=first and i == 0, stop=i == len(parts) - 1,
                                          skip_group_check=not first)
                return mm

            def ranks():
                mk = masks[0:N].rearrange("n b c e -> n (b c e)")
                add = lambda out, lhs, rhs, first, last: nc.tensor.matmul(out, lhs, rhs, start=first, stop=last, skip_group_check=True)
                add(rank_ps, m.tri[0:N, :], mk, True, False)
                for back in range(1, GB):
                    add(rank_ps[:, back * W:], m.ones[0:N, :], mk[:, 0:(GB - back) * W], False, back == GB - 1)
                for b in range(GB):
                    mm = add(count_ps, m.ones[0:N, :], mk[:, b * W:(b + 1) * W], b == 0, b == GB - 1)
                mm.then_inc(q["pos_done"], GROUP)

            def slot(s, k, ok):
                p, a, o, r = s - PROJ, s - ATT, s - OUT, s - ROUTE
                has_p, has_a, has_o, has_r = ok(PROJ, SLOTS), ok(ATT, SLOTS), ok(OUT, SLOTS), ok(ROUTE, SLOTS)

                def turn(b, which, done):
                    n = 2 * a + b
                    if which == 0:
                        if b == 0:
                            pe.wait_ge(q["q_lo"], a + 1)
                            if k == PLACE_AT and ok(PLACE, SLOTS):
                                pe.wait_ge(q["pos_read"], s - 1 - ROUTE)
                        if late(n, 1):
                            pe.wait_ge(q["kT_ready"], n)
                    else:
                        if b == 0:
                            pe.wait_ge(q["k_lo"], a + 1)
                        pe.wait_ge(q["qT_ready"], n + 1)
                    for j in range(HALF):
                        mm = nc.tensor.transpose(kt_ps[:, j, :], qks[0:N, b, which * HEADS + 2 * j:which * HEADS + 2 * j + 2].rearrange("n h c d -> n (h c d)"),
                                                 m.ident[0:N, 0:N])
                    mm.then_inc(done, 1)

                def scores(pair, b, half):
                    n = 8 * pair + 4 * b + 2 * half
                    if half == 0:
                        pe.wait_ge(q["kT_ready"], 2 * pair + b + 1)
                    for u in range(2):
                        if late(n + u, 2):
                            pe.wait_ge(q["sig_ready"], n + u - 1)
                    for j in range(HALF // 2):
                        for u in range(2):
                            rows = slice(64 * u, 64 * u + 64)
                            mm = nc.tensor.matmul(bS[u][0:N, j * N:(j + 1) * N], kT[rows, b, half * 4 + j, :], qT[rows, b, half * 4 + j, :],
                                                  start=True, stop=True)
                            if j == HALF // 2 - 1:
                                mm.then_inc(q["score_done"], 1)

                def collapse(pair, b):
                    n = 2 * pair + b
                    if b == 0:
                        pe.wait_ge(q["gate_q_ready"], pair + 1)
                    if late(n, 1):
                        pe.wait_ge(q["c_ready"], n)
                    for kc in range(KC):
                        mm = nc.tensor.matmul(bC[:, (2 + kc) * N:(3 + kc) * N], gate_q[0:N, b].rearrange("n h d -> n (h d)")[:, kc * P:(kc + 1) * P],
                                              m.ident_f[0:N, 0:N], start=True, stop=True, skip_group_check=True)
                    mm.then_inc(q["col_done"], 1)
                    if b == 0:
                        pe.wait_ge(q["vgate_ready"], pair + 1)
                    for half in range(2):
                        pe.wait_ge(q["sig_ready"], 8 * pair + 4 * b + 2 * half + 2)
                        for j in range(4):
                            for u in range(2):
                                mm = nc.tensor.matmul(bC[32 * j:32 * j + 32, half * N:(half + 1) * N], v_pad[0:N, b, 2 * (4 * half + j) + u, :],
                                                      sig[0:N, half, u, j, :], start=u == 0, stop=u == 1, skip_group_check=True)
                        mm.then_inc(q["col_done"], 1)

                def project_qk(b):
                    if b == 0:
                        pe.wait_ge(q["x1T_hi"], p + 1)
                        pe.wait_ge(q["x1T_lo"], p + 1)
                    if late(p, 1):
                        pe.wait_ge(q["qk_ready"], 2 * p + b - 1)
                    product(bQK[b][0:N, :], x1T, b, m.w_hi, m.w_lo, slice(0, 2 * D)).then_inc(q["qk_done"], 1)

                def project_v(b):
                    n = 2 * p + b
                    if late(n, 1):
                        pe.wait_ge(q["v_copied"], n)
                    if b == 0 and ok(OUT + 1, SLOTS):
                        pe.wait_ge(q["h2_ready"], o)
                    product(bV[0:N, 0:D + 2 * HEADS], x1T, b, m.w_hi, m.w_lo, slice(2 * D, QKV)).then_inc(q["v_done"], 1)

                if has_a:
                    turn(0, 0, q["qT_done"])
                if has_p:
                    project_qk(0)
                if has_o:
                    scores(o, 1, 1)
                if has_p:
                    project_qk(1)
                if has_r:
                    pe.wait_ge(q["x2_ready"], r + 1)
                    if has_p:
                        pe.wait_ge(q["x1T_lo"], p + 1)
                        pe.wait_ge(q["x1T_hi"], p + 1)
                    elif ok(ROUTE + 1, SLOTS):
                        pe.wait_ge(q["lg_read"], r)
                    transposes(x2, q["x2T_done"])
                if has_a:
                    turn(0, 1, q["kT_done"])
                if has_o:
                    collapse(o, 1)
                if has_a:
                    scores(a, 0, 0)
                    turn(1, 0, q["qT_done"])
                if has_r:
                    pe.wait_ge(q["x2T_hi"], r + 1)
                    pe.wait_ge(q["x2T_lo"], r + 1)
                    for b in range(PAIR):
                        mm = product(lg_ps[0:N, b * E:(b + 1) * E], x2T, b, m.w_gate_hi, m.w_gate_lo, slice(0, E))
                    mm.then_inc(q["lg_done"], 1)
                if has_p:
                    project_v(0)
                if has_a:
                    scores(a, 0, 1)
                    turn(1, 1, q["kT_done"])
                if has_p:
                    project_v(1)
                if has_o:
                    pe.wait_ge(q["v_copied"], 2 * p + 2 if has_p else 2 * SLOTS)
                    if late(o, 1) and not has_p:
                        pe.wait_ge(q["h2_ready"], o)
                    nc.tensor.matmul(bV[0:N, :], m.ones[0:BIAS_PARTS, 0:N], m.bo_rows[0:BIAS_PARTS].unsqueeze(1).to_broadcast([BIAS_PARTS, PAIR, D]), start=True, stop=False,
                                     skip_group_check=True)
                    pe.wait_ge(q["c_ready"], 2 * o + 2)
                    for b in range(PAIR):
                        mm = product(bV[0:N, b * D:(b + 1) * D], cTs, b, m.w_out_hi, m.w_out_lo, slice(0, D), first=False)
                    mm.then_inc(q["wo_done"], 1)
                if has_a:
                    scores(a, 1, 0)
                if ok(0, SLOTS):
                    pe.wait_ge(q["x1_ready"], s + 1)
                    if has_r:
                        pe.wait_ge(q["lg_read"], r + 1)
                    elif late(s, 1):
                        pe.wait_ge(q["x1T_lo"], s)
                        pe.wait_ge(q["x1T_hi"], s)
                    transposes(x1, q["x1T_done"])
                if has_a:
                    collapse(a, 0)
                if k == CHOOSE_AT and ok(PLACE - 1, SLOTS):
                    pe.wait_ge(q["masks_ready"], s - ROUTE)
                    pe.wait_ge(q["kT_ready"], 2 * a + 2 if has_a else 2 * SLOTS)
                    ranks()

            run(pe, None, slot)

        @block.scalar
        def _(act):
            def slot(s, k, ok):
                p, a, o = s - PROJ, s - ATT, s - OUT
                has_p, has_a, has_o = ok(PROJ, SLOTS), ok(ATT, SLOTS), ok(OUT, SLOTS)

                def keep_qT(b):
                    n = 2 * a + b
                    act.wait_ge(q["qT_done"], n + 1)
                    if late(n, 2):
                        act.wait_ge(q["score_done"], 4 * n - 4)
                    nc.scalar.copy(qT[:, b], kt_ps).then_inc(q["qT_ready"], 1)

                def keep_v(b):
                    n = 2 * p + b
                    act.wait_ge(q["v_done"], n + 1)
                    if late(p, 1) and b == 0:
                        act.wait_ge(q["vgate_ready"], p)
                    nc.scalar.copy(vg[0:N, b], bV[0:N, 0:D + 2 * HEADS]).then_inc(q["v_copied"], 1)

                def resonance(pair, b, half):
                    for u in range(2):
                        n = 8 * pair + 4 * b + 2 * half + u
                        act.wait_ge(q["score_done"], n + 1)
                        if late(2 * pair + b, 1):
                            act.wait_ge(q["col_done"], 3 * (2 * pair + b - 1) + half + 2)
                        nc.scalar.activation(sig[0:N, half, u], bS[u][0:N, 0:4 * N].rearrange("n (j t) -> n j t", j=4), ACT.Sigmoid,
                                             bias=sig_bias[0:N, :], scale=SHARP).then_inc(q["sig_ready"], 1)

                def keep_gates(pair, b):
                    n = 2 * pair + b
                    act.wait_ge(q["col_done"], 3 * n + 3)
                    if late(n, 1):
                        act.wait_ge(q["c_ready"], n)
                    nc.scalar.copy(cT[:], bC[:, 2 * N:4 * N].rearrange("p (k n) -> p k n", n=N)).then_inc(q["cg_ready"], 1)

                def keep_high(i):
                    act.wait_ge(q[("qn_q_ready", "qn_k_ready")[i]], p + 1)
                    if late(p, 1):
                        act.wait_ge(q[("qT_done", "kT_done")[i]], 2 * p)
                    for b in range(PAIR):
                        dst = qks[0:N, b, i * HEADS:(i + 1) * HEADS, 0:3 - i:2 - i, :]
                        src = qk[0:N, b, i * D:(i + 1) * D].rearrange("n (h d) -> n h d", d=HD).unsqueeze(2).to_broadcast([N, HEADS, 2, HD])
                        ins = nc.scalar.copy(dst, src)
                    ins.then_inc(q[("q_hi", "k_hi")[i]], 1)

                def squares_of(b):
                    act.wait_ge(q["qk_ready"], 2 * p + b + 1)
                    if b == 0:
                        if late(p, 1):
                            act.wait_ge(q["inv_ready"], s)
                    nc.scalar.activation(qk_sq[0:N, b], qk[0:N, b], ACT.Square).then_inc(q["sq_ready"], 1)

                def keep_kT(b):
                    n = 2 * a + b
                    act.wait_ge(q["kT_done"], n + 1)
                    if late(n, 2):
                        act.wait_ge(q["score_done"], 4 * n - 4)
                    nc.scalar.copy(kT[:, b], kt_ps).then_inc(q["kT_ready"], 1)

                if has_a:
                    keep_qT(0)
                if has_p:
                    squares_of(0)
                if has_o:
                    resonance(o, 1, 1)
                if ok(ROUTE, SLOTS):
                    r = s - ROUTE
                    act.wait_ge(q["x2T_done"], r + 1)
                    if late(r, 1):
                        act.wait_ge(q["lg_done"], r)
                    nc.scalar.copy(x2T[:, :, 0], xT_ps).then_inc(q["x2T_hi"], 1)
                if has_p:
                    squares_of(1)
                if has_a:
                    keep_kT(0)
                if has_o:
                    keep_gates(o, 1)
                if has_a:
                    resonance(a, 0, 0)
                    keep_qT(1)
                if has_p:
                    keep_v(0)
                if has_a:
                    resonance(a, 0, 1)
                if has_p:
                    keep_v(1)
                if has_a:
                    keep_kT(1)
                if ok(0, SLOTS):
                    act.wait_ge(q["w_loaded"], 16 * (s + 1))
                    nc.scalar.copy(m.w_ffn_hi[:, bass.ds(s, 1)].rearrange("p o c -> p (o c)"), w_stage[:]).then_inc(q["w_hi_ready"], 1)
                if has_p:
                    keep_high(0)
                if ok(0, SLOTS):
                    act.wait_ge(q["x1T_done"], s + 1)
                    if late(s, 1):
                        act.wait_ge(q["v_done"], 2 * s)
                    nc.scalar.copy(x1T[:, :, 0], xT_ps).then_inc(q["x1T_hi"], 1)
                if has_p:
                    keep_high(1)
                if has_a:
                    keep_gates(a, 0)
                if k == CHOOSE_AT and ok(PLACE - 1, SLOTS):
                    act.wait_ge(q["ex_ready"], s - ROUTE)
                    nc.scalar.activation(sg[0:N, 0], ex[0:N], ACT.Sigmoid)
                    nc.scalar.activation(sg[0:N, 1], ex[0:N], ACT.Sigmoid, scale=-1.0).then_inc(q["sg_ready"], GROUP)
                if has_a:
                    resonance(a, 1, 0)

            act.wait_ge(q["bias_set"], 1)
            run(act, None, slot)

        @block.gpsimd
        def _(pool):
            nc.gpsimd.memset(sig_bias[:], -THRESH * SHARP).then_inc(q["bias_set"], 1)
            nc.gpsimd.memset(v_pad[:], 0.0).then_inc(q["pad_zero"], 1)
            nc.gpsimd.memset(qks[:, :, :, 3, :], 0.0).then_inc(q["pad_zero"], 1)
            pool.wait_ge(q["pad_zero"], 2)

            def scatter(c, k, ok, b):
                if ok(PLACE, SLOTS):
                    first = (k - PLACE) % RING
                    wait_before_dma(pool, (q["pad_zero"], 2), (q["entry_ready"], c + (GROUP - first)))
                    for i in range(2):
                        nc.gpsimd.indirect_dma_start(dram["table"], bass.IndirectOffsetOnAxis(ap=slot_i[0:N, PAIR * first + b, i:i + 1], axis=0),
                                                     entry[0:N, PAIR * first + b, i, :], None).then_inc(q["scattered"], 16)

            def slot(s, k, ok):
                p, a, o, c = s - PROJ, s - ATT, s - OUT, s - PLACE
                if k != PLACE_AT:
                    scatter(c, k, ok, 0)
                if ok(ATT, SLOTS):
                    pool.wait_ge(q["gate_ready"], a + 1)
                    if late(a, 1):
                        pool.wait_ge(q["col_done"], 6 * a)
                    for b in range(PAIR):
                        for u in range(2):
                            ins = nc.gpsimd.tensor_tensor(
                                v_pad[0:N, b].rearrange("n (j u) c -> n j u c", u=2)[:, :, u, u * HD:(u + 1) * HD],
                                vg[0:N, b, 0:D].rearrange("n (j u d) -> n j u d", u=2, d=HD)[:, :, u, :],
                                gate[0:N, b, HEADS:].rearrange("n (j u) -> n j u", u=2)[:, :, u:u + 1].to_broadcast([N, HALF, HD]), ALU.mult)
                    ins.then_inc(q["vgate_ready"], 1)
                if k != PLACE_AT:
                    scatter(c, k, ok, 1)
                if ok(PROJ, SLOTS):
                    pool.wait_ge(q["inv_ready"], s + 1)
                    norm = inv[0:N, k % 2, NQK:NV2].rearrange("n (b i h) -> n b i h", b=PAIR, i=2)
                    for i, done in enumerate(("qn_q_ready", "qn_k_ready")):
                        for b in range(PAIR):
                            part = qk[0:N, b, i * D:(i + 1) * D].rearrange("n (h d) -> n h d", d=HD)
                            ins = nc.gpsimd.tensor_tensor(part, part, norm[:, b, i].unsqueeze(2).to_broadcast([N, HEADS, HD]), ALU.mult)
                        ins.then_inc(q[done], 1)
                if ok(PROJ, SLOTS):
                    pool.wait_ge(q["q_hi"], p + 1)
                    split_rest(nc.gpsimd, 0).then_inc(q["q_lo"], 1)
                if ok(PROJ, SLOTS):
                    pool.wait_ge(q["k_hi"], p + 1)
                    split_rest(nc.gpsimd, 1).then_inc(q["k_lo"], 1)
                if k == PLACE_AT:
                    scatter(c, k, ok, 0)
                    scatter(c, k, ok, 1)
                if ok(0, SLOTS):
                    pool.wait_ge(q["w_hi_ready"], s + 1)
                    nc.gpsimd.tensor_tensor(m.w_ffn_lo[:, bass.ds(s, 1)].rearrange("p o c -> p (o c)"), w_stage[:],
                                            m.w_ffn_hi[:, bass.ds(s, 1)].rearrange("p o c -> p (o c)"), ALU.subtract).then_inc(q["w_lo_ready"], 1)

            run(pool, None, slot)
            pool.wait_ge(q["scattered"], 16 * 4 * SLOTS)

        @block.vector
        def _(dve):
            st = Steps(dve, q["dve_steps2"], ATTENTION_STEPS)
            v = nc.vector
            st.mark(v.memset(squares[:], 1.0))
            st.mark(v.memset(inv[:], 1.0))
            st.settle()
            wide = lambda ap: ap.to_broadcast([N, GB, E])
            col = lambda i: top[0:N, :, i:i + 1]

            def choose(x, mask, best):
                iota = m.rev_e[0:N].unsqueeze(1).to_broadcast([N, GB, E])
                yield st.mark(v.tensor_reduce(col(best), x, AX.X, ALU.max))
                yield st.mark(v.tensor_tensor(mask, x, wide(col(best)), ALU.is_equal))
                yield st.mark(v.tensor_tensor(mask, mask, iota, ALU.mult))
                yield st.mark(v.tensor_reduce(col(2), mask, AX.X, ALU.max))
                yield st.mark(v.tensor_tensor(mask, mask, wide(col(2)), ALU.is_equal))

            def route():
                L, M1, M2, X = logits[0:N], mask1[0:N], mask2[0:N], ex[0:N]
                yield from choose(L, M1, 0)
                yield st.mark(v.scalar_tensor_tensor(out=X, in0=M1, scalar=-3.0e38, in1=L, op0=ALU.mult, op1=ALU.add))
                yield from choose(X, M2, 1)
                st.mark(v.tensor_copy(masks[0:N, :, 0, :], M1))
                v.tensor_copy(masks[0:N, :, 1, :], M2).then_inc(q["masks_ready"], GROUP)
                yield v.tensor_tensor(X, L, wide(col(0)), ALU.subtract).then_inc(q["ex_ready"], GROUP)

            def read_ranks(done):
                dve.wait_ge(q["pos_done"], done)
                st.mark(v.tensor_copy(sums[:], count_ps))
                v.tensor_tensor(places[0:N].rearrange("n b c e -> n b (c e)"), rank_ps[0:N, :].rearrange("n (b w) -> n b w", w=W),
                                m.placed[0:N].unsqueeze(1).to_broadcast([N, GB, W]), ALU.add).then_inc(q["pos_read"], GROUP)

            def place(s):
                done = s - 1 - ROUTE
                both = lambda ap: ap.rearrange("p (c e) -> p c e", c=2).unsqueeze(1).to_broadcast([N, GB, 2, E])
                M2, EX = mask2[0:N], ex[0:N]
                dve.wait_ge(q["sg_ready"], done)
                st.mark(v.reciprocal(EX, sg[0:N, 1]))
                dve.wait_ge(q["pos_read"], done)
                st.mark(v.tensor_tensor(m.placed[:], m.placed[:], sums[:], ALU.add))
                yield st.mark(v.tensor_tensor(places[0:N], places[0:N], both(m.sign[0:N]), ALU.mult))
                st.mark(v.tensor_tensor(EX, EX, sg[0:N, 0], ALU.mult))
                yield st.mark(v.tensor_tensor(places[0:N], places[0:N], both(m.centre[0:N]), ALU.add))
                st.mark(v.tensor_reduce(col(2), EX, AX.X, ALU.add))
                yield st.mark(v.tensor_tensor(places[0:N], places[0:N], masks[0:N], ALU.mult))
                st.mark(v.tensor_tensor(EX, EX, M2, ALU.mult))
                if late(s, PLACE + GROUP):
                    dve.wait_ge(q["scattered"], 64 * (s - PLACE))
                yield st.mark(v.tensor_reduce(slot_f[0:N], places[0:N], AX.X, ALU.add))
                st.mark(v.tensor_reduce(col(3), EX, AX.X, ALU.add))
                st.mark(v.reciprocal(col(2), col(2)))
                yield st.mark(v.tensor_copy(slot_i[0:N], slot_f[0:N]))
                st.mark(v.tensor_scalar(col(6), col(2), 1e-9, None, ALU.add))
                st.mark(v.tensor_tensor(col(3), col(3), col(2), ALU.mult))
                yield st.mark(v.tensor_copy(entry[0:N, :, :, 0], m.token_id[0:N].unsqueeze(2).to_broadcast([N, GB, 2])))
                yield st.mark(v.tensor_tensor(col(6), col(6), col(3), ALU.add))
                st.mark(v.tensor_scalar(m.token_id[0:N], m.token_id[0:N], float(GB * N), None, ALU.add))
                yield st.mark(v.reciprocal(col(6), col(6)))
                yield v.tensor_tensor(entry[0:N, :, :, 1], top[0:N, :, 2:4], col(6).to_broadcast([N, GB, 2]), ALU.mult).then_inc(q["entry_ready"], GROUP)

            def slot(s, k, ok):
                p, a, o, r = s - PROJ, s - ATT, s - OUT, s - ROUTE
                has_p, has_a, has_o, has_r = ok(PROJ, SLOTS), ok(ATT, SLOTS), ok(OUT, SLOTS), ok(ROUTE, SLOTS)
                t, has_n = s - NORM, ok(NORM, SLOTS)
                now, was = inv[0:N, k % 2], inv[0:N, (k + 1) % 2]

                def scaled_qk(b):
                    dve.wait_ge(q["qk_done"], 2 * p + b + 1)
                    if late(p, 1) and b == 0:
                        dve.wait_ge(q["k_hi"], p)
                        dve.wait_ge(q["q_lo"], p)
                        dve.wait_ge(q["k_lo"], p)
                    v.scalar_tensor_tensor(out=qk[0:N, b], in0=bQK[b][0:N, :], scalar=was[:, NR2 + b:NR2 + b + 1], in1=m.bias_qk[0:N],
                                           op0=ALU.mult, op1=ALU.add).then_inc(q["qk_ready"], 1)

                def sum_squares(b):
                    dve.wait_ge(q["sq_ready"], 2 * p + b + 1)
                    at = NQK + b * 2 * HEADS
                    st.mark(v.tensor_reduce(squares[0:N, at:at + 2 * HEADS], qk_sq[0:N, b].rearrange("n (h d) -> n h d", d=HD), AX.X, ALU.add))

                def gate_and_split(pair, b):
                    n = 2 * pair + b
                    dve.wait_ge(q["cg_ready"], n + 1)
                    if b == 0 and late(pair, 1):
                        dve.wait_ge(q["wo_done"], pair)
                    st.do(v.tensor_tensor(cT[:], bC[:, 0:2 * N].rearrange("p (k n) -> p k n", n=N), cT[:], ALU.mult))
                    st.do(v.tensor_copy(cTs[:, b, 0], cT[:]))
                    v.tensor_tensor(cTs[:, b, 1], cT[:], cTs[:, b, 0], ALU.subtract).then_inc(q["c_ready"], 1)

                if has_a:
                    dve.wait_ge(q["v_copied"], 2 * a + 2)
                    for b in range(PAIR):
                        st.mark(v.scalar_tensor_tensor(out=gate[0:N, b], in0=vg[0:N, b, D:], scalar=now[:, NR2 + b:NR2 + b + 1], in1=m.bias_gate[0:N],
                                                       op0=ALU.mult, op1=ALU.add))
                if has_p:
                    scaled_qk(0)
                if ok(0, SLOTS):
                    dve.wait_ge(h_loaded[k], (s - k) * (32 // RING) + 32)
                    for b in range(PAIR):
                        st.mark(v.bn_stats(stats[0:N, 0, b], h[0:N, k, b]))
                    st.settle()
                if has_p:
                    sum_squares(0)
                    scaled_qk(1)
                if ok(0, SLOTS):
                    for b in range(PAIR):
                        st.mark(v.bn_aggr(mv[0:N, 0, b], stats[0:N, 0, b]))
                if has_r:
                    dve.wait_ge(q["x2T_hi"], r + 1)
                    v.tensor_tensor(x2T[:, :, 1], xT_ps, x2T[:, :, 0], ALU.subtract).then_inc(q["x2T_lo"], 1)
                if ok(0, SLOTS):
                    st.settle()
                    st.mark(v.tensor_scalar(squares[0:N, NV1:NR2], mv[0:N, 0, :, 1], LN_EPS, None, ALU.add))
                if has_p:
                    sum_squares(1)
                if ok(0, SLOTS):
                    st.settle()
                    st.mark(v.reciprocal(squares[0:N, NR2:NCOLS], squares[0:N, NV1:NR2]))
                if has_a:
                    st.settle()
                    v.tensor_tensor(gate[0:N], gate[0:N], was[:, NQK:NV2].rearrange("n (b h) -> n b h", b=PAIR), ALU.mult).then_inc(q["gate_ready"], 1)
                if ok(0, SLOTS):
                    st.settle()
                    st.mark(v.tensor_tensor(squares[0:N, NR2:NCOLS], squares[0:N, NR2:NCOLS], mv[0:N, 0, :, 1], ALU.mult))
                if has_o:
                    gate_and_split(o, 1)
                if has_p:
                    st.settle()
                    st.mark(v.tensor_scalar(squares[0:N, NQK:NV2], squares[0:N, NQK:NV2], NORM_EPS * NORM_EPS, None, ALU.max))
                if ok(0, SLOTS):
                    st.settle()
                    st.mark(v.tensor_scalar(squares[0:N, NR2:NCOLS], squares[0:N, NR2:NCOLS], LN_EPS, None, ALU.add))
                chains = []
                if ok(0, SLOTS) or has_p or has_n:
                    if late(s, 3):
                        dve.wait_ge(q["qn_k_ready"], min(s - 2, SLOTS) if isinstance(s, int) else s - 2)
                    chains.append(inverse_sqrt(nc, st, q["inv_ready"], now, squares[0:N], inv_t[0:N]))
                if k == CHOOSE_AT and ok(PLACE - 1, SLOTS):
                    dve.wait_ge(q["lg_read"], s - ROUTE)
                    chains.append(route())
                if k == PLACE_AT and ok(PLACE, SLOTS):
                    chains.append(place(s))
                st.settle()
                in_turn(st, *chains)
                if has_r:
                    if k == CHOOSE_AT and ok(PLACE - 1, SLOTS):
                        dve.wait_ge(q["ex_ready"], s - ROUTE)
                    dve.wait_ge(q["lg_done"], r + 1)
                    at = slice(PAIR * ((k - ROUTE) % RING), PAIR * ((k - ROUTE) % RING + 1))
                    v.tensor_copy(logits[0:N, at], lg_ps[0:N, :].rearrange("n (b e) -> n b e", e=E)).then_inc(q["lg_read"], 1)
                if ok(0, SLOTS) or has_p or has_n:
                    dve.wait_ge(q["inv_ready"], s + 1)
                if ok(0, SLOTS):
                    if late(s, 1):
                        dve.wait_ge(q["x1T_done"], s)
                    for b in range(PAIR):
                        ins = v.tensor_scalar(x1[0:N, b], h[0:N, k, b], mv[0:N, 0, b, 0:1], now[:, NV1 + b:NV1 + b + 1], ALU.subtract, ALU.mult)
                    ins.then_inc(q["x1_ready"], 1)
                if has_n:
                    if late(t, 1):
                        dve.wait_ge(q["xln_stored"], 16 * t)
                        dve.wait_ge(q["x2T_done"], t)
                    for b in range(PAIR):
                        ins = v.tensor_scalar(x2[0:N, b], h2[0:N, b], mv[0:N, 1, b, 0:1], now[:, NV2 + b:NV2 + b + 1], ALU.subtract, ALU.mult)
                    ins.then_inc(q["x2_ready"], 1)
                if has_a:
                    dve.wait_ge(q["gate_ready"], a + 1)
                    v.tensor_copy(gate_q[0:N], gate[0:N, :, 0:HEADS].unsqueeze(3).to_broadcast([N, PAIR, HEADS, HD])).then_inc(q["gate_q_ready"], 1)
                if has_o:
                    dve.wait_ge(q["wo_done"], o + 1)
                    if late(o, 1):
                        dve.wait_ge(q["x2_ready"], o)
                        dve.wait_ge(q["out_stored"], 16 * o)
                    v.tensor_tensor(h2[0:N], bV[0:N, :].rearrange("n (b d) -> n b d", b=PAIR), h[0:N, (k - OUT) % RING],
                                    ALU.add).then_inc(q["h2_ready"], 1)
                    dve.wait_ge(q["h2_ready"], o + 1)
                    for b in range(PAIR):
                        st.mark(v.bn_stats(stats[0:N, 1, b], h2[0:N, b]))
                    st.settle()
                if ok(0, SLOTS):
                    dve.wait_ge(q["x1T_hi"], s + 1)
                    v.tensor_tensor(x1T[:, :, 1], xT_ps, x1T[:, :, 0], ALU.subtract).then_inc(q["x1T_lo"], 1)
                if has_o:
                    for b in range(PAIR):
                        st.mark(v.bn_aggr(mv[0:N, 1, b], stats[0:N, 1, b]))
                if has_a:
                    gate_and_split(a, 0)
                if has_o:
                    st.settle()
                    st.mark(v.tensor_scalar(squares[0:N, NV2:NV1], mv[0:N, 1, :, 1], LN_EPS, None, ALU.add))
                if k == CHOOSE_AT and ok(PLACE - 1, SLOTS):
                    read_ranks(s - ROUTE)

            run(dve, st, slot)
            dve.wait_ge(q["k_lo"], SLOTS)
            st.settle()
            plan_tiles(nc, m, st, qk[:].rearrange("p b c -> p (b c)"), qk_sq[:].rearrange("p b c -> p (b c)"))
            st.settle()


def expert_tiles(nc, m, dram):
    UP, DOWN = 1, 2
    TOTAL = TILES + DOWN
    LOOP_FROM, UNROLL = 4, 2
    with ExitStack() as ctx:
        sb = lambda n, s, d: ctx.enter_context(nc.sbuf_tensor(n, s, d))
        sem = lambda n: ctx.enter_context(nc.semaphore(n))
        pb = lambda n: ctx.enter_context(nc.psum_tensor(n, [P, 512], F32))
        b2_rows = sb("b2_rows", [P, E, D], BF16)
        tab = sb("tab", [P, 2, PARTS, 2], F32)
        away = sb("away", [P, PARTS, 2], F32)
        kept = sb("kept", [P, 2, PARTS, 2], F32)
        from_id = sb("from_id", [P, 2, PARTS], U32)
        to_id = sb("to_id", [P, 2, PARTS], U32)
        weight = sb("weight", [P, 2, PARTS], F32)
        x = sb("x", [P, 2, PARTS, D], F32)
        xT = sb("xT", [P, 2, 2, KC, TILE], BF16)
        act_f = sb("act_f", [P, FC, TILE], F32)
        act_hi = sb("act_hi", [P, 2, FC, TILE], BF16)
        act_lo = sb("act_lo", [P, 2, FC, TILE], BF16)
        y = sb("y", [P, 2, PARTS, D], F32)
        bX = pb("bX")
        bH = [pb(f"bH{i}") for i in range(FC // 2)]
        bY = [pb(f"bY{i}") for i in range(2)]
        x_ps = bX[:, :].rearrange("p (c n) -> p c n", c=KC)
        names = """b2_in ids_ready weight_ready gathered0 gathered1 turned xT_hi xT_lo up_done gelu_ready act_ready
            down_done y_ready added dve_steps4 tab_in0 tab_in1""".split()
        q = {n: sem(n) for n in names}
        tab_in = [q["tab_in0"], q["tab_in1"]]
        gathered = [q["gathered0"], q["gathered1"]]
        block = ctx.enter_context(nc.Block())
        late = lambda v, n: not isinstance(v, int) or v >= n

        def run(eng, steps, slot):
            slots(eng, steps, slot, LOOP_FROM, UNROLL, (TILES - LOOP_FROM) // UNROLL, TOTAL)

        def info(eng, which, t, top):
            return eng.value_load(m.tile_info[0:1, which, bass.ds(t, 1)], min_val=0, max_val=top)

        def uses(s, k, each):
            return (s - k % 2) * (each // 2) + each

        @block.sync
        def _(sp):
            sp.dma_start(b2_rows[0:BIAS_PARTS].rearrange("p e d -> p (e d)"), dram["bias_parts"][:, D:]).then_inc(q["b2_in"], 16)

            def slot(s, k, ok):
                if ok(0, TILES):
                    if late(s, 2):
                        sp.wait_ge(q["ids_ready"], s - 1)
                    start = info(sp, 1, s, E * ROWS - TILE)
                    sp.dma_start(tab[:, k % 2], dram["table"][bass.ds(start, TILE), :].rearrange("(h p) c -> p h c", p=P)).then_inc(tab_in[k % 2], 16)

            run(sp, None, slot)
            sp.wait_ge(q["added"], 16 * PARTS * TILES)

        @block.gpsimd
        def _(pool):
            def add(d, k, h):
                before = [(q["added"], 16 * (PARTS * d + h))] if h or late(d, 1) else []
                wait_before_dma(pool, (q["b2_in"], 16), *([] if h else [(q["y_ready"], d + 1)]), *before)
                nc.gpsimd.indirect_dma_start(dram["out"], bass.IndirectOffsetOnAxis(ap=to_id[:, k % 2, h:h + 1], axis=0),
                                             y[:, k % 2, h], None, compute_op=ALU.add).then_inc(q["added"], 16)

            def slot(s, k, ok):
                d = s - DOWN
                if ok(0, TILES):
                    wait_before_dma(pool, (q["b2_in"], 16), (q["ids_ready"], s + 1), *([(q["turned"], s - 1)] if late(s, 2) else []))
                    for h in range(PARTS):
                        nc.gpsimd.indirect_dma_start(x[:, k % 2, h], None, dram["xln"], bass.IndirectOffsetOnAxis(ap=from_id[:, k % 2, h:h + 1], axis=0)
                                                     ).then_inc(gathered[k % 2], 16)
                if ok(DOWN, TILES):
                    for h in range(PARTS):
                        add(d, k, h)

            run(pool, None, slot)

        @block.tensor
        def _(pe):
            pe.wait_ge(q["b2_in"], 16)

            def slot(s, k, ok):
                u, d = s - UP, s - DOWN
                if ok(DOWN, TILES):
                    e_down = info(pe, 0, d, E - 1)
                if ok(UP, TILES):
                    e_up = info(pe, 0, u, E - 1)
                    pe.wait_ge(gathered[(k - UP) % 2], uses(u, k - UP, 16 * PARTS))
                    if late(u, 1):
                        pe.wait_ge(q["xT_lo"], u)
                    for c in range(KC):
                        for h in range(PARTS):
                            mm = nc.tensor.transpose(x_ps[:, c, h * P:(h + 1) * P], x[:, (k - UP) % 2, h, c * P:(c + 1) * P], m.ident_f)
                    mm.then_inc(q["turned"], 1)
                if ok(DOWN, TILES):
                    at = k % 2
                    if late(d, 2):
                        pe.wait_ge(q["y_ready"], d - 1)
                    for h in range(PARTS):
                        rows = slice(h * P, (h + 1) * P)
                        out = bY[at][:, h * D:(h + 1) * D]
                        nc.tensor.matmul(out, m.ones[0:BIAS_PARTS, :], b2_rows[0:BIAS_PARTS, bass.ds(e_down, 1), :].rearrange("p o d -> p (o d)"), start=True, stop=False)
                        for f in range(FC):
                            if h == 0 and f % 2 == 0:
                                pe.wait_ge(q["act_ready"], (FC // 2) * d + f // 2 + 1)
                            for a, w in ((act_hi, m.w_ffn_hi), (act_lo, m.w_ffn_hi), (act_hi, m.w_ffn_lo)):
                                rhs = w[:, bass.ds(2 * e_down + (2 * E + f // 4), 1), (f % 4) * D:(f % 4 + 1) * D].rearrange("p o d -> p (o d)")
                                mm = nc.tensor.matmul(out, a[:, at, f, rows], rhs, start=False, stop=f == FC - 1 and w is m.w_ffn_lo)
                    mm.then_inc(q["down_done"], 1)
                if ok(UP, TILES):
                    at = (k - UP) % 2
                    pe.wait_ge(q["xT_hi"], u + 1)
                    pe.wait_ge(q["xT_lo"], u + 1)
                    for b in range(FC // 2):
                        if late(u, 1):
                            pe.wait_ge(q["gelu_ready"], (FC // 2) * (u - 1) + b + 1)
                        for f in range(2):
                            parts = [(p, w, kc) for kc in range(KC) for p, w in ((0, m.w_ffn_hi), (1, m.w_ffn_hi), (0, m.w_ffn_lo))]
                            for i, (p, w, kc) in enumerate(parts):
                                lhs = w[:, bass.ds(2 * e_up + kc, 1), (2 * b + f) * P:(2 * b + f + 1) * P].rearrange("p o d -> p (o d)")
                                mm = nc.tensor.matmul(bH[b][:, f * TILE:(f + 1) * TILE], lhs, xT[:, at, p, kc, :],
                                                      start=i == 0, stop=i == len(parts) - 1)
                        mm.then_inc(q["up_done"], 1)

            run(pe, None, slot)

        @block.scalar
        def _(act):
            def slot(s, k, ok):
                u = s - UP
                if ok(UP, TILES):
                    at = (k - UP) % 2
                    e = info(act, 0, u, E - 1)
                    act.wait_ge(q["turned"], u + 1)
                    if late(u, 2):
                        act.wait_ge(q["up_done"], (FC // 2) * (u - 1))
                    nc.scalar.copy(xT[:, at, 0], x_ps).then_inc(q["xT_hi"], 1)
                    for b in range(FC // 2):
                        act.wait_ge(q["up_done"], (FC // 2) * u + b + 1)
                        if late(u, 1):
                            act.wait_ge(q["act_ready"], (FC // 2) * (u - 1) + b + 1)
                        for f in range(2):
                            ins = nc.scalar.activation(act_f[:, 2 * b + f, :], bH[b][:, f * TILE:(f + 1) * TILE], ACT.Gelu,
                                                       bias=m.b1[:, bass.ds(e * FC + (2 * b + f), 1)])
                        ins.then_inc(q["gelu_ready"], 1)

            run(act, None, slot)

        @block.vector
        def _(dve):
            st = Steps(dve, q["dve_steps4"], FFN_STEPS)
            v = nc.vector

            def slot(s, k, ok):
                u, d = s - UP, s - DOWN
                if ok(DOWN, TILES):
                    at = k % 2
                    if late(d, 2):
                        dve.wait_ge(q["added"], 16 * PARTS * (d - 1))
                    st.mark(v.tensor_tensor(to_id[:, at], kept[:, at, :, 0], m.away.rearrange("p (h c) -> p h c", c=2)[:, :, 0], ALU.add))
                    st.do(v.tensor_copy(weight[:, at], kept[:, at, :, 1]))
                if ok(0, TILES):
                    at = k % 2
                    dve.wait_ge(tab_in[at], uses(s, k, 16))
                    if late(s, 2):
                        dve.wait_ge(gathered[at], uses(s, k, 16 * PARTS) - 16 * PARTS)
                    st.mark(v.tensor_copy(from_id[:, at], tab[:, at, :, 0]))
                    st.do(v.tensor_tensor(away[:], tab[:, at], m.away.rearrange("p (h c) -> p h c", c=2), ALU.subtract))
                    v.tensor_tensor(kept[:, at], away[:], m.valid[:, bass.ds(s, 1), :].rearrange("p o h -> p h o").to_broadcast([P, PARTS, 2]),
                                    ALU.mult).then_inc(q["ids_ready"], 1)
                    dve.wait_ge(q["ids_ready"], s + 1)
                if ok(UP, TILES):
                    at = (k - UP) % 2
                    dve.wait_ge(q["xT_hi"], u + 1)
                    v.tensor_tensor(xT[:, at, 1], x_ps, xT[:, at, 0], ALU.subtract).then_inc(q["xT_lo"], 1)
                    for b in range(FC // 2):
                        part = slice(2 * b, 2 * b + 2)
                        dve.wait_ge(q["gelu_ready"], (FC // 2) * u + b + 1)
                        if late(u, 2):
                            dve.wait_ge(q["down_done"], u - 1)
                        st.do(v.tensor_copy(act_hi[:, at, part], act_f[:, part]))
                        v.tensor_tensor(act_lo[:, at, part], act_f[:, part], act_hi[:, at, part], ALU.subtract).then_inc(q["act_ready"], 1)
                        if b == 0 and ok(DOWN, TILES):
                            weigh(d, k % 2)
                elif ok(DOWN, TILES):
                    weigh(d, k % 2)

            def weigh(d, at):
                dve.wait_ge(q["down_done"], d + 1)
                for h in range(PARTS):
                    ins = v.tensor_scalar(y[:, at, h], bY[at][:, h * D:(h + 1) * D], weight[:, at, h:h + 1], None, ALU.mult)
                    if h == 0:
                        st.mark(ins)
                ins.then_inc(q["y_ready"], 1)

            run(dve, st, slot)
            st.settle()


CONSTS = {"ident_f": P, "tri_f": P, "rev_e": E, "index_e": E, "sign": 2 * E, "centre": 2 * E, "centre_e": E,
          "first_tokens": GB, "pos_p": PARTS, "away": 2 * PARTS, "below": E * E, "tile_no": TILES}


def constants():
    p, e = np.arange(P), np.arange(E)
    wide = lambda x: np.broadcast_to(np.asarray(x).reshape(1, -1), (P, np.size(x)))
    tables = {
        "ident_f": np.eye(P),
        "tri_f": p[:, None] < p[None, :],
        "rev_e": wide(E - e),
        "index_e": wide(e),
        "sign": wide(np.repeat([-1, 1], E)),
        "centre": wide(np.concatenate([e * ROWS + CENTRE - 1, e * ROWS + CENTRE])),
        "centre_e": wide(e * ROWS + CENTRE),
        "first_tokens": np.arange(GB)[None, :] * N + p[:, None],
        "pos_p": np.stack([p + h * P for h in range(PARTS)], axis=1),
        "away": np.stack([TOKENS + p, 0 * p] * PARTS, axis=1),
        "below": wide(e[None, :] < e[:, None]),
        "tile_no": wide(np.arange(TILES)),
    }
    return np.concatenate([tables[n].astype(np.float32) for n in CONSTS], axis=1)


class Kept:

    def __init__(self, nc, ctx):
        sb = lambda n, s, d: ctx.enter_context(nc.sbuf_tensor(n, s, d))
        self.w_ffn_hi = sb("w_ffn_hi", [P, WCHUNKS, WCH], BF16)
        self.w_ffn_lo = sb("w_ffn_lo", [P, WCHUNKS, WCH], BF16)
        self.w_hi = sb("w_hi", [P, KC, QKV], BF16)
        self.w_lo = sb("w_lo", [P, KC, QKV], BF16)
        self.w_out_hi = sb("w_out_hi", [P, KC, D], BF16)
        self.w_out_lo = sb("w_out_lo", [P, KC, D], BF16)
        self.w_gate_hi = sb("w_gate_hi", [P, KC, E], BF16)
        self.w_gate_lo = sb("w_gate_lo", [P, KC, E], BF16)
        self.bias_qk = sb("bias_qk", [P, 2 * D], F32)
        self.bias_gate = sb("bias_gate", [P, 2 * HEADS], F32)
        self.bo_rows = sb("bo_rows", [P, D], BF16)
        self.b1 = sb("b1", [P, E * FC], F32)
        self.ident = sb("ident", [P, P], BF16)
        self.tri = sb("tri", [P, P], BF16)
        self.ones = sb("ones", [P, P], BF16)
        self.token_id = sb("token_id", [P, GB], F32)
        self.placed = sb("placed", [P, 2 * E], F32)
        self.valid = sb("valid", [P, TILES, PARTS], F32)
        self.tile_info = sb("tile_info", [P, 2, TILES], I32)
        self.consts = sb("consts", [P, sum(CONSTS.values())], F32)
        at = {}
        col = 0
        for name, width in CONSTS.items():
            at[name] = self.consts[:, col:col + width]
            col += width
        self.ident_f, self.tri_f, self.rev_e, self.index_e = at["ident_f"], at["tri_f"], at["rev_e"], at["index_e"]
        self.sign, self.centre, self.centre_e = at["sign"], at["centre"], at["centre_e"]
        self.first_tokens, self.pos_p, self.away = at["first_tokens"], at["pos_p"], at["away"]
        self.below, self.tile_no = at["below"], at["tile_no"]


def build(nc, dram):
    dram = dict(dram)
    dram["tok"] = nc.dram_tensor("tok_rows", [B * N_PATCH, D], F32, kind="Internal").ap()
    dram["bias_parts"] = nc.dram_tensor("bias_part_rows", [3, (E + 1) * D], BF16, kind="Internal").ap()
    dram["xln"] = nc.dram_tensor("xln_rows", [TOKENS, D], F32, kind="Internal").ap()
    dram["table"] = nc.dram_tensor("table_rows", [E * ROWS, 2], F32, kind="Internal").ap()
    with ExitStack() as ctx:
        m = Kept(nc, ctx)
        prepare_and_tokenise(nc, m, dram)
        fusion_attention(nc, m, dram)
        expert_tiles(nc, m, dram)


def kernel(**inputs):
    import concourse.bacc as bacc
    from concourse.bass_utils import run_bass_kernel_spmd

    a = {k: np.asarray(v) for k, v in inputs.items()}
    img = a["x"][:, :, :GRID * PATCH, :GRID * PATCH].reshape(B, C_IN, GRID, PATCH, GRID, PATCH)
    patches = img.transpose(0, 1, 3, 5, 2, 4).reshape(B * N_PATCH, FLATC, P).transpose(2, 1, 0)
    rows = lambda w: w.reshape(KC, P, -1).transpose(1, 0, 2)
    w1 = a["L0_ffn_W1"].reshape(E * KC, P, F)
    w2 = a["L0_ffn_W2"].reshape(E * 2, 4, P, D).transpose(0, 2, 1, 3).reshape(E * 2, P, 4 * D)
    arrays = {
        "patches": patches,
        "txt": a["txt"],
        "w_tok": a["L0_tok_W"].reshape(FLATC, P, D).transpose(1, 0, 2),
        "w_qk": np.concatenate([rows(a["L0_attn_Wq"]), rows(a["L0_attn_Wk"])], axis=2),
        "w_v": rows(a["L0_attn_Wv"]),
        "w_o": rows(a["L0_attn_Wo"]),
        "w_g": rows(a["L0_ffn_Wg"]),
        "ln_w": a["L0_attn_ln_w"].reshape(KC, P).T,
        "ln_b": a["L0_attn_ln_b"].reshape(KC, P).T,
        "gq": a["L0_attn_gq"],
        "gk": a["L0_attn_gk"],
        "w_ffn": np.concatenate([w1, w2], axis=0),
        "b1": a["L0_ffn_b1"].reshape(E * FC, P).T,
        "biases": np.concatenate([a["L0_attn_bo"], a["L0_ffn_b2"].reshape(E * D)]).reshape(P, -1),
        "consts": constants(),
    }
    arrays = {"in_" + k: np.ascontiguousarray(v) for k, v in arrays.items()}
    nc = bacc.Bacc("TRN2", target_bir_lowering=False, num_devices=1)
    dram = {k[3:]: nc.dram_tensor(k, v.shape, mybir.dt.from_np(v.dtype), kind="ExternalInput").ap() for k, v in arrays.items()}
    dram["out"] = nc.dram_tensor("out_rows", (TOKENS + P, D), F32, kind="ExternalOutput").ap()
    build(nc, dram)
    r = run_bass_kernel_spmd(nc, [arrays], core_ids=[0])
    return r.results[0]["out_rows"][:TOKENS].reshape(B, N, D)
```
